# Optimizing a Trainium2 kernel written in Bass

```python
import numpy as np
import jax
import jax.numpy as jnp

def _softmax(x, axis=-1):
    return jax.nn.softmax(x, axis=axis)

def _gelu(x):
    return jax.nn.gelu(x, approximate=True)

def _silu(x):
    return jax.nn.silu(x)

def _sigmoid(x):
    return jax.nn.sigmoid(x)

def _layernorm(x, axis=-1, eps=1e-05):
    m = jnp.mean(x, axis=axis, keepdims=True)
    v = jnp.var(x, axis=axis, keepdims=True)
    return (x - m) / jnp.sqrt(v + eps)

def _scatter_add(tgt, idx, src, axis=0):
    return tgt.at[idx].add(src)

def _segment_sum(src, seg, n):
    return jax.ops.segment_sum(src, seg, n)
kernel_name = 'mk_xattn_seq_d4_seqx_r8_3c7c26'

def setup_inputs(seed: int=0):
    np.random.seed(seed)
    _w = jnp.asarray

    def _rec_inputs():
        import jax
        import jax.numpy as jnp
        _rk = jax.random.key(seed)
        x = -0.0002928 + 1 * jax.random.normal(jax.random.fold_in(_rk, 1), (32, 100, 128), jnp.float32)
        _lenS = 100 - jax.random.randint(jax.random.fold_in(_rk, 7), (32,), 0, max(1, 100 // 4) + 1, jnp.int32)
        _lenS2 = 1444 - jax.random.randint(jax.random.fold_in(_rk, 8), (32,), 0, max(1, 1444 // 4) + 1, jnp.int32)
        _ctx_1024P = jax.random.normal(jax.random.fold_in(_rk, 11), (32, 16, 128), jnp.float32)
        _ctx_1024c = jax.random.dirichlet(jax.random.fold_in(_rk, 511), 0.3 * jnp.ones((16,), jnp.float32), (32, 1444))
        _ctx_1024t = jnp.einsum('bsk,bkd->bsd', _ctx_1024c, _ctx_1024P)
        _ctx_1024t = _ctx_1024t * jax.lax.rsqrt(jnp.mean(jnp.square(_ctx_1024t)) + 1e-12) * 0.953939
        ctx_1024 = -1.39393e-06 + 0.999914 * (_ctx_1024t + 0.3 * jax.random.normal(jax.random.fold_in(_rk, 611), (32, 1444, 128), jnp.float32))
        return (x, ctx_1024)
    x, ctx_1024 = _rec_inputs()

    def _L0_xattn_setup():
        import jax, jax.numpy as jnp
        import numpy as np
        B, N, DIM = (2, 256, 128)
        HEADS, DH = (16, 64)
        SEG = 64
        NPM = 16
        NM = 16
        DFF = int(DIM * 4 * 2 / 3)
        EPS = 1.1920929e-07

        def rms_norm(x, w):
            return x * jax.lax.rsqrt(jnp.mean(x * x, axis=-1, keepdims=True) + EPS) * w
        key = jax.random.key(seed)
        ks = jax.random.split(key, 10)
        p = lambda i, shape: jax.random.normal(ks[i], shape, jnp.float32) * 0.02
        return {'x': jax.random.normal(ks[0], (B, N, DIM), jnp.float32), 'mem_out': jax.random.normal(ks[1], (B, N, DIM), jnp.float32), 'attn_norm_w': jnp.ones((DIM,), jnp.float32), 'to_qkv_w': p(2, (DIM, 3 * HEADS * DH)), 'to_out_w': p(3, (HEADS * DH, DIM)), 'persist_mem': jax.random.normal(ks[4], (HEADS, NPM, DH), jnp.float32), 'mem_pool_norm_w': jnp.ones((DIM,), jnp.float32), 'to_mem_tokens_w': p(5, (DIM, DIM)), 'ff_norm_w': jnp.ones((DIM,), jnp.float32), 'ff_w1': p(6, (DIM, 2 * DFF)), 'ff_b1': jnp.zeros((2 * DFF,), jnp.float32), 'ff_w2': p(7, (DFF, DIM)), 'ff_b2': jnp.zeros((DIM,), jnp.float32)}
    _L0_xattn_all = _L0_xattn_setup()
    _L0_xattn_in = {k: v for k, v in _L0_xattn_all.items() if k in ('attn_norm_w', 'to_qkv_w', 'to_out_w', 'persist_mem', 'mem_pool_norm_w', 'to_mem_tokens_w', 'ff_norm_w', 'ff_w1', 'ff_b1', 'ff_w2', 'ff_b2')}
    del _L0_xattn_all

    def _L1_xattn_setup():
        import jax, jax.numpy as jnp
        import numpy as np
        D_MODEL = 128
        HEADS = 16
        D_K = D_MODEL // HEADS
        key = jax.random.key(seed)
        ks = jax.random.split(key, 12)
        B, S = (2, 256)
        s = 1.0 / np.sqrt(D_MODEL)
        return {'queries': jax.random.normal(ks[0], (B, S, D_MODEL), jnp.float32), 'keys': jax.random.normal(ks[1], (B, S, D_MODEL), jnp.float32), 'values': jax.random.normal(ks[2], (B, S, D_MODEL), jnp.float32), 'Wq': jax.random.normal(ks[3], (D_MODEL, D_MODEL), jnp.float32) * s, 'bq': jnp.zeros((D_MODEL,), jnp.float32), 'Wk': jax.random.normal(ks[4], (D_MODEL, D_MODEL), jnp.float32) * s, 'bk': jnp.zeros((D_MODEL,), jnp.float32), 'Wv': jax.random.normal(ks[5], (D_MODEL, D_MODEL), jnp.float32) * s, 'bv': jnp.zeros((D_MODEL,), jnp.float32), 'Wo': jax.random.normal(ks[6], (D_MODEL, D_MODEL), jnp.float32) * s, 'bo': jnp.zeros((D_MODEL,), jnp.float32), 'gamma': jnp.ones((D_MODEL,), jnp.float32), 'beta': jnp.zeros((D_MODEL,), jnp.float32)}
    _L1_xattn_all = _L1_xattn_setup()
    _L1_xattn_in = {k: v for k, v in _L1_xattn_all.items() if k in ('Wq', 'bq', 'Wk', 'bk', 'Wv', 'bv', 'Wo', 'bo', 'gamma', 'beta')}
    del _L1_xattn_all

    def _L2_xattn_setup():
        import jax, jax.numpy as jnp
        import numpy as np
        from functools import partial
        HEADS = 16
        DIM_HEAD = 64
        SCALE = DIM_HEAD ** (-0.5)
        MAX_ALLOWABLE = 128 * 128 * 8
        EPS = 1e-05

        def ln32(x, scale, bias):
            x32 = x.astype(jnp.float32)
            mean = jnp.mean(x32, axis=-1, keepdims=True)
            var = jnp.mean(jnp.square(x32 - mean), axis=-1, keepdims=True)
            y = (x32 - mean) * jax.lax.rsqrt(var + EPS) * scale.astype(jnp.float32) + bias.astype(jnp.float32)
            return y.astype(x.dtype)

        def heads_to_batch(t):
            b, s, d = t.shape
            return t.reshape(b, s, HEADS, d // HEADS).transpose(0, 2, 1, 3).reshape(b * HEADS, s, d // HEADS)

        def batch_to_heads(t):
            bh, s, dh = t.shape
            return t.reshape(bh // HEADS, HEADS, s, dh).transpose(0, 2, 1, 3).reshape(bh // HEADS, s, dh * HEADS)

        def _max_pow2(n):
            i = 1
            while n % 2 == 0:
                i *= 2
                n //= 2
            return i

        def sdpa(q, k, v):
            scores = jnp.einsum('bid,bjd->bij', q, k) * SCALE
            probs = jax.nn.softmax(scores, axis=2)
            return jnp.einsum('bij,bjd->bid', probs, v)

        def lowmem_attention(q, k, v):
            dimprod = q.shape[0] * q.shape[1] * k.shape[1]
            true_divisor = dimprod / MAX_ALLOWABLE
            if true_divisor < 1:
                n_splits = 1
            elif true_divisor >= q.shape[0]:
                n_splits = q.shape[0]
            else:
                nearest_pow2 = 2 ** np.round(np.log2(true_divisor))
                n_splits = int(min(_max_pow2(q.shape[0]), nearest_pow2))
            nq, nk, nv = [h.reshape(n_splits, h.shape[0] // n_splits, h.shape[-2], h.shape[-1]) for h in (q, k, v)]
            outs = jax.lax.scan(lambda c, a: (None, sdpa(*a)), None, (nq, nk, nv))[1]
            return outs.reshape(-1, outs.shape[-2], outs.shape[-1])

        def attention(x, ctx, Wq, Wkv, Wo, bo):
            q = x @ Wq
            k, v = jnp.split(ctx @ Wkv, 2, axis=-1)
            out = lowmem_attention(heads_to_batch(q), heads_to_batch(k), heads_to_batch(v))
            return batch_to_heads(out) @ Wo + bo

        def geglu_ff(x, Wff1, bff1, Wff2, bff2):
            h = x @ Wff1 + bff1
            lin, gelu = jnp.split(h, 2, axis=-1)
            h = lin * (gelu * jax.nn.sigmoid(1.702 * gelu))
            return h @ Wff2 + bff2
        key = jax.random.key(seed)
        ks = jax.random.split(key, 12)
        B, S, D, CTX = (4, 256, 128, 77)
        s = 0.02
        return {'hidden_states': jax.random.normal(ks[0], (B, S, D), jnp.float32), 'context': jax.random.normal(ks[1], (B, CTX, D), jnp.float32), 'Wq1': jax.random.normal(ks[2], (D, D), jnp.float32) * s, 'Wkv1': jax.random.normal(ks[3], (D, 2 * D), jnp.float32) * s, 'Wo1': jax.random.normal(ks[4], (D, D), jnp.float32) * s, 'bo1': jnp.zeros((D,), jnp.float32), 'Wq2': jax.random.normal(ks[5], (D, D), jnp.float32) * s, 'Wkv2': jax.random.normal(ks[6], (D, 2 * D), jnp.float32) * s, 'Wo2': jax.random.normal(ks[7], (D, D), jnp.float32) * s, 'bo2': jnp.zeros((D,), jnp.float32), 'Wff1': jax.random.normal(ks[8], (D, 8 * D), jnp.float32) * s, 'bff1': jnp.zeros((8 * D,), jnp.float32), 'Wff2': jax.random.normal(ks[9], (4 * D, D), jnp.float32) * s, 'bff2': jnp.zeros((D,), jnp.float32), 'ln1_s': jnp.ones((D,), jnp.float32), 'ln1_b': jnp.zeros((D,), jnp.float32), 'ln2_s': jnp.ones((D,), jnp.float32), 'ln2_b': jnp.zeros((D,), jnp.float32), 'ln3_s': jnp.ones((D,), jnp.float32), 'ln3_b': jnp.zeros((D,), jnp.float32)}
    _L2_xattn_all = _L2_xattn_setup()
    _L2_xattn_in = {k: v for k, v in _L2_xattn_all.items() if k in ('Wq1', 'Wkv1', 'Wo1', 'bo1', 'Wq2', 'Wkv2', 'Wo2', 'bo2', 'Wff1', 'bff1', 'Wff2', 'bff2', 'ln1_s', 'ln1_b', 'ln2_s', 'ln2_b', 'ln3_s', 'ln3_b')}
    del _L2_xattn_all

    def _L3_xattn_setup():
        import jax, jax.numpy as jnp
        import numpy as np
        B, SR, SF, D = (8, 256, 256, 128)
        key = jax.random.key(seed)
        k1, k2 = jax.random.split(key)
        H_real = jax.random.normal(k1, (B, SR, D), dtype=jnp.float32)
        H_fake = jax.random.normal(k2, (B, SF, D), dtype=jnp.float32)
        return {'H_real': H_real, 'H_fake': H_fake}
    _L3_xattn_all = _L3_xattn_setup()
    _L3_xattn_in = {k: v for k, v in _L3_xattn_all.items() if k in ()}
    del _L3_xattn_all
    return {'x': x, 'ctx_1024': ctx_1024, 'L0_xattn_attn_norm_w': _L0_xattn_in['attn_norm_w'], 'L0_xattn_to_qkv_w': _L0_xattn_in['to_qkv_w'], 'L0_xattn_to_out_w': _L0_xattn_in['to_out_w'], 'L0_xattn_persist_mem': _L0_xattn_in['persist_mem'], 'L0_xattn_mem_pool_norm_w': _L0_xattn_in['mem_pool_norm_w'], 'L0_xattn_to_mem_tokens_w': _L0_xattn_in['to_mem_tokens_w'], 'L0_xattn_ff_norm_w': _L0_xattn_in['ff_norm_w'], 'L0_xattn_ff_w1': _L0_xattn_in['ff_w1'], 'L0_xattn_ff_b1': _L0_xattn_in['ff_b1'], 'L0_xattn_ff_w2': _L0_xattn_in['ff_w2'], 'L0_xattn_ff_b2': _L0_xattn_in['ff_b2'], 'L1_xattn_Wq': _L1_xattn_in['Wq'], 'L1_xattn_bq': _L1_xattn_in['bq'], 'L1_xattn_Wk': _L1_xattn_in['Wk'], 'L1_xattn_bk': _L1_xattn_in['bk'], 'L1_xattn_Wv': _L1_xattn_in['Wv'], 'L1_xattn_bv': _L1_xattn_in['bv'], 'L1_xattn_Wo': _L1_xattn_in['Wo'], 'L1_xattn_bo': _L1_xattn_in['bo'], 'L1_xattn_gamma': _L1_xattn_in['gamma'], 'L1_xattn_beta': _L1_xattn_in['beta'], 'L2_xattn_Wq1': _L2_xattn_in['Wq1'], 'L2_xattn_Wkv1': _L2_xattn_in['Wkv1'], 'L2_xattn_Wo1': _L2_xattn_in['Wo1'], 'L2_xattn_bo1': _L2_xattn_in['bo1'], 'L2_xattn_Wq2': _L2_xattn_in['Wq2'], 'L2_xattn_Wkv2': _L2_xattn_in['Wkv2'], 'L2_xattn_Wo2': _L2_xattn_in['Wo2'], 'L2_xattn_bo2': _L2_xattn_in['bo2'], 'L2_xattn_Wff1': _L2_xattn_in['Wff1'], 'L2_xattn_bff1': _L2_xattn_in['bff1'], 'L2_xattn_Wff2': _L2_xattn_in['Wff2'], 'L2_xattn_bff2': _L2_xattn_in['bff2'], 'L2_xattn_ln1_s': _L2_xattn_in['ln1_s'], 'L2_xattn_ln1_b': _L2_xattn_in['ln1_b'], 'L2_xattn_ln2_s': _L2_xattn_in['ln2_s'], 'L2_xattn_ln2_b': _L2_xattn_in['ln2_b'], 'L2_xattn_ln3_s': _L2_xattn_in['ln3_s'], 'L2_xattn_ln3_b': _L2_xattn_in['ln3_b']}

def reference(x, ctx_1024, L0_xattn_attn_norm_w, L0_xattn_to_qkv_w, L0_xattn_to_out_w, L0_xattn_persist_mem, L0_xattn_mem_pool_norm_w, L0_xattn_to_mem_tokens_w, L0_xattn_ff_norm_w, L0_xattn_ff_w1, L0_xattn_ff_b1, L0_xattn_ff_w2, L0_xattn_ff_b2, L1_xattn_Wq, L1_xattn_bq, L1_xattn_Wk, L1_xattn_bk, L1_xattn_Wv, L1_xattn_bv, L1_xattn_Wo, L1_xattn_bo, L1_xattn_gamma, L1_xattn_beta, L2_xattn_Wq1, L2_xattn_Wkv1, L2_xattn_Wo1, L2_xattn_bo1, L2_xattn_Wq2, L2_xattn_Wkv2, L2_xattn_Wo2, L2_xattn_bo2, L2_xattn_Wff1, L2_xattn_bff1, L2_xattn_Wff2, L2_xattn_bff2, L2_xattn_ln1_s, L2_xattn_ln1_b, L2_xattn_ln2_s, L2_xattn_ln2_b, L2_xattn_ln3_s, L2_xattn_ln3_b):
    import jax
    import jax.numpy as jnp

    def _L0_xattn_ref(x, mem_out, attn_norm_w, to_qkv_w, to_out_w, persist_mem, mem_pool_norm_w, to_mem_tokens_w, ff_norm_w, ff_w1, ff_b1, ff_w2, ff_b2):
        import jax, jax.numpy as jnp
        import numpy as np
        B, N, DIM = (2, 256, 128)
        HEADS, DH = (16, 64)
        SEG = 64
        NPM = 16
        NM = 16
        DFF = int(DIM * 4 * 2 / 3)
        EPS = 1.1920929e-07

        def rms_norm(x, w):
            return x * jax.lax.rsqrt(jnp.mean(x * x, axis=-1, keepdims=True) + EPS) * w
        b, n, _ = x.shape
        split_heads = lambda t: t.reshape(b, -1, HEADS, DH).transpose(0, 2, 1, 3)
        pooled = rms_norm(mem_out.mean(axis=1), mem_pool_norm_w)
        mem_tok = jnp.broadcast_to((pooled @ to_mem_tokens_w)[:, None, :], (b, NM, DIM))
        _, k_c, v_c = jnp.split(mem_tok @ to_qkv_w, 3, axis=-1)
        k_extra, v_extra = (split_heads(k_c), split_heads(v_c))
        xn = rms_norm(x, attn_norm_w)
        q, k, v = jnp.split(xn @ to_qkv_w, 3, axis=-1)
        q, k, v = (split_heads(q), split_heads(k), split_heads(v))
        pos = jnp.arange(n)
        inv = 1.0 / 10000.0 ** (jnp.arange(0, DH, 2, dtype=jnp.float32) / DH)
        ang = jnp.repeat(pos[:, None].astype(jnp.float32) * inv[None, :], 2, axis=-1)
        cos, sin = (jnp.cos(ang), jnp.sin(ang))

        def rope(t):
            z = t.reshape(t.shape[:-1] + (-1, 2))
            rh = jnp.stack([-z[..., 1], z[..., 0]], axis=-1).reshape(t.shape)
            return t * cos + rh * sin
        q, k = (rope(q), rope(k))
        pm = jnp.broadcast_to(persist_mem[None], (b, HEADS, NPM, DH))
        kf = jnp.concatenate([k_extra, pm, k], axis=2)
        vf = jnp.concatenate([v_extra, pm, v], axis=2)
        P = NPM + NM
        ki = jnp.arange(kf.shape[2])[None, :]
        qi = pos[:, None]
        causal = qi >= ki - P
        seg = qi // SEG == (ki - P) // SEG
        mask = causal & seg | (ki < P)
        scores = jnp.einsum('bhid,bhjd->bhij', q, kf) * DH ** (-0.5)
        scores = jnp.where(mask[None, None], scores, -1e+30)
        probs = jax.nn.softmax(scores, axis=-1)
        o = jnp.einsum('bhij,bhjd->bhid', probs, vf)
        attn_out = o.transpose(0, 2, 1, 3).reshape(b, n, HEADS * DH) @ to_out_w
        x = x + attn_out
        h = rms_norm(x, ff_norm_w) @ ff_w1 + ff_b1
        a, g = jnp.split(h, 2, axis=-1)
        x = x + jax.nn.silu(g) * a @ ff_w2 + ff_b2
        return x

    def _L1_xattn_ref(queries, keys, values, Wq, bq, Wk, bk, Wv, bv, Wo, bo, gamma, beta):
        import jax, jax.numpy as jnp
        import numpy as np
        D_MODEL = 128
        HEADS = 16
        D_K = D_MODEL // HEADS
        B, Nq, D = queries.shape
        Nk = keys.shape[1]
        q = (queries @ Wq.T + bq).reshape(B, Nq, HEADS, D_K).transpose(0, 2, 1, 3)
        k = (keys @ Wk.T + bk).reshape(B, Nk, HEADS, D_K).transpose(0, 2, 1, 3)
        v = (values @ Wv.T + bv).reshape(B, Nk, HEADS, D_K).transpose(0, 2, 1, 3)
        att = jnp.einsum('bhqd,bhkd->bhqk', q, k) / np.sqrt(D_K).astype(np.float32)
        att = jax.nn.softmax(att, axis=-1)
        out = jnp.einsum('bhqk,bhkd->bhqd', att, v)
        out = out.transpose(0, 2, 1, 3).reshape(B, Nq, HEADS * D_K)
        out = out @ Wo.T + bo
        out = queries + out
        mean = jnp.mean(out, axis=-1, keepdims=True)
        var = jnp.var(out, axis=-1, keepdims=True)
        out = (out - mean) / jnp.sqrt(var + 1e-05) * gamma + beta
        return out

    def _L2_xattn_ref(hidden_states, context, Wq1, Wkv1, Wo1, bo1, Wq2, Wkv2, Wo2, bo2, Wff1, bff1, Wff2, bff2, ln1_s, ln1_b, ln2_s, ln2_b, ln3_s, ln3_b):
        import jax, jax.numpy as jnp
        import numpy as np
        from functools import partial
        HEADS = 16
        DIM_HEAD = 64
        SCALE = DIM_HEAD ** (-0.5)
        MAX_ALLOWABLE = 128 * 128 * 8
        EPS = 1e-05

        def ln32(x, scale, bias):
            x32 = x.astype(jnp.float32)
            mean = jnp.mean(x32, axis=-1, keepdims=True)
            var = jnp.mean(jnp.square(x32 - mean), axis=-1, keepdims=True)
            y = (x32 - mean) * jax.lax.rsqrt(var + EPS) * scale.astype(jnp.float32) + bias.astype(jnp.float32)
            return y.astype(x.dtype)

        def heads_to_batch(t):
            b, s, d = t.shape
            return t.reshape(b, s, HEADS, d // HEADS).transpose(0, 2, 1, 3).reshape(b * HEADS, s, d // HEADS)

        def batch_to_heads(t):
            bh, s, dh = t.shape
            return t.reshape(bh // HEADS, HEADS, s, dh).transpose(0, 2, 1, 3).reshape(bh // HEADS, s, dh * HEADS)

        def _max_pow2(n):
            i = 1
            while n % 2 == 0:
                i *= 2
                n //= 2
            return i

        def sdpa(q, k, v):
            scores = jnp.einsum('bid,bjd->bij', q, k) * SCALE
            probs = jax.nn.softmax(scores, axis=2)
            return jnp.einsum('bij,bjd->bid', probs, v)

        def lowmem_attention(q, k, v):
            dimprod = q.shape[0] * q.shape[1] * k.shape[1]
            true_divisor = dimprod / MAX_ALLOWABLE
            if true_divisor < 1:
                n_splits = 1
            elif true_divisor >= q.shape[0]:
                n_splits = q.shape[0]
            else:
                nearest_pow2 = 2 ** np.round(np.log2(true_divisor))
                n_splits = int(min(_max_pow2(q.shape[0]), nearest_pow2))
            nq, nk, nv = [h.reshape(n_splits, h.shape[0] // n_splits, h.shape[-2], h.shape[-1]) for h in (q, k, v)]
            outs = jax.lax.scan(lambda c, a: (None, sdpa(*a)), None, (nq, nk, nv))[1]
            return outs.reshape(-1, outs.shape[-2], outs.shape[-1])

        def attention(x, ctx, Wq, Wkv, Wo, bo):
            q = x @ Wq
            k, v = jnp.split(ctx @ Wkv, 2, axis=-1)
            out = lowmem_attention(heads_to_batch(q), heads_to_batch(k), heads_to_batch(v))
            return batch_to_heads(out) @ Wo + bo

        def geglu_ff(x, Wff1, bff1, Wff2, bff2):
            h = x @ Wff1 + bff1
            lin, gelu = jnp.split(h, 2, axis=-1)
            h = lin * (gelu * jax.nn.sigmoid(1.702 * gelu))
            return h @ Wff2 + bff2
        x = hidden_states
        x = attention(ln32(x, ln1_s, ln1_b), ln32(x, ln1_s, ln1_b), Wq1, Wkv1, Wo1, bo1) + x
        x = attention(ln32(x, ln2_s, ln2_b), context, Wq2, Wkv2, Wo2, bo2) + x
        x = geglu_ff(ln32(x, ln3_s, ln3_b), Wff1, bff1, Wff2, bff2) + x
        return x

    def _L3_xattn_ref(H_real, H_fake):
        import jax, jax.numpy as jnp
        import numpy as np
        B, SR, SF, D = (8, 256, 256, 128)
        scores = jnp.einsum('brd,bfd->brf', H_real, H_fake)
        weights = jax.nn.softmax(scores, axis=-1)
        context = jnp.einsum('brf,bfd->brd', weights, H_fake)
        return H_real + context
    x = _L0_xattn_ref(x, ctx_1024, L0_xattn_attn_norm_w, L0_xattn_to_qkv_w, L0_xattn_to_out_w, L0_xattn_persist_mem, L0_xattn_mem_pool_norm_w, L0_xattn_to_mem_tokens_w, L0_xattn_ff_norm_w, L0_xattn_ff_w1, L0_xattn_ff_b1, L0_xattn_ff_w2, L0_xattn_ff_b2)
    x = _L1_xattn_ref(x, ctx_1024, ctx_1024, L1_xattn_Wq, L1_xattn_bq, L1_xattn_Wk, L1_xattn_bk, L1_xattn_Wv, L1_xattn_bv, L1_xattn_Wo, L1_xattn_bo, L1_xattn_gamma, L1_xattn_beta)
    x = _L2_xattn_ref(x, ctx_1024, L2_xattn_Wq1, L2_xattn_Wkv1, L2_xattn_Wo1, L2_xattn_bo1, L2_xattn_Wq2, L2_xattn_Wkv2, L2_xattn_Wo2, L2_xattn_bo2, L2_xattn_Wff1, L2_xattn_bff1, L2_xattn_Wff2, L2_xattn_bff2, L2_xattn_ln1_s, L2_xattn_ln1_b, L2_xattn_ln2_s, L2_xattn_ln2_b, L2_xattn_ln3_s, L2_xattn_ln3_b)
    x = _L3_xattn_ref(x, ctx_1024)
    return x

_drawn_inputs = setup_inputs


def setup_inputs(seed=0):
    import zlib

    import numpy as np

    out = dict(_drawn_inputs(seed))
    spreads = {'L0_xattn_attn_norm_w': (1.0, 0.6),
     'L0_xattn_mem_pool_norm_w': (1.0, 0.6),
     'L0_xattn_ff_norm_w': (1.0, 0.6),
     'L0_xattn_ff_b1': (0.0, 0.689),
     'L0_xattn_ff_b2': (0.0, 0.1),
     'L1_xattn_bq': (0.0, 0.1),
     'L1_xattn_bk': (0.0, 2.0),
     'L1_xattn_bv': (0.0, 0.1),
     'L1_xattn_bo': (0.0, 0.1),
     'L1_xattn_gamma': (1.0, 0.2),
     'L1_xattn_beta': (0.0, 0.1),
     'L2_xattn_bo1': (0.0, 0.1),
     'L2_xattn_bo2': (0.0, 0.1),
     'L2_xattn_bff1': (0.0, 0.517),
     'L2_xattn_bff2': (0.0, 0.1),
     'L2_xattn_ln1_s': (1.0, 0.6),
     'L2_xattn_ln1_b': (0.0, 0.745),
     'L2_xattn_ln2_s': (1.0, 0.6),
     'L2_xattn_ln2_b': (0.0, 2.0),
     'L2_xattn_ln3_s': (1.0, 0.6),
     'L2_xattn_ln3_b': (0.0, 0.8)}
    factors = {'L0_xattn_to_mem_tokens_w': 2.873, 'L2_xattn_Wq1': 48.159, 'L2_xattn_Wq2': 64.0}
    for name, (base, spread) in spreads.items():
        noise = np.random.default_rng([zlib.crc32(name.encode()), seed]).standard_normal(out[name].shape)
        drawn = base * np.exp(spread * noise) if base else spread * noise
        out[name] = jnp.asarray(drawn.astype(out[name].dtype))
    for name, factor in factors.items():
        out[name] = (out[name] * factor).astype(out[name].dtype)
    return out
```

```python
from contextlib import ExitStack

import numpy as np

import concourse.bass as bass
from concourse import mybir

F32 = mybir.dt.float32
BF16 = mybir.dt.bfloat16
ALU = mybir.AluOpType
ACT = mybir.ActivationFunctionType
AX = mybir.AxisListType

B, T, S, D = 32, 100, 1444, 128
H = 16
P = 128
NFULL = S // P
TAIL = S - NFULL * P
CHUNKS = [(c * P, P) for c in range(NFULL)] + [(NFULL * P, TAIL)]
NC = len(CHUNKS)
DH0, NPM, NM, SEG = 64, 16, 16, 64
PAIRS = H // 2
KEYS0 = T + 1 + NPM
E0 = H * DH0
DFF0 = int(D * 4 * 2 / 3)
FF0_TILES = 3
FF0 = -(-DFF0 // FF0_TILES)
FF2_TILES = 4
DH = D // H
TERMS = [("hi", "hi"), ("mid", "hi"), ("hi", "mid"), ("mid", "mid"), ("lo", "hi"), ("hi", "lo")]
KROWS = len(TERMS) * 2 * DH
VW = DH + 1
VWIN = 32
VCOLS = H * VW + VWIN - VW
EPS_RMS, EPS_LN = 1.1920929e-07, 1e-05
GELU = 1.702

COLS = ["attn_norm", "mem_norm", "ff_norm", "bq", "bk", "bv", "ln1_s", "ln1_b", "ln2_s", "ln2_b", "ln3_s", "ln3_b"]
ROWS = ["ff_b2", "bo", "gamma", "beta", "bo1", "bo2", "bff2"]

LIGHT_BANKS = 3
LIGHT = [
    ("pool_ms", 1, "dve"), ("mem", 1, "dve"), ("xn", 1, "dve"), ("qk", PAIRS, "dve"), ("val0", 2, "act"), ("score0", 4, "dve"), ("probT0", 4, "act"), ("oT0", 2, "act"),
    ("out0", 1, "dve"), ("fx0", 1, "dve"), ("ffa", 1, "dve"), ("ffg", 1, "dve"), ("ffo", 1, "dve"),
    ("x1T", 1, "dve"), ("q1", 1, "dve"), ("k1", 3, "act"), ("v1", 3, "dve"), ("max1T", 1, "dve"), ("pv1T", 1, "dve"), ("o1T", 1, "dve"), ("out1", 1, "dve"),
    ("hT", 1, "dve"), ("qs", 1, "dve"), ("ks", 1, "dve"), ("vs", 1, "dve"), ("scs", 4, "dve"), ("probTs", 4, "act"), ("os", 1, "dve"), ("osT", 1, "dve"), ("outs", 1, "dve"),
    ("h2T", 1, "dve"), ("q2", 1, "dve"), ("k2", 3, "act"), ("v2", 3, "dve"), ("max2T", 1, "dve"), ("pv2T", 1, "dve"), ("o2T", 1, "dve"), ("out2", 1, "dve"),
    ("h3T", 1, "dve"), ("lin", 1, "dve"), ("gate", 1, "dve"), ("ff2o", 1, "dve"),
    ("x3T", 1, "dve"), ("sc3", 3, "act"), ("pT3", 3, "dve"), ("out3", 1, "dve"),
]
USES = [(name, i) for name, n, _ in LIGHT for i in range(n)]
READER = {name: reader for name, _, reader in LIGHT}
NORMS = ["xs0", "xs_ff", "xs_l1", "xs_ln1", "xs_ln2", "xs_ln3"]


def xattn_program(nc, a):
    with ExitStack() as ctx:
        def sb(name, shape, dt=F32):
            return ctx.enter_context(nc.sbuf_tensor(name, shape, dt))

        sems = {}

        def sem(name):
            if name in READER:
                name = "light_filled"
            elif name.removesuffix("_out") in READER:
                name = "light_read_" + READER[name.removesuffix("_out")]
            if name not in sems:
                sems[name] = ctx.enter_context(nc.semaphore(name))
            return sems[name]

        def nth(name, n):
            base = name.removesuffix("_out")
            if base not in READER:
                return sem(name), n
            at = USES.index((base, n - 1))
            if name in READER:
                return sem(name), at + 1
            return sem(name), sum(READER[use] == READER[base] for use, _ in USES[:at + 1])

        loaded = ctx.enter_context(nc.semaphore("weights_loaded"))
        preset = ctx.enter_context(nc.semaphore("preset"))

        ident = sb("ident", [P, P])
        ones_mean = sb("ones_mean", [P, P])
        cos2 = sb("cos2", [P, 2 * (T + 1)])
        sin2 = sb("sin2", [P, 2 * (T + 1)])
        mask0 = sb("mask0", [T, KEYS0])
        head_mask = sb("head_mask", [P, H])
        cols = sb("cols", [P, len(COLS)])
        rows = sb("rows", [T, len(ROWS) * D])
        w_qkv = sb("w_qkv", [P, 3 * E0])
        w_rot = sb("w_rot", [P, 2 * E0])
        w_out0 = sb("w_out0", [P, PAIRS, D])
        w_mem = sb("w_mem", [P, D])
        w_ff1 = sb("w_ff1", [P, 2 * FF0_TILES * FF0])
        b_ff1 = sb("b_ff1", [FF0, 2 * FF0_TILES])
        w_ff2 = sb("w_ff2", [FF0, FF0_TILES, D])
        w1 = sb("w1", [P, 4, D])
        wq1 = sb("wq1", [P, D])
        wkv1 = sb("wkv1", [P, 2 * D])
        wo1 = sb("wo1", [P, D])
        wq2 = sb("wq2", [P, D])
        wkv2 = sb("wkv2", [P, 2 * D])
        wo2 = sb("wo2", [P, D])
        wf1 = sb("wf1", [P, 2 * FF2_TILES * D])
        bf1 = sb("bf1", [P, 2 * FF2_TILES])
        wf2 = sb("wf2", [P, FF2_TILES, D])

        def col(name):
            return cols[:, COLS.index(name):COLS.index(name) + 1]

        def row(name):
            return rows[:, ROWS.index(name) * D:(ROWS.index(name) + 1) * D]

        x0 = sb("x0", [T, D])
        ctxT = sb("ctxT", [P, S])
        ctxN = sb("ctxN", [P, NC, D])
        pool = sb("pool", [P, 4])
        xnT = sb("xnT", [P, T + 1])
        rope_a = sb("rope_a", [P, 2, 2 * (T + 1)])
        rope_b = sb("rope_b", [P, 2, 2 * (T + 1)])
        qT0 = sb("qT0", [P, PAIRS, T])
        kbd0 = sb("kbd0", [P, PAIRS, 2, KEYS0])
        val0 = sb("val0", [KEYS0, E0])
        sm = sb("sm", [T, H, KEYS0])
        probT = sb("probT", [KEYS0, H, T])
        oT0 = sb("oT0", [P, PAIRS, T])
        stat = sb("stat", [P, 64])
        junk = sb("junk", [T, D])
        xs = sb("xs", [T, D])
        hT = sb("hT", [P, T])
        gate = sb("gate", [P, 4, T])
        egate = sb("egate", [P, 4, T])
        hid = sb("hid", [P, 4, T])
        x1 = sb("x1", [T, D])
        x2 = sb("x2", [T, D])
        qf = sb("qf", [P, T])
        qr = sb("qr", [P, T])
        qpart = {n: sb("q" + n, [P, T], BF16) for n in ("hi", "mid", "lo")}
        kf = sb("kf", [P, S])
        kr = sb("kr", [P, S])
        kpart = {n: sb("k" + n, [P, S], BF16) for n in ("hi", "mid", "lo")}
        q_rows = sb("q_rows", [P, H, T], BF16)
        k_stack = sb("k_stack", [KROWS + 1, PAIRS, S], BF16)
        q_stack = sb("q_stack", [KROWS + 1, H, T], BF16)
        v_aug = sb("v_aug", [P, NC, VCOLS])
        prob = [sb(f"prob{i}", [P, H // 2 * T]) for i in range(3)]
        mx = sb("mx", [P, 13, 2])
        mxm = sb("mxm", [P, 13])
        mrow = sb("mrow", [13, P], BF16)
        pv = sb("pv", [P, 4 * T])
        on = sb("on", [T, D])
        oT = sb("oT", [P, T])
        kbds = sb("kbds", [P, H, T])
        vs = sb("vs", [T, D])
        p3 = sb("p3", [T, S])
        pT3 = sb("pT3", [P, NC, T])
        y = sb("y", [T, D])
        q_dram = nc.dram_tensor("q_parts", (3, D, T), BF16).ap()
        minus_half = sb("minus_half", [P, 1])

        heavy = ctx.enter_context(nc.psum_tensor("heavy", [P, 4, 512], F32))
        pv_acc = ctx.enter_context(nc.psum_tensor("pv_acc", [P, 512], F32))
        light = ctx.enter_context(nc.psum_tensor("light", [P, LIGHT_BANKS, 512], F32))

        def bank(name, i=0):
            return light[:, USES.index((name, i)) % LIGHT_BANKS, :]

        def bank_free(eng, name, i=0):
            n = USES.index((name, i)) - LIGHT_BANKS
            if n >= 0:
                before, k = USES[n]
                eng.wait_ge(*nth(before + "_out", k + 1))

        loads = [
            (ident[:], a["c_ident"]), (ones_mean[:], a["c_mean"]), (cos2[:], a["c_cos"]), (sin2[:], a["c_sin"]),
            (mask0[:], a["c_mask"]), (head_mask[:], a["c_head_mask"]), (cols[:], a["cols"]), (rows[:], a["rows"]),
            (w_qkv[:], a["w_qkv"]), (w_rot[:], a["w_rot"]), (w_out0[:], a["w_out0"]), (w_mem[:], a["w_mem"]),
            (w_ff1[:], a["w_ff1"]), (b_ff1[:], a["b_ff1"]), (w_ff2[:], a["w_ff2"]), (w1[:], a["w1"]),
            (wq1[:], a["wq1"]), (wkv1[:], a["wkv1"]), (wo1[:], a["wo1"]),
            (wq2[:], a["wq2"]), (wkv2[:], a["wkv2"]), (wo2[:], a["wo2"]),
            (wf1[:], a["wf1"]), (bf1[:], a["bf1"]), (wf2[:], a["wf2"]),
            (val0[T + 1:KEYS0, :], a["pm_v"]),
        ]
        with nc.Block() as block:
            @block.sync
            def _(sp):
                for dst, src in loads:
                    sp.dma_start(dst, src).then_inc(loaded, 16)
                sp.wait_ge(preset, 1)
                for j in range(2):
                    sp.dma_start(kbd0[64 * j:64 * j + 64, :, j, T + 1:KEYS0],
                                 a["pm_k"][64 * j:64 * j + 64]).then_inc(loaded, 16)
                sp.wait_ge(loaded, 16 * (len(loads) + 2))

            @block.vector
            def _(dve):
                nc.vector.memset(k_stack[KROWS:KROWS + 1], 1.0)

            @block.gpsimd
            def _(pool_eng):
                nc.gpsimd.memset(kbd0[:], 0.0).then_inc(preset, 1)
                nc.gpsimd.memset(q_stack[0:KROWS], 0.0)
                nc.gpsimd.memset(v_aug[:], 0.0).then_inc(preset, 1)
                nc.gpsimd.memset(mxm[:], 0.0)
                nc.gpsimd.memset(minus_half[:], -0.5)
                pool_eng.wait_ge(preset, 2)
                nc.gpsimd.memset(v_aug[:, :, 0:H * VW].rearrange("p c (h w) -> p c h w", w=VW)[:, :, :, DH:VW],
                                 1.0).then_inc(preset, 1)

        with nc.Fori(0, B) as b:
            with nc.Block() as block:
                @block.sync
                def _(sp):
                    sp.dma_start(x0[:], a["x"][b]).then_inc(sem("x0_in"), 16)
                    sp.dma_start(ctxT[:], a["ctxT"][b]).then_inc(sem("ctxT_in"), 16)
                    sp.dma_start(ctxN[:, 0:NFULL, :], a["ctx_main"][b]).then_inc(sem("ctxN_in"), 16)
                    sp.dma_start(ctxN[0:TAIL, NFULL, :], a["ctx_tail"][b]).then_inc(sem("ctxN_in"), 16)

                    def stack(layer):
                        if layer == 2:
                            sp.wait_ge(*nth("prob1_used", 2 * NC))
                        for part in ("hi", "mid", "lo"):
                            sp.wait_ge(*nth(f"k{layer}_{part}", 3 if part == "hi" else 1))
                            for t, (kp, _) in enumerate(TERMS):
                                if kp == part:
                                    for p in range(PAIRS):
                                        sp.dma_start(k_stack[16 * t:16 * t + 16, p, :],
                                                     kpart[part][16 * p:16 * p + 16, :]).then_inc(sem(f"k{layer}_stacked"), 16)

                    def queries(layer):
                        for n, part in enumerate(("hi", "mid", "lo")):
                            sp.wait_ge(*nth(f"q{layer}_{part}", 1))
                            sp.dma_start(q_dram[n], qpart[part][:]).then_inc(sem(f"q{layer}_parked"), 16)
                        sp.wait_ge(*nth(f"q{layer}_parked", 48))
                        for t, (_, qp) in enumerate(TERMS):
                            src = q_dram[("hi", "mid", "lo").index(qp)].rearrange("(p j d) t -> j d p t", j=2, d=DH)
                            for j in range(2):
                                r = 16 * t + DH * j
                                sp.dma_start(q_stack[r:r + DH, j::2, :], src[j]).then_inc(sem(f"q{layer}_stacked"), 16)

                    def maxima(layer):
                        flat = q_stack[KROWS:KROWS + 1].rearrange("p h t -> p (h t)")
                        sp.wait_ge(*nth(f"max{layer}T_out", 1))
                        sp.dma_start(flat[:, 0:12 * P], mrow[0:12, :]).then_inc(sem(f"max{layer}_stacked"), 16)
                        sp.dma_start(flat[:, 12 * P:H * T], mrow[12:13, 0:H * T - 12 * P]).then_inc(sem(f"max{layer}_stacked"), 16)

                    queries(1)
                    stack(1)
                    maxima(1)
                    stack(2)
                    queries(2)
                    maxima(2)
                    sp.wait_ge(*nth("y", 1))
                    sp.dma_start(a["out"][b], y[:]).then_inc(sem("stored"), 16)
                    sp.wait_ge(*nth("stored", 16))

                @block.tensor
                def _(pe):
                    mm = nc.tensor.matmul

                    def transpose(name, src, width, rows_, wait):
                        pe.wait_ge(*(nth("xs", NORMS.index(wait) + 1) if wait in NORMS else nth(wait, 1)))
                        bank_free(pe, name)
                        nc.tensor.transpose(bank(name)[0:width, 0:rows_], src, ident[0:rows_, 0:rows_]).then_inc(sem(name), 1)

                    def project(name, lhsT, rhs, m, n, wait):
                        pe.wait_ge(*nth(wait, 1))
                        bank_free(pe, name)
                        mm(bank(name)[0:m, 0:n], lhsT, rhs, start=True, stop=True).then_inc(sem(name), 1)

                    def l0():
                        project("pool_ms", ones_mean[:], pool[:, 1:2], P, 1, "pool_sq")
                        project("mem", w_mem[:], pool[:, 3:4], P, 1, "pool_normed")
                        transpose("xn", xs[:], D, T, "xs0")
                        pe.wait_ge(*nth("xn_out", 1))
                        pe.wait_ge(*nth("mem_out", 1))
                        W = T + 1
                        for p in range(PAIRS):
                            bank_free(pe, "qk", p)
                            for n, (w, at) in enumerate(((w_qkv, 0), (w_qkv, E0), (w_rot, 0), (w_rot, E0))):
                                last = mm(bank("qk", p)[:, n * W:(n + 1) * W], w[:, at + p * P:at + (p + 1) * P], xnT[:],
                                          start=True, stop=True)
                            last.then_inc(sem("qk"), 1)
                        for n in range(2):
                            bank_free(pe, "val0", n)
                            mm(bank("val0", n)[0:W, :], xnT[:], w_qkv[:, 2 * E0 + n * 512:2 * E0 + (n + 1) * 512],
                               start=True, stop=True).then_inc(sem("val0"), 1)
                        for g in range(4):
                            pe.wait_ge(*nth("roped", 3 * (2 * g + 2)))
                            bank_free(pe, "score0", g)
                            for i in range(2):
                                p = 2 * g + i
                                last = mm(bank("score0", g)[0:T, i * 2 * KEYS0:(i + 1) * 2 * KEYS0], qT0[:, p, :],
                                          kbd0[:, p].rearrange("p j k -> p (j k)"), start=True, stop=True)
                            last.then_inc(sem("score0"), 1)
                        for g in range(4):
                            pe.wait_ge(*nth("prob0", g + 1))
                            bank_free(pe, "probT0", g)
                            for i in range(4):
                                last = nc.tensor.transpose(bank("probT0", g)[0:KEYS0, i * T:(i + 1) * T], sm[:, 4 * g + i, :],
                                                           ident[0:T, 0:T])
                            last.then_inc(sem("probT0"), 1)
                        pe.wait_ge(*nth("val0_out", 2))
                        for n in range(2):
                            pe.wait_ge(*nth("probT0_out", 2 * n + 2))
                            bank_free(pe, "oT0", n)
                            for i in range(8):
                                h = 8 * n + i
                                j, k = h % 2, i // 2
                                last = mm(bank("oT0", n)[64 * j:64 * j + 64, k * T:(k + 1) * T], val0[:, h * DH0:(h + 1) * DH0],
                                          probT[:, h, :], start=True, stop=True)
                            last.then_inc(sem("oT0"), 1)
                        pe.wait_ge(*nth("oT0_out", 2))
                        bank_free(pe, "out0")
                        for p in range(PAIRS):
                            last = mm(bank("out0")[0:T, 0:D], oT0[:, p, :], w_out0[:, p, :], start=(p == 0), stop=(p == PAIRS - 1))
                        last.then_inc(sem("out0"), 1)
                        transpose("fx0", xs[:], D, T, "xs_ff")
                        pe.wait_ge(*nth("fx0_out", 1))
                        for n, name in enumerate(("ffa", "ffg")):
                            bank_free(pe, name)
                            for t in range(FF0_TILES):
                                at = (n * FF0_TILES + t) * FF0
                                last = mm(bank(name)[0:FF0, t * T:(t + 1) * T], w_ff1[:, at:at + FF0], hT[:], start=True, stop=True)
                            last.then_inc(sem(name), 1)
                        pe.wait_ge(*nth("hid0", 1))
                        bank_free(pe, "ffo")
                        for t in range(FF0_TILES):
                            last = mm(bank("ffo")[0:T, 0:D], hid[0:FF0, t, :], w_ff2[:, t, :], start=(t == 0), stop=(t == FF0_TILES - 1))
                        last.then_inc(sem("ffo"), 1)

                    def cross_keys(layer, wk, wv):
                        pe.wait_ge(*nth("ctxT_in", 16))
                        for n in range(3):
                            bank_free(pe, f"k{layer}", n)
                            at, w = K_CUTS[n]
                            mm(bank(f"k{layer}", n)[:, 0:w], wk, ctxT[:, at:at + w], start=True, stop=True).then_inc(sem(f"k{layer}"), 1)
                        for n in range(3):
                            bank_free(pe, f"v{layer}", n)
                            for i in range(4):
                                at, w = CHUNKS[4 * n + i]
                                last = mm(bank(f"v{layer}", n)[0:w, i * D:(i + 1) * D], ctxT[:, at:at + w], wv, start=True, stop=True)
                            last.then_inc(sem(f"v{layer}"), 1)

                    def cross(layer):
                        L = str(layer)
                        flat = q_rows[:].rearrange("p h t -> p (h t)")
                        pe.wait_ge(*nth(f"q{L}_rows", 1))
                        pe.wait_ge(*nth(f"k{L}_hi", 3))
                        for n in range(2 * 13):
                            t, s = n // 2, n % 2
                            w = min(P, H * T - t * P)
                            if n >= 2:
                                pe.wait_ge(*nth(f"max{L}_read", n - 1))
                            for i in range(2):
                                at = (2 * s + i) * (S // 4)
                                last = mm(heavy[0:w, 2 * (n % 2) + i, 0:S // 4], flat[:, t * P:t * P + w], kpart["hi"][:, at:at + S // 4],
                                          start=True, stop=True)
                            last.then_inc(sem(f"max{L}_scored"), 1)
                        transpose(f"max{L}T", mxm[:], 13, P, f"max{L}")
                        pe.wait_ge(*nth(f"k{L}_stacked", 16 * len(TERMS) * PAIRS))
                        pe.wait_ge(*nth(f"q{L}_stacked", 16 * len(TERMS) * 2))
                        pe.wait_ge(*nth(f"max{L}_stacked", 32))
                        pe.wait_ge(*nth(f"v{L}_out", 3))
                        qs = q_stack[:].rearrange("p h t -> p (h t)")

                        def scores(u):
                            c, half, slot = u // 2, u % 2, u % 2
                            at, w = CHUNKS[c]
                            if u >= 2:
                                pe.wait_ge(*nth(f"prob{L}", u - 1))
                            else:
                                pe.wait_ge(*nth(f"max{L}_read", 2 * 13))
                            for i in range(4):
                                p = 4 * half + i
                                last = mm(heavy[0:w, 2 * slot + i // 2, (i % 2) * 2 * T:(i % 2 + 1) * 2 * T],
                                          k_stack[:, p, at:at + w], qs[:, 2 * p * T:2 * (p + 1) * T], start=True, stop=True)
                            last.then_inc(sem(f"score{L}"), 1)

                        def values(u):
                            c, half = u // 2, u % 2
                            w = CHUNKS[c][1]
                            pe.wait_ge(*nth(f"prob{L}", u + 1))
                            for i in range(8):
                                h = 8 * half + i
                                j, g = h % 4, h // 4
                                last = mm(pv_acc[VWIN * j:VWIN * (j + 1), g * T:(g + 1) * T], v_aug[0:w, c, VW * h:VW * h + VWIN],
                                          prob[u % 3][0:w, i * T:(i + 1) * T], start=(c == 0 and g == 0), stop=(c == NC - 1),
                                          skip_group_check=True)
                            last.then_inc(sem(f"prob{L}_used"), 1)

                        for u in range(2 * NC):
                            scores(u)
                            if u:
                                values(u - 1)
                        values(2 * NC - 1)
                        pe.wait_ge(*nth(f"pv{L}", 1))
                        bank_free(pe, f"pv{L}T")
                        for g in range(4):
                            last = nc.tensor.transpose(bank(f"pv{L}T")[0:T, g * P:(g + 1) * P], pv[:, g * T:(g + 1) * T], ident[:])
                        last.then_inc(sem(f"pv{L}T"), 1)
                        transpose(f"o{L}T", on[:], D, T, f"pv{L}T_out")
                        project(f"out{L}", oT[:], w1[:, 3, :] if layer == 1 else wo2[:], T, D, f"o{L}T_out")

                    def self_attention():
                        transpose("hT", xs[:], D, T, "xs_ln1")
                        project("qs", wq1[:], hT[:], D, T, "hT_out")
                        project("ks", wkv1[:, 0:D], hT[:], D, T, "hT_out")
                        project("vs", hT[:], wkv1[:, D:2 * D], T, D, "hT_out")
                        pe.wait_ge(*nth("qs_out", 1))
                        pe.wait_ge(*nth("ks_out", 1))
                        kb = kbds[:].rearrange("p h t -> p (h t)")
                        for g in range(4):
                            bank_free(pe, "scs", g)
                            mm(bank("scs", g)[0:T, 0:4 * T], qf[:], kb[:, g * 4 * T:(g + 1) * 4 * T], start=True, stop=True).then_inc(sem("scs"), 1)
                        for g in range(4):
                            pe.wait_ge(*nth("exps", g + 1))
                            bank_free(pe, "probTs", g)
                            for i in range(4):
                                last = nc.tensor.transpose(bank("probTs", g)[0:T, i * T:(i + 1) * T], sm[:, 4 * g + i, 0:T], ident[0:T, 0:T])
                            last.then_inc(sem("probTs"), 1)
                        pe.wait_ge(*nth("probTs_out", 4))
                        pe.wait_ge(*nth("vs_out", 1))
                        bank_free(pe, "os")
                        for h in range(H):
                            last = mm(bank("os")[0:T, h * DH:(h + 1) * DH], probT[0:T, h, :], vs[:, h * DH:(h + 1) * DH], start=True, stop=True)
                        last.then_inc(sem("os"), 1)
                        transpose("osT", on[:], D, T, "os_out")
                        project("outs", oT[:], wo1[:], T, D, "osT_out")

                    def ff2():
                        transpose("h3T", xs[:], D, T, "xs_ln3")
                        pe.wait_ge(*nth("h3T_out", 1))
                        for n, name in enumerate(("lin", "gate")):
                            bank_free(pe, name)
                            for t in range(FF2_TILES):
                                at = (n * FF2_TILES + t) * D
                                last = mm(bank(name)[:, t * T:(t + 1) * T], wf1[:, at:at + D], hT[:], start=True, stop=True)
                            last.then_inc(sem(name), 1)
                        pe.wait_ge(*nth("hid2", 1))
                        bank_free(pe, "ff2o")
                        for t in range(FF2_TILES):
                            last = mm(bank("ff2o")[0:T, 0:D], hid[:, t, :], wf2[:, t, :], start=(t == 0), stop=(t == FF2_TILES - 1))
                        last.then_inc(sem("ff2o"), 1)

                    def l3():
                        transpose("x3T", x2[:], D, T, "x6")
                        pe.wait_ge(*nth("x3T_out", 1))
                        for n in range(3):
                            at, w = K_CUTS[n]
                            bank_free(pe, "sc3", n)
                            mm(bank("sc3", n)[0:T, 0:w], hT[:], ctxT[:, at:at + w], start=True, stop=True).then_inc(sem("sc3"), 1)
                        pe.wait_ge(*nth("sc3_out", 3))
                        for n in range(3):
                            bank_free(pe, "pT3", n)
                            for i in range(4):
                                at, w = CHUNKS[4 * n + i]
                                last = nc.tensor.transpose(bank("pT3", n)[0:w, i * T:(i + 1) * T], p3[:, at:at + w], ident[0:T, 0:T])
                            last.then_inc(sem("pT3"), 1)
                        pe.wait_ge(*nth("ctxN_in", 32))
                        for c in range(NC):
                            if c % 4 == 0:
                                pe.wait_ge(*nth("pT3_out", c // 4 + 1))
                            if c == 0:
                                bank_free(pe, "out3")
                            w = CHUNKS[c][1]
                            last = mm(bank("out3")[0:T, 0:D], pT3[0:w, c, :], ctxN[0:w, c, :], start=(c == 0), stop=(c == NC - 1))
                        last.then_inc(sem("out3"), 1)

                    l0()
                    transpose("x1T", x2[:], D, T, "x2")
                    project("q1", w1[:, 0, :], hT[:], D, T, "x1T_out")
                    cross_keys(1, w1[:, 1, :], w1[:, 2, :])
                    cross(1)
                    self_attention()
                    transpose("h2T", xs[:], D, T, "xs_ln2")
                    project("q2", wq2[:], hT[:], D, T, "h2T_out")
                    cross_keys(2, wkv2[:, 0:D], wkv2[:, D:2 * D])
                    cross(2)
                    ff2()
                    l3()

                @block.scalar
                def _(act):
                    def exps(n, name, width, src_sem):
                        for g in range(4):
                            act.wait_ge(*nth(src_sem, g + 1))
                            v = sm[:, 4 * g:4 * g + 4, 0:width]
                            nc.scalar.activation(v, v, ACT.Exp, scale=0.125).then_inc(sem(name), 1)

                    def keys(layer):
                        for n in range(3):
                            at, w = K_CUTS[n]
                            act.wait_ge(*nth(f"k{layer}", n + 1))
                            if layer == 2 and n == 0:
                                act.wait_ge(*nth("k1_stacked", 16 * len(TERMS) * PAIRS))
                                act.wait_ge(*nth("max1_read", 2 * 13))
                            bias = col("bk") if layer == 1 else 0.0
                            nc.scalar.activation(kpart["hi"][:, at:at + w], bank(f"k{layer}", n)[:, 0:w], ACT.Identity, bias=bias
                                                 ).then_inc(sem(f"k{layer}_hi"), 1)
                            nc.scalar.activation(kf[:, at:at + w], bank(f"k{layer}", n)[:, 0:w], ACT.Identity, bias=bias
                                                 ).then_inc(sem(f"k{layer}_out"), 1)

                    def cross(layer):
                        scale = float(np.float32(1) / np.sqrt(np.float32(DH))) if layer == 1 else 0.125
                        for u in range(2 * NC):
                            w = CHUNKS[u // 2][1]
                            slot = u % 2
                            act.wait_ge(*nth(f"score{layer}", u + 1))
                            if u >= 3:
                                act.wait_ge(*nth(f"prob{layer}_used", u - 2))
                            nc.scalar.activation(prob[u % 3][0:w, :].rearrange("p (a n) -> p a n", a=2),
                                                 heavy[0:w, 2 * slot:2 * slot + 2, 0:4 * T], ACT.Exp, scale=scale
                                                 ).then_inc(sem(f"prob{layer}"), 1)
                        act.wait_ge(*nth(f"prob{layer}_used", 2 * NC))
                        nc.scalar.activation(pv[:], pv_acc[:, 0:4 * T], ACT.Copy).then_inc(sem(f"pv{layer}"), 1)

                    for n in range(2):
                        act.wait_ge(*nth("val0", n + 1))
                        nc.scalar.activation(val0[0:T + 1, n * 512:(n + 1) * 512], bank("val0", n)[0:T + 1, :], ACT.Copy
                                             ).then_inc(sem("val0_out"), 1)
                    exps(4, "exp0", KEYS0, "shifted0")
                    for g in range(4):
                        act.wait_ge(*nth("probT0", g + 1))
                        nc.scalar.activation(probT[:, 4 * g:4 * g + 4, :], bank("probT0", g)[0:KEYS0, 0:4 * T].rearrange("p (a n) -> p a n", a=4),
                                             ACT.Copy).then_inc(sem("probT0_out"), 1)
                    for n in range(2):
                        act.wait_ge(*nth("oT0", n + 1))
                        nc.scalar.activation(oT0[:, 4 * n:4 * n + 4, :], bank("oT0", n)[:, 0:4 * T].rearrange("p (a n) -> p a n", a=4),
                                             ACT.Copy).then_inc(sem("oT0_out"), 1)
                    act.wait_ge(*nth("ffg_out", 1))
                    nc.scalar.activation(egate[0:FF0, 0:3, :], gate[0:FF0, 0:3, :], ACT.Exp, scale=-1.0).then_inc(sem("eg0"), 1)
                    keys(1)
                    cross(1)
                    exps(4, "exps", T, "scs_out")
                    for g in range(4):
                        act.wait_ge(*nth("probTs", g + 1))
                        nc.scalar.activation(probT[0:T, 4 * g:4 * g + 4, :], bank("probTs", g)[0:T, 0:4 * T].rearrange("p (a n) -> p a n", a=4),
                                             ACT.Copy).then_inc(sem("probTs_out"), 1)
                    keys(2)
                    cross(2)
                    act.wait_ge(*nth("gate_out", 1))
                    nc.scalar.activation(egate[:], gate[:], ACT.Exp, scale=-GELU).then_inc(sem("eg2"), 1)
                    act.wait_ge(*nth("max3", 1))
                    for n in range(3):
                        at, w = K_CUTS[n]
                        nc.scalar.activation(p3[:, at:at + w], bank("sc3", n)[0:T, 0:w], ACT.Exp, bias=stat[0:T, 52:53],
                                             accum_out=stat[0:T, 53 + n:54 + n]).then_inc(sem("sc3_out"), 1)

                @block.vector
                def _(dve):
                    v = nc.vector
                    steps = [0]

                    def link(ins):
                        steps[0] += 1
                        ins.then_inc(sem("dve_step"), 1)
                        dve.wait_ge(sem("dve_step"), steps[0])

                    def normed(name, src, wait, kind):
                        n = NORMS.index(name) + 1
                        dve.wait_ge(*nth(wait, 1))
                        if kind == "rms":
                            link(v.tensor_tensor_reduce(junk[:], src, src, 1.0 / D, 0.0, ALU.mult, ALU.add, stat[0:T, 11:12]))
                        else:
                            link(v.bn_stats(stat[0:T, 4:10], src))
                            link(v.bn_aggr(stat[0:T, 10:12], stat[0:T, 4:10]))
                        v.tensor_scalar(stat[0:T, 1:2], stat[0:T, 11:12], EPS_RMS if kind == "rms" else EPS_LN, None, ALU.add
                                        ).then_inc(sem("norm_var"), 1)
                        dve.wait_ge(*nth("norm_rstd", n))
                        if kind == "rms":
                            v.tensor_scalar(xs[:], src, stat[0:T, 2:3], None, ALU.mult).then_inc(sem("xs"), 1)
                        else:
                            v.tensor_scalar(xs[:], src, stat[0:T, 10:11], stat[0:T, 2:3], ALU.subtract, ALU.mult).then_inc(sem("xs"), 1)

                    def to_hT(name, scale=None, shift=None):
                        dve.wait_ge(*nth(name, 1))
                        src = bank(name)[:, 0:T]
                        if scale is None:
                            ins = v.tensor_copy(hT[:], src)
                        elif shift is None:
                            ins = v.tensor_scalar(hT[:], src, scale, None, ALU.mult)
                        else:
                            ins = v.tensor_scalar(hT[:], src, scale, shift, ALU.mult, ALU.add)
                        ins.then_inc(sem(name + "_out"), 1)

                    def wide(t, n):
                        return t.unsqueeze(2).to_broadcast([t.shape[0], t.shape[1], n])

                    def softmax(psum_name, width, mask, tag):
                        for g in range(4):
                            dve.wait_ge(*nth(psum_name, g + 1))
                            s = bank(psum_name, g)[0:T, 0:4 * width].rearrange("p (a n) -> p a n", a=4)
                            d = sm[:, 4 * g:4 * g + 4, 0:width]
                            m = stat[0:T, 16 + 4 * g:20 + 4 * g]
                            if mask is not None:
                                v.tensor_tensor(d, s, mask, ALU.add).then_inc(sem(psum_name + "_out"), 1)
                                dve.wait_ge(*nth(psum_name + "_out", g + 1))
                                link(v.tensor_reduce(m, d, AX.X, ALU.max))
                                v.tensor_tensor(d, d, wide(m, width), ALU.subtract).then_inc(sem("shifted" + tag), 1)
                            else:
                                link(v.tensor_reduce(m, s, AX.X, ALU.max))
                                v.tensor_tensor(d, s, wide(m, width), ALU.subtract).then_inc(sem(psum_name + "_out"), 1)

                    def sums(width, tag):
                        for g in range(4):
                            dve.wait_ge(*nth("exp" + tag, g + 1))
                            d = sm[:, 4 * g:4 * g + 4, 0:width]
                            last = v.tensor_reduce(stat[0:T, 32 + 4 * g:36 + 4 * g], d, AX.X, ALU.add)
                        link(last)
                        v.reciprocal(stat[0:T, 32:48], stat[0:T, 32:48]).then_inc(sem("rsum" + tag), 1)

                    def add_out(name, dst, res, bias, tag):
                        dve.wait_ge(*nth(name, 1))
                        v.tensor_tensor(junk[:], bank(name)[0:T, 0:D], bias, ALU.add).then_inc(sem(name + "_out"), 1)
                        dve.wait_ge(*nth(name + "_out", 1))
                        v.tensor_tensor(dst, junk[:], res, ALU.add).then_inc(sem(tag), 1)

                    def split_queries(layer):
                        L = str(layer)
                        dve.wait_ge(*nth("q" + L, 1))
                        if layer == 1:
                            v.tensor_scalar(qf[:], bank("q1")[:, 0:T], col("bq"), None, ALU.add).then_inc(sem("q1_out"), 1)
                        else:
                            v.tensor_copy(qf[:], bank("q2")[:, 0:T]).then_inc(sem("q2_out"), 1)
                        dve.wait_ge(*nth(f"q{L}_out", 1))
                        v.tensor_copy(qpart["hi"][:], qf[:]).then_inc(sem(f"q{L}_hi"), 1)
                        dve.wait_ge(*nth(f"q{L}_hi", 1))
                        link(v.tensor_tensor(qr[:], qf[:], qpart["hi"][:], ALU.subtract))
                        v.tensor_copy(qpart["mid"][:], qr[:]).then_inc(sem(f"q{L}_mid"), 1)
                        dve.wait_ge(*nth(f"q{L}_mid", 1))
                        v.tensor_tensor(qpart["lo"][:], qr[:], qpart["mid"][:], ALU.subtract).then_inc(sem(f"q{L}_lo"), 1)
                        v.tensor_tensor(q_rows[:], qpart["hi"][:].unsqueeze(1).to_broadcast([P, H, T]), wide(head_mask[:], T),
                                        ALU.mult).then_inc(sem(f"q{L}_rows"), 1)

                    def values(layer):
                        for n in range(3):
                            dve.wait_ge(*nth(f"v{layer}", n + 1))
                            if layer == 2 and n == 0:
                                dve.wait_ge(*nth("prob1_used", 2 * NC))
                            src = bank(f"v{layer}", n).rearrange("p (c h d) -> p c h d", c=4, d=DH)
                            full = 4 if n < 2 else 3
                            for c0, c1, w in ((0, full, P),) + (((3, 4, TAIL),) if n == 2 else ()):
                                for c in range(c0, c1):
                                    dst = v_aug[0:w, 4 * n + c, 0:H * VW].rearrange("p (h w) -> p h w", w=VW)[:, :, 0:DH]
                                    last = v.tensor_copy(dst, src[0:w, c])
                            last.then_inc(sem(f"v{layer}_out"), 1)

                    def maxima(layer):
                        L = str(layer)
                        for n in range(2 * 13):
                            t, s = n // 2, n % 2
                            w = min(P, H * T - t * P)
                            dve.wait_ge(*nth(f"max{L}_scored", n + 1))
                            v.tensor_reduce(mx[0:w, t, s:s + 1], heavy[0:w, 2 * (n % 2):2 * (n % 2) + 2, 0:S // 4], AX.XY, ALU.max
                                            ).then_inc(sem(f"max{L}_read"), 1)
                        dve.wait_ge(*nth(f"max{L}_read", 2 * 13))
                        v.tensor_reduce(mxm[:, 0:12], mx[:, 0:12, :], AX.X, ALU.max)
                        v.tensor_reduce(mxm[0:H * T - 12 * P, 12:13], mx[0:H * T - 12 * P, 12:13, :], AX.X, ALU.max).then_inc(sem(f"max{L}"), 1)
                        dve.wait_ge(*nth(f"max{L}T", 1))
                        v.tensor_scalar(mrow[:], bank(f"max{L}T")[0:13, 0:P], -1.0, None, ALU.mult).then_inc(sem(f"max{L}T_out"), 1)

                    def attended(layer):
                        L = str(layer)
                        dve.wait_ge(*nth(f"pv{L}T", 1))
                        view = bank(f"pv{L}T")[0:T, :].rearrange("p (h w) -> p h w", w=VWIN)
                        link(v.reciprocal(stat[0:T, 16:32], view[:, :, DH]))
                        v.tensor_tensor(on[:].rearrange("p (h d) -> p h d", d=DH), view[:, :, 0:DH], wide(stat[0:T, 16:32], DH), ALU.mult
                                        ).then_inc(sem(f"pv{L}T_out"), 1)
                        dve.wait_ge(*nth(f"o{L}T", 1))
                        if layer == 1:
                            v.tensor_scalar(oT[:], bank("o1T")[:, 0:T], col("bv"), None, ALU.add).then_inc(sem("o1T_out"), 1)
                        else:
                            v.tensor_copy(oT[:], bank("o2T")[:, 0:T]).then_inc(sem("o2T_out"), 1)

                    def gated(bank_lin, bank_gate, m, tiles, biases, tag):
                        dve.wait_ge(*nth(bank_lin, 1))
                        v.tensor_tensor(hid[0:m, 0:tiles, :], bank(bank_lin)[0:m, 0:tiles * T].rearrange("p (a n) -> p a n", a=tiles),
                                        wide(biases[:, 0:tiles], T), ALU.add).then_inc(sem(bank_lin + "_out"), 1)
                        dve.wait_ge(*nth(bank_gate, 1))
                        g = gate[0:m, 0:tiles, :]
                        e = egate[0:m, 0:tiles, :]
                        v.tensor_tensor(g, bank(bank_gate)[0:m, 0:tiles * T].rearrange("p (a n) -> p a n", a=tiles),
                                        wide(biases[:, tiles:2 * tiles], T), ALU.add).then_inc(sem(bank_gate + "_out"), 1)
                        dve.wait_ge(*nth(bank_gate + "_out", 1))
                        dve.wait_ge(*nth(bank_lin + "_out", 1))
                        v.tensor_tensor(hid[0:m, 0:tiles, :], hid[0:m, 0:tiles, :], g, ALU.mult)
                        dve.wait_ge(*nth("eg" + tag, 1))
                        link(v.tensor_scalar(e, e, 1.0, None, ALU.add))
                        link(v.reciprocal(e, e))
                        v.tensor_tensor(hid[0:m, 0:tiles, :], hid[0:m, 0:tiles, :], e, ALU.mult).then_inc(sem("hid" + tag), 1)

                    dve.wait_ge(*nth("ctxT_in", 16))
                    link(v.tensor_reduce(pool[:, 2:3], ctxT[:], AX.X, ALU.add))
                    v.tensor_scalar(pool[:, 0:1], pool[:, 2:3], 1.0 / S, None, ALU.mult).then_inc(sem("pool"), 1)
                    dve.wait_ge(*nth("pool_ms", 1))
                    v.tensor_scalar(stat[:, 12:13], bank("pool_ms")[:, 0:1], EPS_RMS, None, ALU.add).then_inc(sem("pool_ms_out"), 1)
                    dve.wait_ge(*nth("pool_rstd", 1))
                    v.tensor_scalar(pool[:, 3:4], pool[:, 0:1], stat[:, 13:14], col("mem_norm"), ALU.mult, ALU.mult).then_inc(sem("pool_normed"), 1)
                    dve.wait_ge(*nth("mem", 1))
                    v.tensor_copy(xnT[:, T:T + 1], bank("mem")[:, 0:1]).then_inc(sem("mem_out"), 1)
                    dve.wait_ge(*nth("x0_in", 16))
                    normed("xs0", x0[:], "mem_out", "rms")
                    dve.wait_ge(*nth("xn", 1))
                    v.tensor_scalar(xnT[:, 0:T], bank("xn")[:, 0:T], col("attn_norm"), None, ALU.mult).then_inc(sem("xn_out"), 1)
                    W = T + 1
                    for p in range(PAIRS):
                        dve.wait_ge(*nth("qk", p + 1))
                        if p >= 2:
                            dve.wait_ge(*nth("roped", 3 * (p - 1)))
                        v.tensor_tensor(rope_a[:, p % 2, :], bank("qk", p)[:, 0:2 * W], cos2[:], ALU.mult)
                        v.tensor_tensor(rope_b[:, p % 2, :], bank("qk", p)[:, 2 * W:4 * W], sin2[:], ALU.mult).then_inc(sem("qk_out"), 1)
                    softmax("score0", KEYS0, mask0[:].unsqueeze(1).to_broadcast([T, 4, KEYS0]), "0")
                    sums(KEYS0, "0")
                    dve.wait_ge(*nth("out0", 1))
                    v.tensor_tensor(x1[:], bank("out0")[0:T, 0:D], x0[:], ALU.add).then_inc(sem("out0_out"), 1)
                    normed("xs_ff", x1[:], "out0_out", "rms")
                    to_hT("fx0", col("ff_norm"))
                    gated("ffa", "ffg", FF0, FF0_TILES, b_ff1[:], "0")
                    add_out("ffo", x2[:], x1[:], row("ff_b2"), "x2")
                    to_hT("x1T")
                    split_queries(1)
                    values(1)
                    maxima(1)
                    attended(1)
                    add_out("out1", x1[:], x2[:], row("bo"), "x3")
                    normed("xs_l1", x1[:], "x3", "ln")
                    dve.wait_ge(*nth("xs", NORMS.index("xs_l1") + 1))
                    link(v.tensor_tensor(junk[:], xs[:], row("gamma"), ALU.mult))
                    v.tensor_tensor(x1[:], junk[:], row("beta"), ALU.add).then_inc(sem("x3b"), 1)
                    normed("xs_ln1", x1[:], "x3b", "ln")
                    to_hT("hT", col("ln1_s"), col("ln1_b"))
                    dve.wait_ge(*nth("qs", 1))
                    v.tensor_copy(qf[:], bank("qs")[:, 0:T]).then_inc(sem("qs_out"), 1)
                    dve.wait_ge(*nth("ks", 1))
                    v.tensor_tensor(kbds[:], bank("ks")[:, 0:T].unsqueeze(1).to_broadcast([P, H, T]), wide(head_mask[:], T), ALU.mult
                                    ).then_inc(sem("ks_out"), 1)
                    dve.wait_ge(*nth("vs", 1))
                    v.tensor_copy(vs[:], bank("vs")[0:T, 0:D]).then_inc(sem("vs_out"), 1)
                    softmax("scs", T, None, "s")
                    sums(T, "s")
                    dve.wait_ge(*nth("rsums", 1))
                    dve.wait_ge(*nth("os", 1))
                    v.tensor_tensor(on[:].rearrange("p (h d) -> p h d", d=DH), bank("os")[0:T, 0:D].rearrange("p (h d) -> p h d", d=DH),
                                    wide(stat[0:T, 32:48], DH), ALU.mult).then_inc(sem("os_out"), 1)
                    dve.wait_ge(*nth("osT", 1))
                    v.tensor_copy(oT[:], bank("osT")[:, 0:T]).then_inc(sem("osT_out"), 1)
                    add_out("outs", x2[:], x1[:], row("bo1"), "x4")
                    normed("xs_ln2", x2[:], "x4", "ln")
                    to_hT("h2T", col("ln2_s"), col("ln2_b"))
                    split_queries(2)
                    values(2)
                    maxima(2)
                    attended(2)
                    add_out("out2", x1[:], x2[:], row("bo2"), "x5")
                    normed("xs_ln3", x1[:], "x5", "ln")
                    to_hT("h3T", col("ln3_s"), col("ln3_b"))
                    gated("lin", "gate", P, FF2_TILES, bf1[:], "2")
                    add_out("ff2o", x2[:], x1[:], row("bff2"), "x6")
                    to_hT("x3T")
                    for n in range(3):
                        dve.wait_ge(*nth("sc3", n + 1))
                        last = v.tensor_reduce(stat[0:T, 48 + n:49 + n], bank("sc3", n)[0:T, 0:K_CUTS[n][1]], AX.X, ALU.max)
                    link(last)
                    v.tensor_reduce(stat[0:T, 52:53], stat[0:T, 48:51], AX.X, ALU.max, negate=True).then_inc(sem("max3"), 1)
                    for n in range(3):
                        dve.wait_ge(*nth("pT3", n + 1))
                        src = bank("pT3", n)[:, 0:4 * T].rearrange("p (a n) -> p a n", a=4)
                        if n < 2:
                            v.tensor_copy(pT3[:, 4 * n:4 * n + 4, :], src).then_inc(sem("pT3_out"), 1)
                        else:
                            v.tensor_copy(pT3[:, 8:11, :], src[:, 0:3])
                            v.tensor_copy(pT3[0:TAIL, 11, :], src[0:TAIL, 3]).then_inc(sem("pT3_out"), 1)
                    link(v.tensor_reduce(stat[0:T, 57:58], stat[0:T, 53:56], AX.X, ALU.add))
                    link(v.reciprocal(stat[0:T, 58:59], stat[0:T, 57:58]))
                    dve.wait_ge(*nth("out3", 1))
                    v.scalar_tensor_tensor(y[:], bank("out3")[0:T, 0:D], stat[0:T, 58:59], x2[:], ALU.mult, ALU.add).then_inc(sem("y"), 1)

                @block.gpsimd
                def _(pool_eng):
                    g = nc.gpsimd

                    def rstd(ready, done, dst, src, n, count=1):
                        pool_eng.wait_ge(*nth(ready, count))
                        g.tensor_tensor(dst, src, minus_half[0:n, :], ALU.pow).then_inc(sem(done), 1)

                    def split_keys(layer):
                        pool_eng.wait_ge(*nth(f"k{layer}_out", 3))
                        pool_eng.wait_ge(*nth(f"k{layer}_hi", 3))
                        g.tensor_tensor(kr[:], kf[:], kpart["hi"][:], ALU.subtract).then_inc(sem(f"k{layer}_r"), 1)
                        pool_eng.wait_ge(*nth(f"k{layer}_r", 1))
                        if layer == 2:
                            pool_eng.wait_ge(*nth("k1_stacked", 16 * len(TERMS) * PAIRS))
                        g.tensor_copy(kpart["mid"][:], kr[:]).then_inc(sem(f"k{layer}_mid"), 1)
                        pool_eng.wait_ge(*nth(f"k{layer}_mid", 1))
                        g.tensor_tensor(kpart["lo"][:], kr[:], kpart["mid"][:], ALU.subtract).then_inc(sem(f"k{layer}_lo"), 1)

                    def stats_rstd(name):
                        rstd("norm_var", "norm_rstd", stat[0:T, 2:3], stat[0:T, 1:2], T, NORMS.index(name) + 1)

                    pool_eng.wait_ge(*nth("pool", 1))
                    g.tensor_tensor(pool[:, 1:2], pool[:, 0:1], pool[:, 0:1], ALU.mult).then_inc(sem("pool_sq"), 1)
                    rstd("pool_ms_out", "pool_rstd", stat[:, 13:14], stat[:, 12:13], P)
                    stats_rstd("xs0")
                    W = T + 1
                    for p in range(PAIRS):
                        pool_eng.wait_ge(*nth("qk_out", p + 1))
                        ra, rb = rope_a[:, p % 2, :], rope_b[:, p % 2, :]
                        g.tensor_tensor(qT0[:, p, :], ra[:, 0:T], rb[:, 0:T], ALU.add).then_inc(sem("roped"), 1)
                        for j in range(2):
                            pool_eng.wait_ge(*nth("roped", 3 * p + j + 1))
                            q = slice(64 * j, 64 * j + 64)
                            last = g.tensor_tensor(kbd0[q, p, j, 0:W], ra[q, W:2 * W], rb[q, W:2 * W], ALU.add
                                                   ).then_inc(sem("roped"), 1)
                        pool_eng.wait_ge(*nth("roped", 3 * p + 3))
                    pool_eng.wait_ge(*nth("rsum0", 1))
                    for n in range(4):
                        d = sm[:, 4 * n:4 * n + 4, :]
                        g.tensor_tensor(d, d, stat[0:T, 32 + 4 * n:36 + 4 * n].unsqueeze(2).to_broadcast([T, 4, KEYS0]), ALU.mult
                                        ).then_inc(sem("prob0"), 1)
                    stats_rstd("xs_ff")
                    split_keys(1)
                    stats_rstd("xs_l1")
                    stats_rstd("xs_ln1")
                    stats_rstd("xs_ln2")
                    split_keys(2)
                    stats_rstd("xs_ln3")

            used = [s.num for s in sems.values()]
            nc.all_engine_barrier(sems_to_clear=range(min(used), max(used) + 1))


K_CUTS = [(0, 482), (482, 481), (963, 481)]


def _constants():
    W = T + 1
    inv = (1.0 / 10000.0 ** (np.arange(0, DH0, 2, dtype=np.float32) / np.float32(DH0))).astype(np.float32)
    ang = np.repeat(np.arange(T, dtype=np.float32)[:, None] * inv[None, :], 2, axis=-1).astype(np.float32)
    cos = np.ones((DH0, W), np.float32)
    sin = np.zeros((DH0, W), np.float32)
    cos[:, :T] = np.cos(ang.astype(np.float64)).T
    sin[:, :T] = np.sin(ang.astype(np.float64)).T
    sin[0::2] = -sin[0::2]
    q, k = np.arange(T)[:, None], np.arange(T)[None, :]
    mask = np.zeros((T, KEYS0), np.float32)
    mask[:, :T] = np.where((q >= k) & (q // SEG == k // SEG), 0.0, -1e30)
    mask[:, T] = DH0 ** 0.5 * np.log(float(NM))
    heads = (np.arange(D)[:, None] // DH == np.arange(H)[None, :]).astype(np.float32)
    return {
        "c_ident": np.eye(P, dtype=np.float32), "c_mean": np.full((P, P), 1.0 / D, np.float32),
        "c_cos": np.tile(cos, (2, 2)), "c_sin": np.tile(sin, (2, 2)), "c_mask": mask, "c_head_mask": heads,
    }


def _padded(x, n, axis=-1):
    shape = list(x.shape)
    shape[axis] = n
    out = np.zeros(shape, x.dtype)
    out[tuple(slice(0, k) for k in x.shape)] = x
    return out


def kernel(**inputs):
    import concourse.bacc as _bacc
    from concourse import mybir as _mybir
    from concourse.bass_utils import run_bass_kernel_spmd as _run

    i = {k: np.asarray(v) for k, v in inputs.items()}
    ctx = i["ctx_1024"]
    main = ctx[:, :NFULL * P].reshape(B, P, NFULL, D)
    tail = ctx[:, NFULL * P:]
    qkv = i["L0_xattn_to_qkv_w"]
    swapped = qkv[:, :2 * E0].reshape(D, E0, 2)[:, :, ::-1].reshape(D, 2 * E0)
    pm = i["L0_xattn_persist_mem"]
    ff1, ffb = i["L0_xattn_ff_w1"], i["L0_xattn_ff_b1"]
    n0 = FF0_TILES * FF0
    data = {
        "x": i["x"], "ctx_main": main, "ctx_tail": tail,
        "ctxT": np.concatenate([main.transpose(0, 3, 2, 1).reshape(B, D, NFULL * P), tail.transpose(0, 2, 1)], axis=2),
        "cols": np.stack([i["L0_xattn_attn_norm_w"], i["L0_xattn_mem_pool_norm_w"], i["L0_xattn_ff_norm_w"], i["L1_xattn_bq"],
                          i["L1_xattn_bk"], i["L1_xattn_bv"]] + [i[f"L2_xattn_ln{n}_{c}"] for n in (1, 2, 3) for c in "sb"], axis=1),
        "rows": np.tile(np.concatenate([i["L0_xattn_ff_b2"], i["L1_xattn_bo"], i["L1_xattn_gamma"], i["L1_xattn_beta"],
                                        i["L2_xattn_bo1"], i["L2_xattn_bo2"], i["L2_xattn_bff2"]])[None], (T, 1)),
        "w_qkv": qkv, "w_rot": swapped,
        "w_out0": i["L0_xattn_to_out_w"].reshape(PAIRS, P, D).transpose(1, 0, 2),
        "w_mem": i["L0_xattn_to_mem_tokens_w"],
        "w_ff1": np.concatenate([_padded(ff1[:, :DFF0], n0), _padded(ff1[:, DFF0:], n0)], axis=1),
        "b_ff1": np.concatenate([_padded(ffb[:DFF0], n0), _padded(ffb[DFF0:], n0)]).reshape(2 * FF0_TILES, FF0).T,
        "w_ff2": _padded(i["L0_xattn_ff_w2"], n0, 0).reshape(FF0_TILES, FF0, D).transpose(1, 0, 2),
        "w1": np.stack([i[f"L1_xattn_W{c}"].T for c in "qkvo"], axis=1),
        "wq1": i["L2_xattn_Wq1"], "wkv1": i["L2_xattn_Wkv1"], "wo1": i["L2_xattn_Wo1"],
        "wq2": i["L2_xattn_Wq2"], "wkv2": i["L2_xattn_Wkv2"], "wo2": i["L2_xattn_Wo2"],
        "wf1": i["L2_xattn_Wff1"], "bf1": i["L2_xattn_bff1"].reshape(2 * FF2_TILES, P).T,
        "wf2": i["L2_xattn_Wff2"].reshape(FF2_TILES, P, D).transpose(1, 0, 2),
        "pm_k": pm.reshape(PAIRS, 2, NPM, DH0).transpose(1, 3, 0, 2).reshape(P, PAIRS, NPM),
        "pm_v": pm.transpose(1, 0, 2).reshape(NPM, E0),
        **_constants(),
    }
    nc = _bacc.Bacc("TRN2", target_bir_lowering=False, num_devices=1)
    arrays, aps = {}, {}
    for name, arr in data.items():
        arr = np.ascontiguousarray(arr)
        arrays[f"in_{name}"] = arr
        aps[name] = nc.dram_tensor(f"in_{name}", arr.shape, _mybir.dt.from_np(arr.dtype), kind="ExternalInput").ap()
    aps["out"] = nc.dram_tensor("out_0", (B, T, D), F32, kind="ExternalOutput").ap()
    xattn_program(nc, aps)
    return _run(nc, [arrays], core_ids=[0]).results[0]["out_0"]
```

```python
from contextlib import ExitStack

import numpy as np

import concourse.bass as bass
from concourse import mybir

F32 = mybir.dt.float32
BF16 = mybir.dt.bfloat16
ALU = mybir.AluOpType
ACT = mybir.ActivationFunctionType
AX = mybir.AxisListType

B, T, S, D = 32, 100, 1444, 128
H = 16
P = 128
NFULL = S // P
TAIL = S - NFULL * P
CHUNKS = [(c * P, P) for c in range(NFULL)] + [(NFULL * P, TAIL)]
NC = len(CHUNKS)
DH0, NPM, NM, SEG = 64, 16, 16, 64
PAIRS = H // 2
KEYS0 = T + 1 + NPM
E0 = H * DH0
DFF0 = int(D * 4 * 2 / 3)
FF0_TILES = 3
FF0 = -(-DFF0 // FF0_TILES)
FF2_TILES = 4
DH = D // H
TERMS = [("hi", "hi"), ("mid", "hi"), ("hi", "mid"), ("mid", "mid"), ("lo", "hi"), ("hi", "lo")]
KROWS = len(TERMS) * 2 * DH
VW = DH + 1
EPS_RMS, EPS_LN = 1.1920929e-07, 1e-05
GELU = 1.702

COLS = ["attn_norm", "mem_norm", "ff_norm", "bq", "bk", "bv", "ln1_s", "ln1_b", "ln2_s", "ln2_b", "ln3_s", "ln3_b"]
ROWS = ["ff_b2", "bo", "gamma", "beta", "bo1", "bo2", "bff2"]

LIGHT = {
    "front": [
        ("xn", 1, "dve"), ("pool_ms", 1, "dve"), ("mem", 1, "dve"), ("qk", PAIRS, "dve"), ("val0", 2, "act"),
        ("score0", 4, "dve"), ("probT0", 4, "act"), ("oT0", 2, "act"), ("out0", 1, "dve"), ("fx0", 1, "dve"),
        ("ffa", 1, "dve"), ("ffg", 1, "dve"), ("ffo", 1, "dve"), ("x1T", 1, "act"), ("q1", 1, "dve"),
        ("k1", 3, "act"), ("v1", 3, "act")],
    "mid": [
        ("max1T", 1, "dve"), ("pv1T", 1, "dve"), ("o1T", 1, "dve"), ("out1", 1, "dve"), ("k2", 3, "act"),
        ("hT", 1, "dve"), ("qs", 1, "act"), ("ks", 1, "dve"), ("vs", 1, "act"), ("scs", 4, "dve"), ("probTs", 4, "act"),
        ("os", 1, "dve"), ("osT", 1, "act"), ("outs", 1, "dve"), ("v2", 3, "act"), ("h2T", 1, "dve"), ("q2", 1, "dve")],
    "back": [
        ("max2T", 1, "dve"), ("pv2T", 1, "dve"), ("o2T", 1, "act"), ("out2", 1, "dve"), ("h3T", 1, "dve"),
        ("lin", 1, "dve"), ("gate", 1, "dve"), ("ff2o", 1, "dve"), ("x3T", 1, "act"), ("sc3", 3, "act"), ("pT3", 3, "act"),
        ("out3", 1, "dve")],
}
STREAMS = list(LIGHT)
USES = {stream: [(name, i) for name, n, _ in table for i in range(n)] for stream, table in LIGHT.items()}
STREAM_OF = {name: stream for stream, table in LIGHT.items() for name, _, _ in table}
READER = {name: reader for table in LIGHT.values() for name, _, reader in table}
NORMS = {"front": ["xs0", "xs_ff"], "mid": ["xs_l1", "xs_ln1", "xs_ln2"], "back": ["xs_ln3"]}

K_CUTS = [(0, 482), (482, 481), (963, 481)]
TILES = -(-H * T // P)
MSTEPS = TILES * len(K_CUTS)
GROUP = 4
USTEPS = H // GROUP * NC
STACKED = 16 * len(TERMS) * 2
PROBS = 4
LAG = 2
PRE = len(STREAMS) - 1


def merged(*streams):
    live = [[next(s), n, s] for n, s in enumerate(streams)]
    while live:
        first = min(live, key=lambda e: e[:2])
        tick = next(first[2], None)
        if tick is None:
            live.remove(first)
        else:
            assert tick >= first[0], (tick, first[0])
            first[0] = tick




def xattn_program(nc, a):
    with ExitStack() as ctx:
        def sb(name, shape, dt=F32):
            return ctx.enter_context(nc.sbuf_tensor(name, shape, dt))

        sems = {}

        def sem(name):
            base = name.removesuffix("_out")
            if name in READER:
                name = STREAM_OF[name] + "_filled"
            elif base in READER:
                name = STREAM_OF[base] + "_read_" + READER[base]
            if name not in sems:
                sems[name] = ctx.enter_context(nc.semaphore(name))
            return sems[name]

        def nth(name, n):
            base = name.removesuffix("_out")
            if base not in READER:
                return sem(name), n
            uses = USES[STREAM_OF[base]]
            at = uses.index((base, n - 1))
            if name in READER:
                return sem(name), at + 1
            return sem(name), sum(READER[use] == READER[base] for use, _ in uses[:at + 1])

        loaded = ctx.enter_context(nc.semaphore("weights_loaded"))
        preset = ctx.enter_context(nc.semaphore("preset"))

        ident = sb("ident", [P, P])
        ones_mean = sb("ones_mean", [P, P])
        cos2 = sb("cos2", [P, 2 * (T + 1)])
        sin2 = sb("sin2", [P, 2 * (T + 1)])
        mask0 = sb("mask0", [T, KEYS0])
        head_mask = sb("head_mask", [P, H])
        cols = sb("cols", [P, len(COLS)])
        rows = sb("rows", [T, len(ROWS) * D])
        w_qkv = sb("w_qkv", [P, 3 * E0])
        w_rot = sb("w_rot", [P, 2 * E0])
        w_out0 = sb("w_out0", [P, PAIRS, D])
        w_mem = sb("w_mem", [P, D])
        w_ff1 = sb("w_ff1", [P, 2 * FF0_TILES * FF0])
        b_ff1 = sb("b_ff1", [FF0, 2 * FF0_TILES])
        w_ff2 = sb("w_ff2", [FF0, FF0_TILES, D])
        w1 = sb("w1", [P, 4, D])
        wq1 = sb("wq1", [P, D])
        wkv1 = sb("wkv1", [P, 2 * D])
        wo1 = sb("wo1", [P, D])
        wq2 = sb("wq2", [P, D])
        wkv2 = sb("wkv2", [P, 2 * D])
        wo2 = sb("wo2", [P, D])
        wf1 = sb("wf1", [P, 2 * FF2_TILES * D])
        bf1 = sb("bf1", [P, 2 * FF2_TILES])
        wf2 = sb("wf2", [P, FF2_TILES, D])

        def col(name):
            return cols[:, COLS.index(name):COLS.index(name) + 1]

        def row(name):
            return rows[:, ROWS.index(name) * D:(ROWS.index(name) + 1) * D]

        x0 = sb("x0", [T, D])
        ctxT = {st: sb("ctxT_" + st, [P, S]) for st in STREAMS}
        ctxN = sb("ctxN", [P, NC, D])
        pool = sb("pool", [P, 8])
        xnT = sb("xnT", [P, T + 1])
        rope_a = sb("rope_a", [P, 2, 2 * (T + 1)])
        rope_b = sb("rope_b", [P, 2, 2 * (T + 1)])
        wide0 = sb("wide0", [P, H, T])
        qT0, oT0, kbds = wide0[:, 0:PAIRS, :], wide0[:, PAIRS:H, :], wide0
        kbd0 = sb("kbd0", [P, PAIRS, 2, KEYS0])
        val0 = sb("val0", [KEYS0, E0])
        sm = sb("sm", [T, H, KEYS0])
        p3 = sm[:].rearrange("p h k -> p (h k)")[:, 0:S]
        probT = sb("probT", [P, H, T])
        pT3 = probT[:, 0:NC, :]
        gate = sb("gate", [P, 4, T])
        egate = sb("egate", [P, 4, T])
        hid = sb("hid", [P, 4, T])
        vs = sb("vs", [T, D])
        stat = {st: sb("stat_" + st, [P, 64]) for st in STREAMS}
        junk = {st: sb("junk_" + st, [T, D]) for st in STREAMS}
        xs = {st: sb("xs_" + st, [T, D]) for st in STREAMS}
        hT = {st: sb("hT_" + st, [P, T]) for st in STREAMS}
        on = {st: sb("on_" + st, [T, D]) for st in STREAMS}
        oT = {st: sb("oT_" + st, [P, T]) for st in STREAMS}
        x1 = sb("x1", [T, D])
        x2 = sb("x2", [T, D])
        x3 = sb("x3", [T, D])
        x4 = sb("x4", [T, D])
        x5 = sb("x5", [T, D])
        x6 = sb("x6", [T, D])
        qf = sb("qf", [P, T])
        qr = sb("qr", [P, T])
        qss = sb("qss", [P, T])
        kf = sb("kf", [P, 2, K_CUTS[0][1]])
        kr = sb("kr", [P, 2, K_CUTS[0][1]])
        qpart = {n: sb("q" + n, [P, T], BF16) for n in ("hi", "mid", "lo")}
        kpart = {(L, n): sb(f"k{n}{L}", [P, S], BF16) for L in (1, 2) for n in ("hi", "mid", "lo")}
        q_rows = {L: sb(f"q_rows{L}", [P, H, T], BF16) for L in (1, 2)}
        q_stack = {L: sb(f"q_stack{L}", [P, H, T], BF16) for L in (1, 2)}
        k_stack = sb("k_stack", [P, PAIRS, S], BF16)
        v_aug = {L: sb(f"v_aug{L}", [P, NC, H * VW]) for L in (1, 2)}
        prob = [sb(f"prob{i}", [P, GROUP * T]) for i in range(PROBS)]
        mx = {L: sb(f"mx{L}", [P, TILES, 3]) for L in (1, 2)}
        mxm = {L: sb(f"mxm{L}", [P, TILES]) for L in (1, 2)}
        mrow = {L: sb(f"mrow{L}", [TILES, P], BF16) for L in (1, 2)}
        pv = {L: sb(f"pv{L}", [P, 4 * T]) for L in (1, 2)}
        y = sb("y", [T, D])
        q_dram = {L: nc.dram_tensor(f"q_parts{L}", (3, D, T), BF16).ap() for L in (1, 2)}
        minus_half = sb("minus_half", [P, 1])

        unit = ctx.enter_context(nc.psum_tensor("unit", [P, 2, 512], F32))
        rowmax = ctx.enter_context(nc.psum_tensor("rowmax", [P, 2, 512], F32))
        pv_acc = ctx.enter_context(nc.psum_tensor("pv_acc", [P, 512], F32))
        light = {st: ctx.enter_context(nc.psum_tensor("light_" + st, [P, 512], F32)) for st in STREAMS}

        def bank(name, i=0):
            return light[STREAM_OF[name]]

        def bank_free(eng, name, i=0):
            uses = USES[STREAM_OF[name]]
            n = uses.index((name, i)) - 1
            if n >= 0:
                before, k = uses[n]
                eng.wait_ge(*nth(before + "_out", k + 1))

        loads = [
            (ident[:], a["c_ident"]), (ones_mean[:], a["c_mean"]), (cos2[:], a["c_cos"]), (sin2[:], a["c_sin"]),
            (mask0[:], a["c_mask"]), (head_mask[:], a["c_head_mask"]), (cols[:], a["cols"]), (rows[:], a["rows"]),
            (w_qkv[:], a["w_qkv"]), (w_rot[:], a["w_rot"]), (w_out0[:], a["w_out0"]), (w_mem[:], a["w_mem"]),
            (w_ff1[:], a["w_ff1"]), (b_ff1[:], a["b_ff1"]), (w_ff2[:], a["w_ff2"]), (w1[:], a["w1"]),
            (wq1[:], a["wq1"]), (wkv1[:], a["wkv1"]), (wo1[:], a["wo1"]),
            (wq2[:], a["wq2"]), (wkv2[:], a["wkv2"]), (wo2[:], a["wo2"]),
            (wf1[:], a["wf1"]), (bf1[:], a["bf1"]), (wf2[:], a["wf2"]),
            (val0[T + 1:KEYS0, :], a["pm_v"]),
        ]
        with nc.Block() as block:
            @block.sync
            def _(sp):
                for dst, src in loads:
                    sp.dma_start(dst, src).then_inc(loaded, 16)
                sp.wait_ge(preset, 1)
                for j in range(2):
                    sp.dma_start(kbd0[64 * j:64 * j + 64, :, j, T + 1:KEYS0],
                                 a["pm_k"][64 * j:64 * j + 64]).then_inc(loaded, 16)
                sp.wait_ge(loaded, 16 * (len(loads) + 2))

            @block.vector
            def _(dve):
                nc.vector.memset(k_stack[KROWS:P], 1.0)
                for L in (1, 2):
                    nc.vector.memset(mxm[L][:], 0.0)
                    nc.vector.memset(pv[L][:], 0.0)

            @block.gpsimd
            def _(pool_eng):
                nc.gpsimd.memset(kbd0[:], 0.0).then_inc(preset, 1)
                nc.gpsimd.memset(minus_half[:], -0.5)
                for L in (1, 2):
                    nc.gpsimd.memset(q_stack[L][:], 0.0)
                    nc.gpsimd.memset(v_aug[L][:], 1.0)

        def iteration(batches):

            def other(eng, stream, name, n):
                if stream in batches:
                    eng.wait_ge(*nth(name, n))

            def normed_at(name):
                stream = next(s for s in NORMS if name in NORMS[s])
                return nth("xs_" + stream, NORMS[stream].index(name) + 1)

            def run(**streams):
                merged(*[streams[s]() for s in STREAMS if s in batches])

            with nc.Block() as block:
                @block.sync
                def _(sp):
                    def park_queries(L):
                        for n, part in enumerate(("hi", "mid", "lo")):
                            sp.wait_ge(*nth(f"q{L}_{part}", 1))
                            sp.dma_start(q_dram[L][n], qpart[part][:]).then_inc(sem(f"q{L}_parked"), 16)

                    def stack_queries(L):
                        sp.wait_ge(*nth(f"q{L}_parked", 48))
                        for t, (_, qp) in enumerate(TERMS):
                            src = q_dram[L][("hi", "mid", "lo").index(qp)].rearrange("(p j d) t -> j d p t", j=2, d=DH)
                            for j in range(2):
                                r = 16 * t + DH * j
                                sp.dma_start(q_stack[L][r:r + DH, j::2, :], src[j]).then_inc(sem(f"q{L}_stacked"), 16)

                    def stack_keys(L, g):
                        for t, (kp, _) in enumerate(TERMS):
                            for p in (2 * g, 2 * g + 1):
                                sp.dma_start(k_stack[16 * t:16 * t + 16, p, :],
                                             kpart[L, kp][16 * p:16 * p + 16, :]).then_inc(sem(f"k{L}_stacked{g}"), 16)

                    def stack_maxima(L):
                        flat = q_stack[L][KROWS:KROWS + 1].rearrange("p h t -> p (h t)")
                        full = H * T // P
                        sp.wait_ge(*nth(f"max{L}T_out", 1))
                        sp.dma_start(flat[:, 0:full * P], mrow[L][0:full, :]).then_inc(sem(f"max{L}_stacked"), 16)
                        sp.dma_start(flat[:, full * P:H * T], mrow[L][full:TILES, 0:H * T - full * P]).then_inc(sem(f"max{L}_stacked"), 16)

                    def front():
                        b = batches["front"]
                        yield 0
                        sp.dma_start(x0[:], a["x"][b]).then_inc(sem("x0_in"), 16)
                        sp.dma_start(ctxT["front"][:], a["ctxT"][b]).then_inc(sem("ctxT_front_in"), 16)
                        yield 77
                        park_queries(1)
                        yield 79
                        other(sp, "mid", "score1", USTEPS)
                        stack_queries(1)
                        yield 118
                        sp.wait_ge(*nth("q1_stacked", STACKED))

                    def mid():
                        b = batches["mid"]
                        for g in range(4):
                            yield 0.1
                            stack_keys(1, g)
                        yield 20
                        sp.dma_start(ctxT["mid"][:], a["ctxT"][b]).then_inc(sem("ctxT_mid_in"), 16)
                        yield 24
                        stack_maxima(1)
                        yield 101
                        park_queries(2)
                        yield 102
                        other(sp, "back", "score2", USTEPS)
                        stack_queries(2)
                        yield 118
                        sp.wait_ge(*nth("q2_stacked", STACKED))

                    def back():
                        b = batches["back"]
                        yield 20.5
                        sp.dma_start(ctxT["back"][:], a["ctxT"][b]).then_inc(sem("ctxT_back_in"), 16)
                        sp.dma_start(ctxN[:, 0:NFULL, :], a["ctx_main"][b]).then_inc(sem("ctxN_in"), 16)
                        sp.dma_start(ctxN[0:TAIL, NFULL, :], a["ctx_tail"][b]).then_inc(sem("ctxN_in"), 16)
                        for g in range(4):
                            yield 34 + 6.6 * g
                            other(sp, "mid", "score1", NC * (g + 1))
                            stack_keys(2, g)
                            if g == 2:
                                yield 47.5
                                stack_maxima(2)
                        yield 116
                        sp.wait_ge(*nth("y", 1))
                        sp.dma_start(a["out"][b], y[:]).then_inc(sem("stored"), 16)
                        yield 117
                        sp.wait_ge(*nth("stored", 16))

                    run(front=front, mid=mid, back=back)

                @block.tensor
                def _(pe):
                    mm = nc.tensor.matmul

                    def transpose(name, src, width, rows_, *ready):
                        pe.wait_ge(*ready)
                        bank_free(pe, name)
                        nc.tensor.transpose(bank(name)[0:width, 0:rows_], src, ident[0:rows_, 0:rows_]).then_inc(sem(name), 1)

                    def project(name, lhsT, rhs, m, n, *ready):
                        pe.wait_ge(*ready)
                        bank_free(pe, name)
                        mm(bank(name)[0:m, 0:n], lhsT, rhs, start=True, stop=True).then_inc(sem(name), 1)

                    def key_piece(L, n, wk, stream):
                        pe.wait_ge(*nth(f"ctxT_{stream}_in", 16))
                        bank_free(pe, f"k{L}", n)
                        at, w = K_CUTS[n]
                        mm(bank(f"k{L}", n)[:, 0:w], wk, ctxT[stream][:, at:at + w], start=True, stop=True).then_inc(sem(f"k{L}"), 1)

                    def value_piece(L, n, wv, stream):
                        bank_free(pe, f"v{L}", n)
                        for i in range(4):
                            at, w = CHUNKS[4 * n + i]
                            last = mm(bank(f"v{L}", n)[0:w, i * D:(i + 1) * D], ctxT[stream][:, at:at + w], wv, start=True, stop=True)
                        last.then_inc(sem(f"v{L}"), 1)

                    def row_scores(L, n):
                        t, s = n // 3, n % 3
                        w = min(P, H * T - t * P)
                        if n >= 2:
                            pe.wait_ge(*nth(f"max{L}_read", n - 1))
                        elif L == 2:
                            other(pe, "mid", "max1_read", MSTEPS)
                        at, cw = K_CUTS[s]
                        flat = q_rows[L][:].rearrange("p h t -> p (h t)")
                        mm(rowmax[0:w, n % 2, 0:cw], flat[:, t * P:t * P + w], kpart[L, "hi"][:, at:at + cw], start=True, stop=True
                           ).then_inc(sem(f"max{L}_scored"), 1)

                    def scores(L, u):
                        g, c = u // NC, u % NC
                        at, w = CHUNKS[c]
                        qs = q_stack[L][:].rearrange("p h t -> p (h t)")
                        if c == 0:
                            pe.wait_ge(*nth(f"k{L}_stacked{g}", STACKED))
                        if u == 0:
                            pe.wait_ge(*nth(f"max{L}_stacked", 32))
                        if u >= 2:
                            pe.wait_ge(*nth(f"prob{L}", u - 1))
                        elif L == 2:
                            other(pe, "mid", "prob1", USTEPS)
                        for i in range(2):
                            p = 2 * g + i
                            last = mm(unit[0:w, u % 2, i * 2 * T:(i + 1) * 2 * T], k_stack[:, p, at:at + w],
                                      qs[:, 2 * p * T:2 * (p + 1) * T], start=True, stop=True)
                        last.then_inc(sem(f"score{L}"), 1)

                    def values(L, u):
                        g, c = u // NC, u % NC
                        w = CHUNKS[c][1]
                        pe.wait_ge(*nth(f"prob{L}", u + 1))
                        if u == 0 and L == 2:
                            other(pe, "mid", "pv1", 4)
                        for j in range(GROUP):
                            h = GROUP * g + j
                            last = mm(pv_acc[32 * j:32 * j + VW, g * T:(g + 1) * T], v_aug[L][0:w, c, VW * h:VW * (h + 1)],
                                      prob[u % PROBS][0:w, j * T:(j + 1) * T], start=(c == 0), stop=(c == NC - 1),
                                      skip_group_check=True)
                        last.then_inc(sem(f"prob{L}_used"), 1)

                    def cross(L, tick):
                        for u in range(USTEPS + LAG):
                            yield tick + 0.55 * u
                            if u < USTEPS:
                                scores(L, u)
                            if u >= LAG:
                                values(L, u - LAG)

                    def pv_rows(L):
                        pe.wait_ge(*nth(f"pv{L}", 4))
                        bank_free(pe, f"pv{L}T")
                        for g in range(4):
                            last = nc.tensor.transpose(bank(f"pv{L}T")[0:T, g * P:(g + 1) * P], pv[L][:, g * T:(g + 1) * T], ident[:])
                        last.then_inc(sem(f"pv{L}T"), 1)

                    def front():
                        W = T + 1
                        yield 5
                        transpose("xn", xs["front"][:], D, T, *normed_at("xs0"))
                        yield 6
                        project("pool_ms", ones_mean[:], pool[:, 1:2], P, 1, *nth("pool_sq", 1))
                        yield 10
                        project("mem", w_mem[:], pool[:, 3:4], P, 1, *nth("pool_normed", 1))
                        for p in range(PAIRS):
                            yield 12 + 2 * p
                            if p == 0:
                                pe.wait_ge(*nth("xn_out", 1))
                                pe.wait_ge(*nth("mem_out", 1))
                            bank_free(pe, "qk", p)
                            for n, (w, at) in enumerate(((w_qkv, 0), (w_qkv, E0), (w_rot, 0), (w_rot, E0))):
                                last = mm(bank("qk", p)[:, n * W:(n + 1) * W], w[:, at + p * P:at + (p + 1) * P], xnT[:],
                                          start=True, stop=True)
                            last.then_inc(sem("qk"), 1)
                        for n in range(2):
                            yield 28 + 2 * n
                            bank_free(pe, "val0", n)
                            mm(bank("val0", n)[0:W, :], xnT[:], w_qkv[:, 2 * E0 + n * 512:2 * E0 + (n + 1) * 512],
                               start=True, stop=True).then_inc(sem("val0"), 1)
                        for g in range(4):
                            yield 32 + 2 * g
                            pe.wait_ge(*nth("roped", 3 * (2 * g + 2)))
                            bank_free(pe, "score0", g)
                            for i in range(2):
                                p = 2 * g + i
                                last = mm(bank("score0", g)[0:T, i * 2 * KEYS0:(i + 1) * 2 * KEYS0], qT0[:, p, :],
                                          kbd0[:, p].rearrange("p j k -> p (j k)"), start=True, stop=True)
                            last.then_inc(sem("score0"), 1)
                        for g in range(4):
                            yield 45 + 2 * g
                            pe.wait_ge(*nth("prob0", g + 1))
                            bank_free(pe, "probT0", g)
                            for i in range(4):
                                last = nc.tensor.transpose(bank("probT0", g)[0:KEYS0, i * T:(i + 1) * T], sm[:, 4 * g + i, :],
                                                           ident[0:T, 0:T])
                            last.then_inc(sem("probT0"), 1)
                        pe.wait_ge(*nth("val0_out", 2))
                        for n in range(2):
                            yield 53 + 2 * n
                            pe.wait_ge(*nth("probT0_out", 2 * n + 2))
                            bank_free(pe, "oT0", n)
                            for i in range(8):
                                h = 8 * n + i
                                j, k = h % 2, i // 2
                                last = mm(bank("oT0", n)[64 * j:64 * j + 64, k * T:(k + 1) * T], val0[:, h * DH0:(h + 1) * DH0],
                                          probT[0:KEYS0, h, :], start=True, stop=True)
                            last.then_inc(sem("oT0"), 1)
                        yield 57
                        pe.wait_ge(*nth("oT0_out", 2))
                        bank_free(pe, "out0")
                        for p in range(PAIRS):
                            last = mm(bank("out0")[0:T, 0:D], oT0[:, p, :], w_out0[:, p, :], start=(p == 0), stop=(p == PAIRS - 1))
                        last.then_inc(sem("out0"), 1)
                        yield 62
                        transpose("fx0", xs["front"][:], D, T, *normed_at("xs_ff"))
                        for n, name in enumerate(("ffa", "ffg")):
                            yield 64 + 2 * n
                            pe.wait_ge(*nth("fx0_out", 1))
                            bank_free(pe, name)
                            for t in range(FF0_TILES):
                                at = (n * FF0_TILES + t) * FF0
                                last = mm(bank(name)[0:FF0, t * T:(t + 1) * T], w_ff1[:, at:at + FF0], hT["front"][:], start=True, stop=True)
                            last.then_inc(sem(name), 1)
                        yield 71
                        pe.wait_ge(*nth("hid0", 1))
                        bank_free(pe, "ffo")
                        for t in range(FF0_TILES):
                            last = mm(bank("ffo")[0:T, 0:D], hid[0:FF0, t, :], w_ff2[:, t, :], start=(t == 0), stop=(t == FF0_TILES - 1))
                        last.then_inc(sem("ffo"), 1)
                        yield 72
                        transpose("x1T", x2[:], D, T, *nth("x2", 1))
                        yield 74
                        project("q1", w1[:, 0, :], hT["front"][:], D, T, *nth("x1T_out", 1))
                        for n in range(3):
                            yield 77 + 2 * n
                            key_piece(1, n, w1[:, 1, :], "front")
                        for n in range(3):
                            yield 83 + 2 * n
                            value_piece(1, n, w1[:, 2, :], "front")

                    def mid():
                        for n in range(MSTEPS):
                            yield 0.55 * n
                            row_scores(1, n)
                        yield 23
                        transpose("max1T", mxm[1][:], TILES, P, *nth("max1", 1))
                        yield from cross(1, 27)
                        yield 55
                        pv_rows(1)
                        yield 57
                        transpose("o1T", on["mid"][:], D, T, *nth("pv1T_out", 1))
                        yield 59
                        project("out1", oT["mid"][:], w1[:, 3, :], T, D, *nth("o1T_out", 1))
                        for n in range(3):
                            yield 61 + 1.5 * n
                            key_piece(2, n, wkv2[:, 0:D], "mid")
                        yield 67
                        transpose("hT", xs["mid"][:], D, T, *normed_at("xs_ln1"))
                        yield 69
                        project("qs", wq1[:], hT["mid"][:], D, T, *nth("hT_out", 1))
                        yield 70.5
                        project("ks", wkv1[:, 0:D], hT["mid"][:], D, T, *nth("hT_out", 1))
                        yield 72
                        project("vs", hT["mid"][:], wkv1[:, D:2 * D], T, D, *nth("hT_out", 1))
                        kb = kbds[:].rearrange("p h t -> p (h t)")
                        for g in range(4):
                            yield 74 + 2 * g
                            if g == 0:
                                pe.wait_ge(*nth("qs_out", 1))
                                pe.wait_ge(*nth("ks_out", 1))
                            bank_free(pe, "scs", g)
                            mm(bank("scs", g)[0:T, 0:4 * T], qss[:], kb[:, g * 4 * T:(g + 1) * 4 * T], start=True, stop=True
                               ).then_inc(sem("scs"), 1)
                        for g in range(4):
                            yield 82 + 1.5 * g
                            pe.wait_ge(*nth("exps", g + 1))
                            bank_free(pe, "probTs", g)
                            for i in range(4):
                                last = nc.tensor.transpose(bank("probTs", g)[0:T, i * T:(i + 1) * T], sm[:, 4 * g + i, 0:T], ident[0:T, 0:T])
                            last.then_inc(sem("probTs"), 1)
                        yield 88
                        pe.wait_ge(*nth("probTs_out", 4))
                        pe.wait_ge(*nth("vs_out", 1))
                        bank_free(pe, "os")
                        for h in range(H):
                            last = mm(bank("os")[0:T, h * DH:(h + 1) * DH], probT[0:T, h, :], vs[:, h * DH:(h + 1) * DH], start=True, stop=True)
                        last.then_inc(sem("os"), 1)
                        yield 90
                        transpose("osT", on["mid"][:], D, T, *nth("os_out", 1))
                        yield 92
                        project("outs", oT["mid"][:], wo1[:], T, D, *nth("osT_out", 1))
                        for n in range(3):
                            yield 94 + n
                            value_piece(2, n, wkv2[:, D:2 * D], "mid")
                        yield 97
                        transpose("h2T", xs["mid"][:], D, T, *normed_at("xs_ln2"))
                        yield 99
                        project("q2", wq2[:], hT["mid"][:], D, T, *nth("h2T_out", 1))

                    def back():
                        for n in range(MSTEPS):
                            yield 24 + 0.55 * n
                            row_scores(2, n)
                        yield 46.5
                        transpose("max2T", mxm[2][:], TILES, P, *nth("max2", 1))
                        yield from cross(2, 54.5)
                        yield 83
                        pv_rows(2)
                        yield 85
                        transpose("o2T", on["back"][:], D, T, *nth("pv2T_out", 1))
                        yield 86.5
                        project("out2", oT["back"][:], wo2[:], T, D, *nth("o2T_out", 1))
                        yield 92
                        transpose("h3T", xs["back"][:], D, T, *normed_at("xs_ln3"))
                        for n, name in enumerate(("lin", "gate")):
                            yield 94 + 2 * n
                            pe.wait_ge(*nth("h3T_out", 1))
                            bank_free(pe, name)
                            for t in range(FF2_TILES):
                                at = (n * FF2_TILES + t) * D
                                last = mm(bank(name)[:, t * T:(t + 1) * T], wf1[:, at:at + D], hT["back"][:], start=True, stop=True)
                            last.then_inc(sem(name), 1)
                        yield 100
                        pe.wait_ge(*nth("hid2", 1))
                        bank_free(pe, "ff2o")
                        for t in range(FF2_TILES):
                            last = mm(bank("ff2o")[0:T, 0:D], hid[:, t, :], wf2[:, t, :], start=(t == 0), stop=(t == FF2_TILES - 1))
                        last.then_inc(sem("ff2o"), 1)
                        yield 102
                        transpose("x3T", x6[:], D, T, *nth("x6", 1))
                        for n in range(3):
                            yield 104 + n
                            if n == 0:
                                pe.wait_ge(*nth("x3T_out", 1))
                                pe.wait_ge(*nth("ctxT_back_in", 16))
                            at, w = K_CUTS[n]
                            bank_free(pe, "sc3", n)
                            mm(bank("sc3", n)[0:T, 0:w], hT["back"][:], ctxT["back"][:, at:at + w], start=True, stop=True
                               ).then_inc(sem("sc3"), 1)
                        for n in range(3):
                            yield 110.5 + n
                            pe.wait_ge(*nth("exp3", 1))
                            bank_free(pe, "pT3", n)
                            for i in range(4):
                                at, w = CHUNKS[4 * n + i]
                                last = nc.tensor.transpose(bank("pT3", n)[0:w, i * T:(i + 1) * T], p3[:, at:at + w], ident[0:T, 0:T])
                            last.then_inc(sem("pT3"), 1)
                        yield 114
                        pe.wait_ge(*nth("ctxN_in", 32))
                        bank_free(pe, "out3")
                        for c in range(NC):
                            w = CHUNKS[c][1]
                            last = mm(bank("out3")[0:T, 0:D], pT3[0:w, c, :], ctxN[0:w, c, :], start=(c == 0), stop=(c == NC - 1))
                        last.then_inc(sem("out3"), 1)

                    run(front=front, mid=mid, back=back)

                @block.scalar
                def _(act):
                    def move(name, n, dst, src, bias=0.0):
                        act.wait_ge(*nth(name, n + 1))
                        nc.scalar.activation(dst, src, ACT.Identity, bias=bias).then_inc(sem(name + "_out"), 1)

                    def four(t, width=T):
                        return t[:, 0:4 * width].rearrange("p (a n) -> p a n", a=4)

                    def key_piece(L, n):
                        at, w = K_CUTS[n]
                        act.wait_ge(*nth(f"k{L}", n + 1))
                        if n == 2:
                            act.wait_ge(*nth(f"k{L}_lo", 1))
                        if n == 0:
                            user = "mid" if L == 1 else "back"
                            other(act, user, f"max{L}_read", MSTEPS)
                            for g in range(4):
                                other(act, user, f"k{L}_stacked{g}", STACKED)
                            if L == 1:
                                other(act, "mid", "k2_lo", 3)
                        bias = col("bk") if L == 1 else 0.0
                        src = bank(f"k{L}", n)[:, 0:w]
                        nc.scalar.activation(kpart[L, "hi"][:, at:at + w], src, ACT.Identity, bias=bias).then_inc(sem(f"k{L}_hi"), 1)
                        nc.scalar.activation(kf[:, n % 2, 0:w], src, ACT.Identity, bias=bias).then_inc(sem(f"k{L}_out"), 1)

                    def value_piece(L, n):
                        act.wait_ge(*nth(f"v{L}", n + 1))
                        if n == 0:
                            other(act, "mid" if L == 1 else "back", f"prob{L}_used", USTEPS)
                        src = bank(f"v{L}", n)[:].rearrange("p (c h d) -> p c h d", c=4, d=DH)
                        dst = v_aug[L][:, 4 * n:4 * n + 4, :].rearrange("p c (h w) -> p c h w", w=VW)[:, :, :, 0:DH]
                        full = min(NFULL - 4 * n, 4)
                        last = nc.scalar.activation(dst[:, 0:full], src[:, 0:full], ACT.Copy)
                        if full < 4:
                            last = nc.scalar.activation(dst[0:TAIL, full], src[0:TAIL, full], ACT.Copy)
                        last.then_inc(sem(f"v{L}_out"), 1)

                    def cross(L, tick):
                        scale = float(np.float32(1) / np.sqrt(np.float32(DH))) if L == 1 else 0.125
                        for u in range(USTEPS):
                            yield tick + 0.55 * u
                            w = CHUNKS[u % NC][1]
                            act.wait_ge(*nth(f"score{L}", u + 1))
                            if u >= PROBS:
                                act.wait_ge(*nth(f"prob{L}_used", u - PROBS + 1))
                            elif L == 2 and u == 0:
                                other(act, "mid", "prob1_used", USTEPS)
                            nc.scalar.activation(prob[u % PROBS][0:w, :], unit[0:w, u % 2, 0:GROUP * T], ACT.Exp, scale=scale
                                                 ).then_inc(sem(f"prob{L}"), 1)

                    def front():
                        for n in range(2):
                            yield 29 + 2 * n
                            move("val0", n, val0[0:T + 1, n * 512:(n + 1) * 512], bank("val0", n)[0:T + 1, :])
                        for g in range(4):
                            yield 35 + 2 * g
                            act.wait_ge(*nth("shifted0", g + 1))
                            d = sm[:, 4 * g:4 * g + 4, :]
                            nc.scalar.activation(d, d, ACT.Exp, scale=0.125).then_inc(sem("exp0"), 1)
                        for g in range(4):
                            yield 46 + 2 * g
                            move("probT0", g, probT[0:KEYS0, 4 * g:4 * g + 4, :], four(bank("probT0", g)[0:KEYS0]))
                        for n in range(2):
                            yield 54 + 2 * n
                            move("oT0", n, oT0[:, 4 * n:4 * n + 4, :], four(bank("oT0", n)))
                        yield 68
                        act.wait_ge(*nth("ffg_out", 1))
                        nc.scalar.activation(egate[0:FF0, 0:FF0_TILES, :], gate[0:FF0, 0:FF0_TILES, :], ACT.Exp, scale=-1.0).then_inc(sem("eg0"), 1)
                        yield 73
                        move("x1T", 0, hT["front"][:], bank("x1T")[:, 0:T])
                        for n in range(3):
                            yield 78 + 2 * n
                            key_piece(1, n)
                        for n in range(3):
                            yield 84 + 2 * n
                            value_piece(1, n)

                    def mid():
                        yield from cross(1, 27.2)
                        for n in range(3):
                            yield 61.5 + 1.5 * n
                            key_piece(2, n)
                        yield 70
                        move("qs", 0, qss[:], bank("qs")[:, 0:T])
                        yield 73
                        move("vs", 0, vs[:], bank("vs")[0:T, 0:D])
                        for g in range(4):
                            yield 76 + 2 * g
                            act.wait_ge(*nth("scs_out", g + 1))
                            d = sm[:, 4 * g:4 * g + 4, 0:T]
                            nc.scalar.activation(d, d, ACT.Exp, scale=0.125).then_inc(sem("exps"), 1)
                        for g in range(4):
                            yield 82.7 + 1.5 * g
                            if g == 0:
                                other(act, "front", "oT0", 2)
                            move("probTs", g, probT[0:T, 4 * g:4 * g + 4, :], four(bank("probTs", g)[0:T]))
                        yield 91
                        move("osT", 0, oT["mid"][:], bank("osT")[:, 0:T])
                        for n in range(3):
                            yield 94.5 + n
                            value_piece(2, n)

                    def back():
                        yield from cross(2, 54.7)
                        yield 86
                        move("o2T", 0, oT["back"][:], bank("o2T")[:, 0:T])
                        yield 98
                        act.wait_ge(*nth("gate_out", 1))
                        nc.scalar.activation(egate[:], gate[:], ACT.Exp, scale=-GELU).then_inc(sem("eg2"), 1)
                        yield 103
                        move("x3T", 0, hT["back"][:], bank("x3T")[:, 0:T])
                        for n in range(3):
                            yield 104.5 + n
                            if n == 0:
                                other(act, "mid", "probTs", 4)
                                other(act, "mid", "rsums", 1)
                            at, w = K_CUTS[n]
                            move("sc3", n, p3[:, at:at + w], bank("sc3", n)[0:T, 0:w])
                        yield 109
                        act.wait_ge(*nth("max3", 1))
                        nc.scalar.activation(p3, p3, ACT.Exp, bias=stat["back"][0:T, 52:53], accum_out=stat["back"][0:T, 53:54]
                                             ).then_inc(sem("exp3"), 1)
                        for n in range(3):
                            yield 111 + n
                            if n == 0:
                                other(act, "mid", "os", 1)
                            act.wait_ge(*nth("pT3", n + 1))
                            full = min(NFULL - 4 * n, 4)
                            src = four(bank("pT3", n))
                            last = nc.scalar.activation(pT3[:, 4 * n:4 * n + full, :], src[:, 0:full], ACT.Copy)
                            if full < 4:
                                last = nc.scalar.activation(pT3[0:TAIL, NFULL, :], src[0:TAIL, full], ACT.Copy)
                            last.then_inc(sem("pT3_out"), 1)

                    run(front=front, mid=mid, back=back)

                @block.vector
                def _(dve):
                    v = nc.vector
                    steps = [0]

                    def link(ins):
                        steps[0] += 1
                        ins.then_inc(sem("dve_step"), 1)
                        dve.wait_ge(sem("dve_step"), steps[0])

                    def normed(name, src, tick, kind, *ready):
                        st = next(s for s in NORMS if name in NORMS[s])
                        sta = stat[st]
                        yield tick
                        dve.wait_ge(*ready)
                        if kind == "rms":
                            link(v.tensor_tensor_reduce(junk[st][:], src, src, 1.0 / D, 0.0, ALU.mult, ALU.add, sta[0:T, 11:12]))
                        else:
                            link(v.bn_stats(sta[0:T, 4:10], src))
                            link(v.bn_aggr(sta[0:T, 10:12], sta[0:T, 4:10]))
                        v.tensor_scalar(sta[0:T, 1:2], sta[0:T, 11:12], EPS_RMS if kind == "rms" else EPS_LN, None, ALU.add
                                        ).then_inc(sem("norm_var_" + st), 1)
                        yield tick + 2
                        dve.wait_ge(*nth("norm_rstd_" + st, NORMS[st].index(name) + 1))
                        if kind == "rms":
                            v.tensor_scalar(xs[st][:], src, sta[0:T, 2:3], None, ALU.mult).then_inc(sem("xs_" + st), 1)
                        else:
                            v.tensor_scalar(xs[st][:], src, sta[0:T, 10:11], sta[0:T, 2:3], ALU.subtract, ALU.mult
                                            ).then_inc(sem("xs_" + st), 1)

                    def to_hT(name, scale, shift=None):
                        dve.wait_ge(*nth(name, 1))
                        dst, src = hT[STREAM_OF[name]][:], bank(name)[:, 0:T]
                        if shift is None:
                            ins = v.tensor_scalar(dst, src, scale, None, ALU.mult)
                        else:
                            ins = v.tensor_scalar(dst, src, scale, shift, ALU.mult, ALU.add)
                        ins.then_inc(sem(name + "_out"), 1)

                    def wide(t, n):
                        return t.unsqueeze(2).to_broadcast([t.shape[0], t.shape[1], n])

                    def sums(st, width, tag):
                        for g in range(4):
                            dve.wait_ge(*nth("exp" + tag, g + 1))
                            last = v.tensor_reduce(stat[st][0:T, 32 + 4 * g:36 + 4 * g], sm[:, 4 * g:4 * g + 4, 0:width], AX.X, ALU.add)
                        link(last)
                        v.reciprocal(stat[st][0:T, 32:48], stat[st][0:T, 32:48]).then_inc(sem("rsum" + tag), 1)

                    def add_out(name, dst, res, bias, tag):
                        st = STREAM_OF[name]
                        dve.wait_ge(*nth(name, 1))
                        v.tensor_tensor(junk[st][:], bank(name)[0:T, 0:D], bias, ALU.add).then_inc(sem(name + "_out"), 1)
                        dve.wait_ge(*nth(name + "_out", 1))
                        v.tensor_tensor(dst, junk[st][:], res, ALU.add).then_inc(sem(tag), 1)

                    def split_queries(L):
                        dve.wait_ge(*nth(f"q{L}", 1))
                        if L == 1:
                            v.tensor_scalar(qf[:], bank("q1")[:, 0:T], col("bq"), None, ALU.add).then_inc(sem("q1_out"), 1)
                        else:
                            other(dve, "front", "q1_parked", 48)
                            v.tensor_copy(qf[:], bank("q2")[:, 0:T]).then_inc(sem("q2_out"), 1)
                        dve.wait_ge(*nth(f"q{L}_out", 1))
                        v.tensor_copy(qpart["hi"][:], qf[:]).then_inc(sem(f"q{L}_hi"), 1)
                        dve.wait_ge(*nth(f"q{L}_hi", 1))
                        link(v.tensor_tensor(qr[:], qf[:], qpart["hi"][:], ALU.subtract))
                        v.tensor_copy(qpart["mid"][:], qr[:]).then_inc(sem(f"q{L}_mid"), 1)
                        dve.wait_ge(*nth(f"q{L}_mid", 1))
                        v.tensor_tensor(qpart["lo"][:], qr[:], qpart["mid"][:], ALU.subtract).then_inc(sem(f"q{L}_lo"), 1)

                    def query_rows(L):
                        other(dve, "mid" if L == 1 else "back", f"max{L}_read", MSTEPS)
                        v.tensor_tensor(q_rows[L][:], qpart["hi"][:].unsqueeze(1).to_broadcast([P, H, T]), wide(head_mask[:], T),
                                        ALU.mult).then_inc(sem(f"q{L}_rows"), 1)

                    def row_max(L, n):
                        t, s = n // 3, n % 3
                        w = min(P, H * T - t * P)
                        dve.wait_ge(*nth(f"max{L}_scored", n + 1))
                        v.tensor_reduce(mx[L][0:w, t, s:s + 1], rowmax[0:w, n % 2, 0:K_CUTS[s][1]], AX.X, ALU.max
                                        ).then_inc(sem(f"max{L}_read"), 1)

                    def row_max_whole(L):
                        full = H * T // P
                        dve.wait_ge(*nth(f"max{L}_read", MSTEPS))
                        v.tensor_reduce(mxm[L][:, 0:full], mx[L][:, 0:full, :], AX.X, ALU.max)
                        v.tensor_reduce(mxm[L][0:H * T - full * P, full:TILES], mx[L][0:H * T - full * P, full:TILES, :], AX.X, ALU.max
                                        ).then_inc(sem(f"max{L}"), 1)

                    def minus_maxima(L):
                        dve.wait_ge(*nth(f"max{L}T", 1))
                        v.tensor_scalar(mrow[L][:], bank(f"max{L}T")[0:TILES, 0:P], -1.0, None, ALU.mult).then_inc(sem(f"max{L}T_out"), 1)

                    def take_pv(L):
                        dve.wait_ge(*nth(f"prob{L}_used", USTEPS))
                        for j in range(GROUP):
                            q = slice(32 * j, 32 * j + VW)
                            v.tensor_copy(pv[L][q, :], pv_acc[q, 0:4 * T]).then_inc(sem(f"pv{L}"), 1)

                    def attended(L):
                        st = STREAM_OF[f"pv{L}T"]
                        dve.wait_ge(*nth(f"pv{L}T", 1))
                        view = bank(f"pv{L}T")[0:T, :].rearrange("p (h w) -> p h w", w=32)
                        link(v.reciprocal(stat[st][0:T, 16:32], view[:, :, DH]))
                        v.tensor_tensor(on[st][:].rearrange("p (h d) -> p h d", d=DH), view[:, :, 0:DH], wide(stat[st][0:T, 16:32], DH),
                                        ALU.mult).then_inc(sem(f"pv{L}T_out"), 1)

                    def gated(bank_lin, bank_gate, tick, m, tiles, biases, tag):
                        yield tick
                        dve.wait_ge(*nth(bank_lin, 1))
                        if tag == "2":
                            other(dve, "front", "ffo", 1)
                        v.tensor_tensor(hid[0:m, 0:tiles, :], bank(bank_lin)[0:m, 0:tiles * T].rearrange("p (a n) -> p a n", a=tiles),
                                        wide(biases[:, 0:tiles], T), ALU.add).then_inc(sem(bank_lin + "_out"), 1)
                        yield tick + 2
                        dve.wait_ge(*nth(bank_gate, 1))
                        g = gate[0:m, 0:tiles, :]
                        e = egate[0:m, 0:tiles, :]
                        v.tensor_tensor(g, bank(bank_gate)[0:m, 0:tiles * T].rearrange("p (a n) -> p a n", a=tiles),
                                        wide(biases[:, tiles:2 * tiles], T), ALU.add).then_inc(sem(bank_gate + "_out"), 1)
                        dve.wait_ge(*nth(bank_gate + "_out", 1))
                        v.tensor_tensor(hid[0:m, 0:tiles, :], hid[0:m, 0:tiles, :], g, ALU.mult)
                        yield tick + 4
                        dve.wait_ge(*nth("eg" + tag, 1))
                        link(v.tensor_scalar(e, e, 1.0, None, ALU.add))
                        link(v.reciprocal(e, e))
                        v.tensor_tensor(hid[0:m, 0:tiles, :], hid[0:m, 0:tiles, :], e, ALU.mult).then_inc(sem("hid" + tag), 1)

                    def front():
                        sta = stat["front"]
                        yield from normed("xs0", x0[:], 2, "rms", *nth("x0_in", 16))
                        dve.wait_ge(*nth("ctxT_front_in", 16))
                        link(v.tensor_reduce(pool[:, 2:3], ctxT["front"][:], AX.X, ALU.add))
                        v.tensor_scalar(pool[:, 0:1], pool[:, 2:3], 1.0 / S, None, ALU.mult).then_inc(sem("pool"), 1)
                        yield 6
                        dve.wait_ge(*nth("xn", 1))
                        v.tensor_scalar(xnT[:, 0:T], bank("xn")[:, 0:T], col("attn_norm"), None, ALU.mult).then_inc(sem("xn_out"), 1)
                        yield 7
                        dve.wait_ge(*nth("pool_ms", 1))
                        v.tensor_scalar(pool[:, 4:5], bank("pool_ms")[:, 0:1], EPS_RMS, None, ALU.add).then_inc(sem("pool_ms_out"), 1)
                        yield 9
                        dve.wait_ge(*nth("pool_rstd", 1))
                        v.tensor_scalar(pool[:, 3:4], pool[:, 0:1], pool[:, 5:6], col("mem_norm"), ALU.mult, ALU.mult
                                        ).then_inc(sem("pool_normed"), 1)
                        yield 11
                        dve.wait_ge(*nth("mem", 1))
                        v.tensor_copy(xnT[:, T:T + 1], bank("mem")[:, 0:1]).then_inc(sem("mem_out"), 1)
                        W = T + 1
                        for p in range(PAIRS):
                            yield 13 + 2 * p
                            dve.wait_ge(*nth("qk", p + 1))
                            if p >= 2:
                                dve.wait_ge(*nth("roped", 3 * (p - 1)))
                            v.tensor_tensor(rope_a[:, p % 2, :], bank("qk", p)[:, 0:2 * W], cos2[:], ALU.mult)
                            v.tensor_tensor(rope_b[:, p % 2, :], bank("qk", p)[:, 2 * W:4 * W], sin2[:], ALU.mult).then_inc(sem("qk_out"), 1)
                        for g in range(4):
                            yield 33 + 2 * g
                            dve.wait_ge(*nth("score0", g + 1))
                            s = bank("score0", g)[0:T, 0:4 * KEYS0].rearrange("p (a n) -> p a n", a=4)
                            v.tensor_tensor(sm[:, 4 * g:4 * g + 4, :], s, mask0[:].unsqueeze(1).to_broadcast([T, 4, KEYS0]), ALU.add
                                            ).then_inc(sem("score0_out"), 1)
                            dve.wait_ge(*nth("score0_out", g + 1))
                            v.tensor_reduce(sta[0:T, 16 + 4 * g:20 + 4 * g], sm[:, 4 * g:4 * g + 4, :], AX.X, ALU.max).then_inc(sem("max0"), 1)
                        yield 42
                        sums("front", KEYS0, "0")
                        yield 58
                        dve.wait_ge(*nth("out0", 1))
                        v.tensor_tensor(x1[:], bank("out0")[0:T, 0:D], x0[:], ALU.add).then_inc(sem("out0_out"), 1)
                        yield from normed("xs_ff", x1[:], 59, "rms", *nth("out0_out", 1))
                        yield 63
                        to_hT("fx0", col("ff_norm"))
                        yield from gated("ffa", "ffg", 65, FF0, FF0_TILES, b_ff1[:], "0")
                        yield 71.5
                        other(dve, "mid", "x3", 1)
                        add_out("ffo", x2[:], x1[:], row("ff_b2"), "x2")
                        yield 75
                        split_queries(1)
                        yield 78
                        query_rows(1)

                    def mid():
                        for n in range(MSTEPS):
                            yield 0.3 + 0.55 * n
                            row_max(1, n)
                        yield 22
                        row_max_whole(1)
                        yield 23.5
                        minus_maxima(1)
                        yield 54
                        take_pv(1)
                        yield 56
                        attended(1)
                        yield 58
                        dve.wait_ge(*nth("o1T", 1))
                        v.tensor_scalar(oT["mid"][:], bank("o1T")[:, 0:T], col("bv"), None, ALU.add).then_inc(sem("o1T_out"), 1)
                        yield 60
                        add_out("out1", x3[:], x2[:], row("bo"), "x3")
                        yield from normed("xs_l1", x3[:], 61, "ln", *nth("x3", 1))
                        dve.wait_ge(*normed_at("xs_l1"))
                        link(v.tensor_tensor(junk["mid"][:], xs["mid"][:], row("gamma"), ALU.mult))
                        v.tensor_tensor(x3[:], junk["mid"][:], row("beta"), ALU.add).then_inc(sem("x3b"), 1)
                        yield from normed("xs_ln1", x3[:], 64, "ln", *nth("x3b", 1))
                        yield 68
                        to_hT("hT", col("ln1_s"), col("ln1_b"))
                        yield 71
                        dve.wait_ge(*nth("ks", 1))
                        other(dve, "front", "out0", 1)
                        v.tensor_tensor(kbds[:], bank("ks")[:, 0:T].unsqueeze(1).to_broadcast([P, H, T]), wide(head_mask[:], T), ALU.mult
                                        ).then_inc(sem("ks_out"), 1)
                        for g in range(4):
                            yield 75 + 2 * g
                            dve.wait_ge(*nth("scs", g + 1))
                            if g == 0:
                                other(dve, "front", "probT0", 4)
                            s = bank("scs", g)[0:T, 0:4 * T].rearrange("p (a n) -> p a n", a=4)
                            m = stat["mid"][0:T, 16 + 4 * g:20 + 4 * g]
                            link(v.tensor_reduce(m, s, AX.X, ALU.max))
                            v.tensor_tensor(sm[:, 4 * g:4 * g + 4, 0:T], s, wide(m, T), ALU.subtract).then_inc(sem("scs_out"), 1)
                        yield 83
                        sums("mid", T, "s")
                        yield 89
                        dve.wait_ge(*nth("rsums", 1))
                        dve.wait_ge(*nth("os", 1))
                        v.tensor_tensor(on["mid"][:].rearrange("p (h d) -> p h d", d=DH), bank("os")[0:T, 0:D].rearrange("p (h d) -> p h d", d=DH),
                                        wide(stat["mid"][0:T, 32:48], DH), ALU.mult).then_inc(sem("os_out"), 1)
                        yield 93
                        other(dve, "back", "x5", 1)
                        add_out("outs", x4[:], x3[:], row("bo1"), "x4")
                        yield from normed("xs_ln2", x4[:], 94, "ln", *nth("x4", 1))
                        yield 98
                        to_hT("h2T", col("ln2_s"), col("ln2_b"))
                        yield 100
                        split_queries(2)
                        query_rows(2)

                    def back():
                        sta = stat["back"]
                        for n in range(MSTEPS):
                            yield 24.3 + 0.55 * n
                            row_max(2, n)
                        yield 46
                        row_max_whole(2)
                        yield 47
                        minus_maxima(2)
                        yield 82
                        take_pv(2)
                        yield 84
                        attended(2)
                        yield 88
                        add_out("out2", x5[:], x4[:], row("bo2"), "x5")
                        yield from normed("xs_ln3", x5[:], 89, "ln", *nth("x5", 1))
                        yield 93
                        to_hT("h3T", col("ln3_s"), col("ln3_b"))
                        yield from gated("lin", "gate", 95, P, FF2_TILES, bf1[:], "2")
                        yield 101
                        add_out("ff2o", x6[:], x5[:], row("bff2"), "x6")
                        yield 107.5
                        dve.wait_ge(*nth("sc3_out", 3))
                        v.tensor_reduce(sta[0:T, 52:53], p3, AX.X, ALU.max, negate=True).then_inc(sem("max3"), 1)
                        yield 111
                        dve.wait_ge(*nth("exp3", 1))
                        link(v.reciprocal(sta[0:T, 58:59], sta[0:T, 53:54]))
                        yield 115
                        dve.wait_ge(*nth("out3", 1))
                        v.scalar_tensor_tensor(y[:], bank("out3")[0:T, 0:D], sta[0:T, 58:59], x6[:], ALU.mult, ALU.add).then_inc(sem("y"), 1)

                    run(front=front, mid=mid, back=back)

                @block.gpsimd
                def _(pool_eng):
                    g = nc.gpsimd

                    def rstd(ready, done, dst, src, n, count=1):
                        pool_eng.wait_ge(*nth(ready, count))
                        g.tensor_tensor(dst, src, minus_half[0:n, :], ALU.pow).then_inc(sem(done), 1)

                    def norm_rstd(name):
                        st = next(s for s in NORMS if name in NORMS[s])
                        rstd("norm_var_" + st, "norm_rstd_" + st, stat[st][0:T, 2:3], stat[st][0:T, 1:2], T, NORMS[st].index(name) + 1)

                    def key_piece(L, n):
                        at, w = K_CUTS[n]
                        f, r = kf[:, n % 2, 0:w], kr[:, n % 2, 0:w]
                        hi, mid_, lo = (kpart[L, part][:, at:at + w] for part in ("hi", "mid", "lo"))
                        pool_eng.wait_ge(*nth(f"k{L}_out", n + 1))
                        pool_eng.wait_ge(*nth(f"k{L}_hi", n + 1))
                        g.tensor_tensor(r, f, hi, ALU.subtract).then_inc(sem(f"k{L}_r"), 1)
                        pool_eng.wait_ge(*nth(f"k{L}_r", n + 1))
                        g.tensor_copy(mid_, r).then_inc(sem(f"k{L}_mid"), 1)
                        pool_eng.wait_ge(*nth(f"k{L}_mid", n + 1))
                        g.tensor_tensor(lo, r, mid_, ALU.subtract).then_inc(sem(f"k{L}_lo"), 1)

                    def by_head(t):
                        return t.unsqueeze(2).to_broadcast([T, 4, KEYS0])

                    def front():
                        sta = stat["front"]
                        yield 3
                        norm_rstd("xs0")
                        yield 5.5
                        pool_eng.wait_ge(*nth("pool", 1))
                        g.tensor_tensor(pool[:, 1:2], pool[:, 0:1], pool[:, 0:1], ALU.mult).then_inc(sem("pool_sq"), 1)
                        yield 8
                        rstd("pool_ms_out", "pool_rstd", pool[:, 5:6], pool[:, 4:5], P)
                        W = T + 1
                        for p in range(PAIRS):
                            yield 14 + 2 * p
                            pool_eng.wait_ge(*nth("qk_out", p + 1))
                            ra, rb = rope_a[:, p % 2, :], rope_b[:, p % 2, :]
                            g.tensor_tensor(qT0[:, p, :], ra[:, 0:T], rb[:, 0:T], ALU.add).then_inc(sem("roped"), 1)
                            for j in range(2):
                                pool_eng.wait_ge(*nth("roped", 3 * p + j + 1))
                                q = slice(64 * j, 64 * j + 64)
                                g.tensor_tensor(kbd0[q, p, j, 0:W], ra[q, W:2 * W], rb[q, W:2 * W], ALU.add).then_inc(sem("roped"), 1)
                            pool_eng.wait_ge(*nth("roped", 3 * p + 3))
                        for n in range(4):
                            yield 34 + 2 * n
                            pool_eng.wait_ge(*nth("max0", n + 1))
                            d = sm[:, 4 * n:4 * n + 4, :]
                            g.tensor_tensor(d, d, by_head(sta[0:T, 16 + 4 * n:20 + 4 * n]), ALU.subtract).then_inc(sem("shifted0"), 1)
                        for n in range(4):
                            yield 44 + n
                            pool_eng.wait_ge(*nth("rsum0", 1))
                            d = sm[:, 4 * n:4 * n + 4, :]
                            g.tensor_tensor(d, d, by_head(sta[0:T, 32 + 4 * n:36 + 4 * n]), ALU.mult).then_inc(sem("prob0"), 1)
                        yield 60
                        norm_rstd("xs_ff")
                        for n in range(3):
                            yield 79 + 2 * n
                            key_piece(1, n)

                    def mid():
                        yield 62
                        norm_rstd("xs_l1")
                        for n in range(2):
                            yield 62.5 + 1.5 * n
                            key_piece(2, n)
                        yield 65
                        norm_rstd("xs_ln1")
                        yield 65.5
                        key_piece(2, 2)
                        yield 95
                        norm_rstd("xs_ln2")

                    def back():
                        yield 90
                        norm_rstd("xs_ln3")

                    run(front=front, mid=mid, back=back)

            used = [s.num for s in sems.values()]
            nc.all_engine_barrier(sems_to_clear=range(min(used), max(used) + 1))

        iteration({"front": 0})
        iteration({"front": 1, "mid": 0})
        with nc.Fori(PRE, B) as b:
            iteration({"front": b, "mid": b - 1, "back": b - 2})
        iteration({"mid": B - 1, "back": B - 2})
        iteration({"back": B - 1})


def _constants():
    W = T + 1
    inv = (1.0 / 10000.0 ** (np.arange(0, DH0, 2, dtype=np.float32) / np.float32(DH0))).astype(np.float32)
    ang = np.repeat(np.arange(T, dtype=np.float32)[:, None] * inv[None, :], 2, axis=-1).astype(np.float32)
    cos = np.ones((DH0, W), np.float32)
    sin = np.zeros((DH0, W), np.float32)
    cos[:, :T] = np.cos(ang.astype(np.float64)).T
    sin[:, :T] = np.sin(ang.astype(np.float64)).T
    sin[0::2] = -sin[0::2]
    q, k = np.arange(T)[:, None], np.arange(T)[None, :]
    mask = np.zeros((T, KEYS0), np.float32)
    mask[:, :T] = np.where((q >= k) & (q // SEG == k // SEG), 0.0, -1e30)
    mask[:, T] = DH0 ** 0.5 * np.log(float(NM))
    heads = (np.arange(D)[:, None] // DH == np.arange(H)[None, :]).astype(np.float32)
    return {
        "c_ident": np.eye(P, dtype=np.float32), "c_mean": np.full((P, P), 1.0 / D, np.float32),
        "c_cos": np.tile(cos, (2, 2)), "c_sin": np.tile(sin, (2, 2)), "c_mask": mask, "c_head_mask": heads,
    }


def _padded(x, n, axis=-1):
    shape = list(x.shape)
    shape[axis] = n
    out = np.zeros(shape, x.dtype)
    out[tuple(slice(0, k) for k in x.shape)] = x
    return out


def kernel(**inputs):
    import concourse.bacc as _bacc
    from concourse import mybir as _mybir
    from concourse.bass_utils import run_bass_kernel_spmd as _run

    i = {k: np.asarray(v) for k, v in inputs.items()}
    ctx = i["ctx_1024"]
    main = ctx[:, :NFULL * P].reshape(B, P, NFULL, D)
    tail = ctx[:, NFULL * P:]
    qkv = i["L0_xattn_to_qkv_w"]
    swapped = qkv[:, :2 * E0].reshape(D, E0, 2)[:, :, ::-1].reshape(D, 2 * E0)
    pm = i["L0_xattn_persist_mem"]
    ff1, ffb = i["L0_xattn_ff_w1"], i["L0_xattn_ff_b1"]
    n0 = FF0_TILES * FF0
    data = {
        "x": i["x"], "ctx_main": main, "ctx_tail": tail,
        "ctxT": np.concatenate([main.transpose(0, 3, 2, 1).reshape(B, D, NFULL * P), tail.transpose(0, 2, 1)], axis=2),
        "cols": np.stack([i["L0_xattn_attn_norm_w"], i["L0_xattn_mem_pool_norm_w"], i["L0_xattn_ff_norm_w"], i["L1_xattn_bq"],
                          i["L1_xattn_bk"], i["L1_xattn_bv"]] + [i[f"L2_xattn_ln{n}_{c}"] for n in (1, 2, 3) for c in "sb"], axis=1),
        "rows": np.tile(np.concatenate([i["L0_xattn_ff_b2"], i["L1_xattn_bo"], i["L1_xattn_gamma"], i["L1_xattn_beta"],
                                        i["L2_xattn_bo1"], i["L2_xattn_bo2"], i["L2_xattn_bff2"]])[None], (T, 1)),
        "w_qkv": qkv, "w_rot": swapped,
        "w_out0": i["L0_xattn_to_out_w"].reshape(PAIRS, P, D).transpose(1, 0, 2),
        "w_mem": i["L0_xattn_to_mem_tokens_w"],
        "w_ff1": np.concatenate([_padded(ff1[:, :DFF0], n0), _padded(ff1[:, DFF0:], n0)], axis=1),
        "b_ff1": np.concatenate([_padded(ffb[:DFF0], n0), _padded(ffb[DFF0:], n0)]).reshape(2 * FF0_TILES, FF0).T,
        "w_ff2": _padded(i["L0_xattn_ff_w2"], n0, 0).reshape(FF0_TILES, FF0, D).transpose(1, 0, 2),
        "w1": np.stack([i[f"L1_xattn_W{c}"].T for c in "qkvo"], axis=1),
        "wq1": i["L2_xattn_Wq1"], "wkv1": i["L2_xattn_Wkv1"], "wo1": i["L2_xattn_Wo1"],
        "wq2": i["L2_xattn_Wq2"], "wkv2": i["L2_xattn_Wkv2"], "wo2": i["L2_xattn_Wo2"],
        "wf1": i["L2_xattn_Wff1"], "bf1": i["L2_xattn_bff1"].reshape(2 * FF2_TILES, P).T,
        "wf2": i["L2_xattn_Wff2"].reshape(FF2_TILES, P, D).transpose(1, 0, 2),
        "pm_k": pm.reshape(PAIRS, 2, NPM, DH0).transpose(1, 3, 0, 2).reshape(P, PAIRS, NPM),
        "pm_v": pm.transpose(1, 0, 2).reshape(NPM, E0),
        **_constants(),
    }
    nc = _bacc.Bacc("TRN2", target_bir_lowering=False, num_devices=1)
    arrays, aps = {}, {}
    for name, arr in data.items():
        arr = np.ascontiguousarray(arr)
        arrays[f"in_{name}"] = arr
        aps[name] = nc.dram_tensor(f"in_{name}", arr.shape, _mybir.dt.from_np(arr.dtype), kind="ExternalInput").ap()
    aps["out"] = nc.dram_tensor("out_0", (B, T, D), F32, kind="ExternalOutput").ap()
    xattn_program(nc, aps)
    return _run(nc, [arrays], core_ids=[0]).results[0]["out_0"]
```

```python
from contextlib import ExitStack

import numpy as np

import concourse.bass as bass
from concourse import mybir

F32 = mybir.dt.float32
BF16 = mybir.dt.bfloat16
ALU = mybir.AluOpType
ACT = mybir.ActivationFunctionType
AX = mybir.AxisListType

B, T, S, D = 32, 100, 1444, 128
H = 16
P = 128
NFULL = S // P
TAIL = S - NFULL * P
CHUNKS = [(c * P, P) for c in range(NFULL)] + [(NFULL * P, TAIL)]
NC = len(CHUNKS)
DH0, NPM, NM, SEG = 64, 16, 16, 64
PAIRS = H // 2
KEYS0 = T + 1 + NPM
E0 = H * DH0
DFF0 = int(D * 4 * 2 / 3)
FF0_TILES = 3
FF0 = -(-DFF0 // FF0_TILES)
FF2_TILES = 4
DH = D // H
TERMS = [("hi", "hi"), ("mid", "hi"), ("hi", "mid"), ("mid", "mid"), ("lo", "hi"), ("hi", "lo")]
KROWS = len(TERMS) * 2 * DH
VW = DH + 1
EPS_RMS, EPS_LN = 1.1920929e-07, 1e-05
GELU = 1.702

COLS = ["attn_norm", "mem_norm", "ff_norm", "bq", "bk", "bv", "ln1_s", "ln1_b", "ln2_s", "ln2_b", "ln3_s", "ln3_b"]
ROWS = ["ff_b2", "bo", "gamma", "beta", "bo1", "bo2", "bff2"]

LAGS = {
    "local": 0,
    "prep1": 1,
    "stacks1": 1,
    "maxima1": 1,
    "cross1": 2,
    "keys2": 2,
    "stacks2": 3,
    "values2": 3,
    "maxima2": 3,
    "cross2": 3,
    "final": 4,
}
STREAMS = list(LAGS)

LIGHT = {
    "bank_l": [
        ("xn", 1, "dve", "local"), ("pool_ms", 1, "dve", "local"), ("mem", 1, "dve", "local"), ("qk", PAIRS, "dve", "local"),
        ("val0", 2, "act", "local"), ("score0", 4, "dve", "local"), ("probT0", 4, "act", "local"), ("oT0", 2, "act", "local"),
        ("out0", 1, "dve", "local"), ("fx0", 1, "dve", "local"), ("ffa", 1, "dve", "local"), ("ffg", 1, "dve", "local"),
        ("ffo", 1, "dve", "local")],
    "bank_c": [
        ("pv1T", 1, "dve", "cross1"), ("o1T", 1, "dve", "cross1"), ("out1", 1, "dve", "cross1"), ("hT", 1, "dve", "cross1"),
        ("qs", 1, "act", "cross1"), ("ks", 1, "dve", "cross1"), ("vs", 1, "act", "cross1"), ("scs", 4, "dve", "cross1"),
        ("probTs", 4, "act", "cross1"), ("os", 1, "dve", "cross1"), ("osT", 1, "act", "cross1"), ("outs", 1, "dve", "cross1"),
        ("h2T", 1, "dve", "cross1"), ("q2", 1, "dve", "cross1")],
    "bank_s": [
        ("x1T", 1, "act", "prep1"), ("q1", 1, "dve", "prep1"), ("h3T", 1, "dve", "final"), ("lin", 1, "dve", "final"),
        ("gate", 1, "dve", "final"), ("ff2o", 1, "dve", "final"), ("x3T", 1, "act", "final"), ("sc3", 3, "act", "final"),
        ("pT3", 3, "act", "final"), ("out3", 1, "dve", "final"), ("v2", 3, "act", "values2"), ("k1", 3, "act", "prep1"),
        ("v1", 3, "act", "prep1"), ("max2T", 4, "dve", "maxima2"), ("k2", 3, "act", "keys2"), ("max1T", 4, "dve", "maxima1"),
        ("pv2T", 1, "dve", "cross2"), ("o2T", 1, "act", "cross2"), ("out2", 1, "dve", "cross2")],
}
BANK_OF = {name: b for b, table in LIGHT.items() for name, _, _, _ in table}
STREAM_OF = {name: stream for table in LIGHT.values() for name, _, _, stream in table}
READER = {name: reader for table in LIGHT.values() for name, _, reader, _ in table}
NORMS = {"local": ["xs0", "xs_ff"], "cross1": ["xs_l1", "xs_ln1", "xs_ln2"], "final": ["xs_ln3"]}

K_CUTS = [(0, 482), (482, 481), (963, 481)]
TILES = -(-H * T // P)
MSTEPS = TILES * len(K_CUTS)
GROUP = 4
TILE_ENDS = [-(-GROUP * T * (g + 1) // P) for g in range(H // GROUP)]
GROUP_TILES = list(zip([0] + TILE_ENDS[:-1], TILE_ENDS))
USTEPS = H // GROUP * NC
STACKED = 16 * len(TERMS) * 2
PROBS = 4
UTICK = 0.95
LAG = 2
PRE = max(LAGS.values())


PLACES = {
    "sync": {
        "local": (
            [0],
            [0]),
        "stacks2": (
            [7, 12.5, 24, 30, 35.5, 47],
            [1.2, 8.4, 18.693, 31.715, 32.315, 43.988]),
        "final": (
            [0.3, 37],
            [15.6, 61.411]),
        "prep1": (
            [0.2, 5, 50],
            [17.4, 40.115, 51.188]),
        "cross1": (
            [14, 98],
            [18, 112.375]),
        "maxima2": (
            [22.55, 36.5, 50.45, 64.4],
            [39.515, 58.388, 63.133, 87.583]),
        "stacks1": (
            [77.7, 89.1, 100.5, 111.9],
            [65.739, 77.549, 89.333, 105.175]),
        "maxima1": (
            [19.85, 32, 44.15, 56.3],
            [84.749, 96.533, 97.881, 103.975]),
    },
    "tensor": {
        "cross1": (
            [0.5, 1.45, 2.4, 3.35, 4.3, 5.25, 6.2, 7.15, 8.1, 9.05, 10, 10.95, 11.9, 12.85, 13.8, 14.75, 15.7, 16.65, 17.6,
             18.55, 19.5, 20.45, 21.4, 22.35, 23.3, 24.25, 25.2, 26.15, 27.1, 28.05, 29, 29.95, 30.9, 31.85, 32.8, 33.75,
             34.7, 35.65, 36.6, 37.55, 38.5, 39.45, 40.4, 41.35, 42.3, 43.25, 44.2, 45.15, 46.1, 47.05, 51, 53, 55, 63, 65,
             66.5, 68, 70, 71.8, 73.6, 75.4, 77.5, 79, 80.5, 82, 84, 86, 88, 93, 95],
            [0, 0.334, 1.07, 1.798, 2.526, 3.254, 3.982, 4.71, 5.414, 6.058, 6.678, 7.196, 9.447, 9.839, 10.983, 12.047,
             12.439, 13.597, 13.989, 14.693, 15.085, 15.789, 16.181, 18.101, 18.493, 19.651, 20.043, 21.201, 21.676, 22.751,
             24.876, 25.268, 28.282, 28.875, 30.321, 31.715, 32.308, 33.763, 34.521, 34.913, 37.155, 37.747, 38.751, 39.344,
             40.268, 40.86, 41.785, 43.396, 44.526, 46.663, 50.317, 59.95, 61.179, 69.389, 74.928, 75.695, 77.942, 78.763,
             82.831, 85.633, 89.133, 92.069, 93.412, 94.667, 95.774, 96.89, 100.375, 101.263, 104.864, 105.916]),
        "maxima2": (
            [0.5, 2.05, 3.6, 5.15, 6.7, 8.25, 9.8, 11.35, 12.9, 14.45, 16, 17.55, 19.1, 20.65, 22.2, 22.51, 23.75, 25.3,
             26.85, 28.4, 29.95, 31.5, 33.05, 34.6, 36.15, 36.46, 37.7, 39.25, 40.8, 42.35, 43.9, 45.45, 47, 48.55, 50.1,
             50.41, 51.65, 53.2, 54.75, 56.3, 57.85, 59.4, 60.95, 62.5, 64.05, 64.36],
            [0.668, 7.713, 7.913, 14.381, 15.477, 26.426, 28.674, 29.267, 31.515, 32.107, 32.783, 34.321, 35.334, 36.955,
             37.547, 38.367, 39.143, 39.736, 40.66, 41.584, 43.196, 44.326, 44.752, 46.889, 48.929, 51.599, 51.706, 51.951,
             53.026, 55.225, 55.818, 58.586, 58.786, 59.75, 60.979, 62.407, 62.514, 63.851, 64.443, 65.539, 66.484, 66.684,
             81.48, 81.48, 81.48, 81.48]),
        "final": (
            [3.5, 6, 8, 16, 18, 20, 21.3, 22.6, 29, 30.3, 31.6, 33.5],
            [7.588, 8.781, 10.317, 16.573, 21.593, 23.4, 26.626, 30.713, 39.936, 41.252, 43.994, 56.018]),
        "local": (
            [5, 6, 10, 12, 14, 16, 18, 20, 22, 24, 26, 28, 30, 32, 34, 36, 38, 40, 42, 44, 46, 48, 50, 57, 62, 64, 66, 71],
            [8.491, 9.445, 10.981, 11.375, 12.925, 17.429, 18.979, 20.529, 22.079, 24.204, 25.754, 27.428, 29.467, 32.983,
             45.883, 48.149, 50.819, 54.659, 59.379, 60.647, 61.683, 63.107, 65.74, 67.276, 101.138, 101.984, 103.857,
             111.444]),
        "prep1": (
            [0.1, 1.2, 45, 47, 49, 52, 54, 56],
            [32.7, 34.155, 36.151, 45.081, 52.224, 104.947, 106.601, 110.281]),
        "values2": (
            [41, 42.5, 44],
            [42.34, 47.293, 49.129]),
        "cross2": (
            [66, 66.95, 67.9, 68.85, 69.8, 70.75, 71.7, 72.65, 73.6, 74.55, 75.5, 76.45, 77.4, 78.35, 79.3, 80.25, 81.2,
             82.15, 83.1, 84.05, 85, 85.95, 86.9, 87.85, 88.8, 89.75, 90.7, 91.65, 92.6, 93.55, 94.5, 95.45, 96.4, 97.35,
             98.3, 99.25, 100.2, 101.15, 102.1, 103.05, 104, 104.95, 105.9, 106.85, 107.8, 108.75, 109.7, 110.65, 111.6,
             112.55, 115.5, 117, 118.5],
            [49.985, 50.151, 53.226, 53.618, 55.426, 58.987, 60.033, 62.015, 62.715, 64.051, 64.643, 65.147, 66.884, 69.472,
             70.276, 70.869, 71.461, 72.548, 73.14, 73.732, 74.325, 75.861, 76.454, 76.957, 77.55, 78.156, 79.937, 80.715,
             82.047, 82.439, 84.145, 84.784, 85.241, 86.96, 88.349, 88.741, 91.285, 91.677, 94.075, 96.106, 96.498, 97.202,
             97.594, 99.215, 99.607, 100.5, 102.524, 103.297, 104.355, 106.082, 112.406, 113.945, 114.566]),
        "maxima1": (
            [0, 1.35, 2.7, 4.05, 5.4, 6.75, 8.1, 9.45, 10.8, 12.15, 13.5, 14.85, 16.2, 17.55, 18.9, 19.17, 20.25, 21.6,
             22.95, 24.3, 25.65, 27, 28.35, 29.7, 31.05, 31.32, 32.4, 33.75, 35.1, 36.45, 37.8, 39.15, 40.5, 41.85, 43.2,
             43.47, 44.55, 45.9, 47.25, 48.6, 49.95, 51.3, 52.65, 54, 55.35, 55.62],
            [68.988, 69.189, 70.076, 70.668, 71.261, 71.853, 72.347, 72.94, 73.532, 74.124, 75.094, 75.495, 76.253, 78.563,
             79.429, 79.629, 79.736, 80.515, 81.28, 81.846, 83.497, 83.945, 84.583, 86.299, 86.76, 87.583, 87.69, 88.149,
             89.88, 90.884, 91.085, 92.545, 93.111, 93.875, 94.467, 94.999, 95.106, 95.574, 98.788, 99.014, 100.173, 101.583,
             102.524, 102.524, 102.524, 103.084]),
        "keys2": (
            [98, 100, 102],
            [90.08, 97.986, 108.255]),
    },
    "scalar": {
        "cross1": (
            [0.7, 1.65, 2.6, 3.55, 4.5, 5.45, 6.4, 7.35, 8.3, 9.25, 10.2, 11.15, 12.1, 13.05, 14, 14.95, 15.9, 16.85, 17.8,
             18.75, 19.7, 20.65, 21.6, 22.55, 23.5, 24.45, 25.4, 26.35, 27.3, 28.25, 29.2, 30.15, 31.1, 32.05, 33, 33.95,
             34.9, 35.85, 36.8, 37.75, 38.7, 39.65, 40.6, 41.55, 42.5, 43.45, 44.4, 45.35, 50, 66, 69, 72, 73.8, 75.6, 77.4,
             78.2, 79.7, 81.2, 82.7, 87],
            [0.534, 0.918, 1.998, 2.726, 3.454, 4.182, 4.91, 5.554, 6.174, 6.692, 8.59, 8.974, 10.039, 10.431, 11.575,
             12.765, 13.149, 14.189, 14.581, 15.285, 15.677, 16.381, 16.773, 18.693, 19.085, 20.243, 20.635, 21.793, 22.311,
             23.343, 25.468, 25.86, 28.96, 29.467, 30.999, 32.307, 33.117, 34.355, 36.251, 36.635, 38.247, 38.631, 39.343,
             39.936, 40.86, 41.452, 42.377, 43.988, 47.656, 75.301, 78.356, 83.415, 85.76, 89.115, 91.99, 92.601, 93.944,
             95.199, 96.306, 100.7]),
        "local": (
            [2, 29, 31, 34.5, 36.5, 38.5, 40.5, 41, 43, 45, 47, 49, 51, 68],
            [7.2, 28.482, 30.521, 47.173, 52.174, 54.316, 55.886, 58.786, 59.963, 61.179, 62.215, 64.051, 66.684, 105.626]),
        "final": (
            [10.5, 19, 21, 22.3, 23.6, 27, 29.8, 31.1, 32.4],
            [12.338, 22.177, 24.404, 27.628, 31.715, 34.768, 40.468, 41.836, 44.526]),
        "prep1": (
            [0.6, 46, 48, 50, 53, 55, 57],
            [32.983, 37.155, 46.083, 53.226, 106.003, 107.657, 111.337]),
        "values2": (
            [42, 43.55, 45.1],
            [43.396, 48.424, 50.185]),
        "cross2": (
            [66.2, 67.15, 68.1, 69.05, 70, 70.95, 71.9, 72.85, 73.8, 74.75, 75.7, 76.65, 77.6, 78.55, 79.5, 80.45, 81.4,
             82.35, 83.3, 84.25, 85.2, 86.15, 87.1, 88.05, 89, 89.95, 90.9, 91.85, 92.8, 93.75, 94.7, 95.65, 96.6, 97.55,
             98.5, 99.45, 100.4, 101.35, 102.3, 103.25, 104.2, 105.15, 106.1, 107.05, 108, 108.95, 109.9, 110.85, 115, 118],
            [50.714, 51.098, 54.799, 55.183, 56.369, 59.579, 60.625, 62.607, 63.307, 64.643, 65.235, 65.739, 67.476, 70.064,
             70.868, 71.461, 72.053, 73.14, 73.732, 74.324, 74.917, 76.453, 77.046, 77.549, 78.514, 78.898, 80.529, 81.307,
             82.639, 83.031, 84.737, 85.376, 86.187, 87.552, 89.542, 89.926, 92.985, 93.369, 94.667, 96.698, 97.09, 97.794,
             98.186, 99.892, 100.276, 101.092, 103.284, 104.057, 106.508, 114.312]),
        "keys2": (
            [98.7, 100.7, 102.7],
            [91.084, 98.988, 109.257]),
    },
    "vector": {
        "final": (
            [0.2, 2.2, 4.5, 7, 9, 11, 17, 25.5, 29, 36],
            [0, 1.05, 8.371, 9.712, 11.248, 12.885, 17.629, 33.075, 38.872, 61.028]),
        "cross2": (
            [0.4, 115, 116.3, 119.5],
            [0.346, 111.324, 113.458, 115.192]),
        "maxima2": (
            [1.2, 2.75, 4.3, 5.85, 7.4, 8.95, 10.5, 12.05, 13.6, 15.15, 16.7, 18.25, 19.8, 21.35, 22.9, 23.675, 24.45, 26,
             27.55, 29.1, 30.65, 32.2, 33.75, 35.3, 36.85, 37.625, 38.4, 39.95, 41.5, 43.05, 44.6, 46.15, 47.7, 49.25, 50.8,
             51.575, 52.35, 53.9, 55.45, 57, 58.55, 60.1, 65.525],
            [1.306, 9.008, 10.606, 16.774, 18.859, 27.184, 29.075, 29.667, 31.915, 32.508, 34.648, 36.031, 36.678, 37.355,
             37.947, 38.674, 39.544, 40.136, 41.06, 41.985, 43.596, 45.638, 46.282, 50.699, 51.265, 51.906, 52.107, 54.539,
             55.105, 56.321, 56.888, 58.986, 59.63, 60.462, 61.379, 62.815, 63.013, 64.251, 64.843, 65.94, 66.884, 67.57,
             87.265]),
        "local": (
            [2, 4, 5, 6, 7, 9, 11, 13, 15, 17, 19, 21, 23, 25, 27, 33, 35, 36.8, 37, 38.8, 39, 40.8, 42, 58, 59, 61, 63, 65,
             67, 69, 71.5],
            [7.2, 8.175, 8.71, 8.779, 9.647, 10.416, 11.183, 12.247, 16.216, 18.301, 19.851, 21.401, 22.951, 25.076, 26.626,
             44.526, 46.863, 47.975, 49.587, 52.777, 53.427, 55.671, 57.454, 98.894, 99.216, 100.822, 101.584, 103.276,
             104.744, 108.774, 112.604]),
        "prep1": (
            [1.8, 58.5],
            [35.214, 68.283]),
        "cross1": (
            [50, 52, 54, 56, 57, 59, 60, 62, 64, 67.5, 71, 72.8, 74.6, 76.4, 78.5, 85, 89, 90, 92, 94, 96.5],
            [48.625, 58.104, 60.233, 61.945, 62.469, 63.58, 65.409, 66.507, 74.518, 76.061, 81.726, 84.463, 88.029, 90.892,
             95.454, 100.053, 101.813, 102.93, 104.488, 105.506, 106.282]),
        "maxima1": (
            [0.5, 1.85, 3.2, 4.55, 5.9, 7.25, 8.6, 9.95, 11.3, 12.65, 14, 15.35, 16.7, 18.05, 19.4, 20.075, 20.75, 22.1,
             23.45, 24.8, 26.15, 27.5, 28.85, 30.2, 31.55, 32.225, 32.9, 34.25, 35.6, 36.95, 38.3, 39.65, 41, 42.35, 43.7,
             44.375, 45.05, 46.4, 47.75, 49.1, 50.45, 51.8, 56.525],
            [69.389, 69.956, 70.522, 71.088, 71.661, 72.253, 72.819, 73.386, 73.952, 74.808, 75.494, 77.796, 78.443, 79.01,
             79.829, 80.395, 80.593, 81.16, 82.692, 83.258, 83.897, 85.429, 86.073, 86.699, 87.463, 88.995, 89.193, 89.76,
             90.326, 91.858, 92.425, 93.111, 93.755, 94.322, 94.888, 97.563, 97.761, 98.328, 99.487, 100.255, 101.018,
             102.217, 103.657]),
    },
    "gpsimd": {
        "final": (
            [1.2],
            [0.466]),
        "local": (
            [3, 5.5, 8, 14, 16, 18, 20, 22, 24, 26, 28, 33.8, 35.8, 37.2, 37.8, 39.2, 39.8, 41.2, 42.5, 60],
            [7.591, 8.899, 9.832, 12.925, 16.894, 18.979, 20.529, 22.079, 23.629, 25.754, 27.304, 45.758, 51.126, 52.054,
             52.982, 53.91, 54.838, 59.599, 60.527, 99.607]),
        "prep1": (
            [6, 47, 49, 51],
            [36.151, 38.966, 47.293, 55.766]),
        "cross1": (
            [58, 61, 91],
            [62.935, 65.875, 103.904]),
        "keys2": (
            [99.5, 101.5, 103.5],
            [92.11, 100.071, 110.281]),
    },
}
M1_TICK, M2_TICK = 1.35, 1.55
SHARED_TICKS = {
    "x1T": [0.1], "q1": [1.2], "h3T": [3.5], "lin": [6], "gate": [8], "ff2o": [16], "x3T": [18],
    "sc3": [20, 21.3, 22.6], "pT3": [29, 30.3, 31.6], "out3": [33.5], "v2": [41, 42.5, 44],
    "k1": [45, 47, 49], "v1": [52, 54, 56], "k2": [98, 100, 102], "pv2T": [115.5], "o2T": [117], "out2": [118.5],
    "max1T": [M1_TICK * (3 * a1 + 2.2) for _, a1 in GROUP_TILES],
    "max2T": [0.5 + M2_TICK * (3 * a1 + 2.2) for _, a1 in GROUP_TILES],
}
LAST = 1000.0


def place(engine, stream, tick):
    return tick if tick >= LAST else float(np.interp(tick, *PLACES[engine][stream]))


def merged(engine, streams):
    live = [[place(engine, name, next(steps)), n, name, steps] for n, (name, steps) in enumerate(streams)]
    while live:
        first = min(live, key=lambda e: e[:2])
        tick = next(first[3], None)
        if tick is None:
            live.remove(first)
        else:
            assert place(engine, first[2], tick) >= first[0], (first[2], tick)
            first[0] = place(engine, first[2], tick)


def xattn_program(nc, a):
    with ExitStack() as ctx:
        def sb(name, shape, dt=F32):
            return ctx.enter_context(nc.sbuf_tensor(name, shape, dt))

        sems = {}

        loaded = ctx.enter_context(nc.semaphore("weights_loaded"))
        preset = ctx.enter_context(nc.semaphore("preset"))

        ident = sb("ident", [P, P])
        ones_mean = sb("ones_mean", [P, P])
        cos2 = sb("cos2", [P, 2 * (T + 1)])
        sin2 = sb("sin2", [P, 2 * (T + 1)])
        mask0 = sb("mask0", [T, KEYS0])
        head_mask = sb("head_mask", [P, H])
        cols = sb("cols", [P, len(COLS)])
        rows = sb("rows", [T, len(ROWS) * D])
        w_qkv = sb("w_qkv", [P, 3 * E0])
        w_rot = sb("w_rot", [P, 2 * E0])
        w_out0 = sb("w_out0", [P, PAIRS, D])
        w_mem = sb("w_mem", [P, D])
        w_ff1 = sb("w_ff1", [P, 2 * FF0_TILES * FF0])
        b_ff1 = sb("b_ff1", [FF0, 2 * FF0_TILES])
        w_ff2 = sb("w_ff2", [FF0, FF0_TILES, D])
        w1 = sb("w1", [P, 4, D])
        wq1 = sb("wq1", [P, D])
        wkv1 = sb("wkv1", [P, 2 * D])
        wo1 = sb("wo1", [P, D])
        wq2 = sb("wq2", [P, D])
        wkv2 = sb("wkv2", [P, 2 * D])
        wo2 = sb("wo2", [P, D])
        wf1 = sb("wf1", [P, 2 * FF2_TILES * D])
        bf1 = sb("bf1", [P, 2 * FF2_TILES])
        wf2 = sb("wf2", [P, FF2_TILES, D])

        def col(name):
            return cols[:, COLS.index(name):COLS.index(name) + 1]

        def row(name):
            return rows[:, ROWS.index(name) * D:(ROWS.index(name) + 1) * D]

        x0 = sb("x0", [T, D])
        ctx_buffers = [sb(f"ctxT{n}", [P, S]) for n in range(3)]
        ctxT = {"local": ctx_buffers[0], "cross1": ctx_buffers[0], "prep1": ctx_buffers[1], "final": ctx_buffers[2],
                "cross2": ctx_buffers[2]}
        ctxN = sb("ctxN", [P, NC, D])
        pool = sb("pool", [P, 8])
        xnT = sb("xnT", [P, T + 1])
        rope_a = sb("rope_a", [P, 2, 2 * (T + 1)])
        rope_b = sb("rope_b", [P, 2, 2 * (T + 1)])
        wide0 = sb("wide0", [P, H, T])
        qT0, oT0, kbds = wide0[:, 0:PAIRS, :], wide0[:, PAIRS:H, :], wide0
        kbd0 = sb("kbd0", [P, PAIRS, 2, KEYS0])
        val0 = sb("val0", [KEYS0, E0])
        sm = sb("sm", [T, H, KEYS0])
        p3 = sm[:].rearrange("p h k -> p (h k)")[:, 0:S]
        probT = sb("probT", [P, H, T])
        pT3 = probT[:, 0:NC, :]
        gate = sb("gate", [P, 4, T])
        egate = sb("egate", [P, 4, T])
        hid = sb("hid", [P, 4, T])
        vs = sb("vs", [T, D])
        stat = {st: sb("stat_" + st, [P, 64]) for st in ("local", "cross1", "cross2", "final")}
        junk = {st: sb("junk_" + st, [T, D]) for st in ("local", "cross1", "cross2", "final")}
        xs = {st: sb("xs_" + st, [T, D]) for st in NORMS}
        hT = {st: sb("hT_" + st, [P, T]) for st in ("local", "prep1", "cross1", "final")}
        on = {st: junk[st] for st in ("cross1", "cross2")}
        oT = {st: sb("oT_" + st, [P, T]) for st in ("cross1", "cross2")}
        x1 = sb("x1", [T, D])
        x2 = sb("x2", [T, D])
        x2_kept = sb("x2_kept", [T, D])
        x3 = sb("x3", [T, D])
        x4 = sb("x4", [T, D])
        x4_kept = sb("x4_kept", [T, D])
        x5 = sb("x5", [T, D])
        x6 = sb("x6", [T, D])
        qf = sb("qf", [P, T])
        qr = sb("qr", [P, T])
        qss = sb("qss", [P, T])
        kf = sb("kf", [P, 2, K_CUTS[0][1]])
        kr = sb("kr", [P, 2, K_CUTS[0][1]])
        qpart = {n: sb("q" + n, [P, T], BF16) for n in ("hi", "mid", "lo")}
        kpart = {(L, n): sb(f"k{n}{L}", [P, S], BF16) for L in (1, 2) for n in ("hi", "mid", "lo")}
        q_rows = {L: sb(f"q_rows{L}", [P, H, T], BF16) for L in (1, 2)}
        q_stack = {L: sb(f"q_stack{L}", [P, H, T], BF16) for L in (1, 2)}
        k_stack = sb("k_stack", [P, PAIRS, S], BF16)
        v_aug = {L: sb(f"v_aug{L}", [P, NC, H * VW]) for L in (1, 2)}
        prob = [sb(f"prob{i}", [P, GROUP * T]) for i in range(PROBS)]
        mx = {L: sb(f"mx{L}", [P, TILES, 3]) for L in (1, 2)}
        mxm = {L: sb(f"mxm{L}", [P, TILES]) for L in (1, 2)}
        mrow = {L: sb(f"mrow{L}", [TILE_ENDS[0], len(GROUP_TILES), P], BF16) for L in (1, 2)}
        pv = sb("pv", [P, 4 * T])
        y = sb("y", [T, D])
        q_dram = {L: nc.dram_tensor(f"q_parts{L}", (3, D, T), BF16).ap() for L in (1, 2)}
        minus_half = sb("minus_half", [P, 1])

        unit = ctx.enter_context(nc.psum_tensor("unit", [P, 2, 512], F32))
        rowmax = ctx.enter_context(nc.psum_tensor("rowmax", [P, 2, 512], F32))
        pv_acc = ctx.enter_context(nc.psum_tensor("pv_acc", [P, 512], F32))
        light = {b: ctx.enter_context(nc.psum_tensor(b, [P, 512], F32)) for b in LIGHT}

        loads = [
            (ident[:], a["c_ident"]), (ones_mean[:], a["c_mean"]), (cos2[:], a["c_cos"]), (sin2[:], a["c_sin"]),
            (mask0[:], a["c_mask"]), (head_mask[:], a["c_head_mask"]), (cols[:], a["cols"]), (rows[:], a["rows"]),
            (w_qkv[:], a["w_qkv"]), (w_rot[:], a["w_rot"]), (w_out0[:], a["w_out0"]), (w_mem[:], a["w_mem"]),
            (w_ff1[:], a["w_ff1"]), (b_ff1[:], a["b_ff1"]), (w_ff2[:], a["w_ff2"]), (w1[:], a["w1"]),
            (wq1[:], a["wq1"]), (wkv1[:], a["wkv1"]), (wo1[:], a["wo1"]),
            (wq2[:], a["wq2"]), (wkv2[:], a["wkv2"]), (wo2[:], a["wo2"]),
            (wf1[:], a["wf1"]), (bf1[:], a["bf1"]), (wf2[:], a["wf2"]),
            (val0[T + 1:KEYS0, :], a["pm_v"]),
        ]
        with nc.Block() as block:
            @block.sync
            def _(sp):
                for dst, src in loads:
                    sp.dma_start(dst, src).then_inc(loaded, 16)
                sp.wait_ge(preset, 1)
                for j in range(2):
                    sp.dma_start(kbd0[64 * j:64 * j + 64, :, j, T + 1:KEYS0],
                                 a["pm_k"][64 * j:64 * j + 64]).then_inc(loaded, 16)
                sp.wait_ge(loaded, 16 * (len(loads) + 2))

            @block.vector
            def _(dve):
                nc.vector.memset(pv[:], 0.0)
                nc.vector.memset(k_stack[KROWS:P], 1.0)
                for L in (1, 2):
                    nc.vector.memset(mxm[L][:], 0.0)

            @block.gpsimd
            def _(pool_eng):
                nc.gpsimd.memset(kbd0[:], 0.0).then_inc(preset, 1)
                nc.gpsimd.memset(minus_half[:], -0.5)
                for L in (1, 2):
                    nc.gpsimd.memset(q_stack[L][:], 0.0)
                    nc.gpsimd.memset(v_aug[L][:], 1.0)

        def iteration(batches):

            uses = {b: [(name, i) for name, n, _, stream in table if stream in batches for i in range(n)]
                    for b, table in LIGHT.items()}
            uses["bank_s"].sort(key=lambda use: place("tensor", STREAM_OF[use[0]], SHARED_TICKS[use[0]][use[1]]))

            def sem(name):
                base = name.removesuffix("_out")
                if name in READER:
                    name = BANK_OF[name] + "_filled"
                elif base in READER:
                    name = BANK_OF[base] + "_read_" + READER[base]
                if name not in sems:
                    sems[name] = ctx.enter_context(nc.semaphore(name))
                return sems[name]

            def nth(name, n):
                base = name.removesuffix("_out")
                if base not in READER:
                    return sem(name), n
                order = uses[BANK_OF[base]]
                at = order.index((base, n - 1))
                if name in READER:
                    return sem(name), at + 1
                return sem(name), sum(READER[use] == READER[base] for use, _ in order[:at + 1])

            def bank(name, i=0):
                return light[BANK_OF[name]]

            def bank_free(eng, name, i=0):
                order = uses[BANK_OF[name]]
                n = order.index((name, i)) - 1
                if n >= 0:
                    before, k = order[n]
                    eng.wait_ge(*nth(before + "_out", k + 1))

            def other(eng, stream, name, n):
                if stream in batches:
                    eng.wait_ge(*nth(name, n))

            def normed_at(name):
                stream = next(s for s in NORMS if name in NORMS[s])
                return nth("xs_" + stream, NORMS[stream].index(name) + 1)

            def run(engine, **streams):
                merged(engine, [(s, streams[s]()) for s in STREAMS if s in batches and s in streams])

            with nc.Block() as block:
                @block.sync
                def _(sp):
                    def park_queries(L):
                        for n, part in enumerate(("hi", "mid", "lo")):
                            sp.wait_ge(*nth(f"q{L}_{part}", 1))
                            sp.dma_start(q_dram[L][n], qpart[part][:]).then_inc(sem(f"q{L}_parked"), 16)

                    def stack_queries(L):
                        if L == 1:
                            sp.wait_ge(*nth("q1_parked", 48))
                        for t, (_, qp) in enumerate(TERMS):
                            src = q_dram[L][("hi", "mid", "lo").index(qp)].rearrange("(p j d) t -> j d p t", j=2, d=DH)
                            for j in range(2):
                                r = 16 * t + DH * j
                                sp.dma_start(q_stack[L][r:r + DH, j::2, :], src[j]).then_inc(sem(f"q{L}_stacked"), 16)

                    def stack_keys(L, g):
                        for t, (kp, _) in enumerate(TERMS):
                            for p in (2 * g, 2 * g + 1):
                                sp.dma_start(k_stack[16 * t:16 * t + 16, p, :],
                                             kpart[L, kp][16 * p:16 * p + 16, :]).then_inc(sem(f"k{L}_stacked{g}"), 16)

                    def stack_maxima(L, g):
                        a0, a1 = GROUP_TILES[g]
                        flat = q_stack[L][KROWS:KROWS + 1].rearrange("p h t -> p (h t)")
                        full = min(a1, H * T // P)
                        sp.wait_ge(*nth(f"max{L}T_out", g + 1))
                        sp.dma_start(flat[:, a0 * P:full * P], mrow[L][0:full - a0, g, :]).then_inc(sem(f"max{L}_stacked{g}"), 16)
                        if full < a1:
                            sp.dma_start(flat[:, full * P:H * T], mrow[L][full - a0:a1 - a0, g, 0:H * T - full * P]
                                         ).then_inc(sem(f"max{L}_stacked{g}"), 16)

                    def local():
                        b = batches["local"]
                        yield 0
                        sp.dma_start(x0[:], a["x"][b]).then_inc(sem("x0_in"), 16)
                        sp.dma_start(ctxT["local"][:], a["ctxT"][b]).then_inc(sem("ctxT_local_in"), 16)

                    def prep1():
                        b = batches["prep1"]
                        yield 0.2
                        sp.dma_start(ctxT["prep1"][:], a["ctxT"][b]).then_inc(sem("ctxT_prep1_in"), 16)
                        yield 5
                        park_queries(1)
                        yield 50
                        other(sp, "cross1", "score1", USTEPS)
                        stack_queries(1)
                        yield LAST
                        sp.wait_ge(*nth("q1_stacked", STACKED))

                    def stacks1():
                        for g in range(4):
                            yield 77.7 + 11.4 * g
                            for part in ("hi", "mid", "lo"):
                                sp.wait_ge(*nth(f"k1_{part}", 3))
                            other(sp, "cross2", "score2", NC * (g + 1))
                            stack_keys(1, g)
                        yield LAST
                        for g in range(4):
                            sp.wait_ge(*nth(f"k1_stacked{g}", STACKED))

                    def maxima1():
                        for g, (_, a1) in enumerate(GROUP_TILES):
                            yield M1_TICK * (3 * a1 - 1) + 5
                            stack_maxima(1, g)
                        yield LAST
                        for g in range(4):
                            sp.wait_ge(*nth(f"max1_stacked{g}", 32 if g == 3 else 16))

                    def cross1():
                        b = batches["cross1"]
                        yield 14
                        other(sp, "local", "pool", 1)
                        sp.dma_start(ctxT["cross1"][:], a["ctxT"][b]).then_inc(sem("ctxT_cross1_in"), 16)
                        yield 98
                        park_queries(2)
                        yield LAST
                        sp.wait_ge(*nth("q2_parked", 48))

                    def stacks2():
                        yield 7
                        stack_queries(2)
                        for g in range(4):
                            yield 12.5 + 11.5 * g
                            other(sp, "cross1", "score1", NC * (g + 1))
                            stack_keys(2, g)
                            if g == 1:
                                yield 30
                                other(sp, "final", "sc3", 3)
                                sp.dma_start(ctxT["cross2"][:], a["ctxT"][batches["cross2"]]).then_inc(sem("ctxT_cross2_in"), 16)

                    def maxima2():
                        for g, (_, a1) in enumerate(GROUP_TILES):
                            yield M2_TICK * (3 * a1 - 1) + 5.5
                            stack_maxima(2, g)

                    def final():
                        b = batches["final"]
                        yield 0.3
                        sp.dma_start(ctxT["final"][:], a["ctxT"][b]).then_inc(sem("ctxT_final_in"), 16)
                        sp.dma_start(ctxN[:, 0:NFULL, :], a["ctx_main"][b]).then_inc(sem("ctxN_in"), 16)
                        sp.dma_start(ctxN[0:TAIL, NFULL, :], a["ctx_tail"][b]).then_inc(sem("ctxN_in"), 16)
                        yield 37
                        sp.wait_ge(*nth("out3_out", 1))
                        sp.dma_start(a["out"][b], y[:]).then_inc(sem("stored"), 16)
                        yield LAST
                        sp.wait_ge(*nth("stored", 16))

                    run("sync", local=local, prep1=prep1, stacks1=stacks1, maxima1=maxima1, cross1=cross1, stacks2=stacks2, maxima2=maxima2, final=final)

                @block.tensor
                def _(pe):
                    mm = nc.tensor.matmul

                    def transpose(name, src, width, rows_, *ready, i=0):
                        if ready:
                            pe.wait_ge(*ready)
                        bank_free(pe, name, i)
                        nc.tensor.transpose(bank(name)[0:width, 0:rows_], src, ident[0:rows_, 0:rows_]).then_inc(sem(name), 1)

                    def project(name, lhsT, rhs, m, n, *ready):
                        pe.wait_ge(*ready)
                        bank_free(pe, name)
                        mm(bank(name)[0:m, 0:n], lhsT, rhs, start=True, stop=True).then_inc(sem(name), 1)

                    def key_piece(L, n, wk, stream):
                        pe.wait_ge(*nth(f"ctxT_{stream}_in", 16))
                        bank_free(pe, f"k{L}", n)
                        at, w = K_CUTS[n]
                        mm(bank(f"k{L}", n)[:, 0:w], wk, ctxT[stream][:, at:at + w], start=True, stop=True).then_inc(sem(f"k{L}"), 1)

                    def value_piece(L, n, wv, stream):
                        pe.wait_ge(*nth(f"ctxT_{stream}_in", 16))
                        bank_free(pe, f"v{L}", n)
                        for i in range(4):
                            at, w = CHUNKS[4 * n + i]
                            last = mm(bank(f"v{L}", n)[0:w, i * D:(i + 1) * D], ctxT[stream][:, at:at + w], wv, start=True, stop=True)
                        last.then_inc(sem(f"v{L}"), 1)

                    def row_scores(L, n):
                        t, s = n // 3, n % 3
                        w = min(P, H * T - t * P)
                        if n >= 2:
                            pe.wait_ge(*nth(f"max{L}_read", n - 1))
                        elif L == 1:
                            other(pe, "cross2", "max2_read", MSTEPS)
                        if n == 0 and L == 1:
                            pe.wait_ge(*nth("q1_rows", 1))
                            pe.wait_ge(*nth("k1_hi", 3))
                        at, cw = K_CUTS[s]
                        flat = q_rows[L][:].rearrange("p h t -> p (h t)")
                        mm(rowmax[0:w, n % 2, 0:cw], flat[:, t * P:t * P + w], kpart[L, "hi"][:, at:at + cw], start=True, stop=True
                           ).then_inc(sem(f"max{L}_scored"), 1)

                    def row_maxima(L, tick, step):
                        ends = {3 * a1 - 1: g for g, (_, a1) in enumerate(GROUP_TILES)}
                        for n in range(MSTEPS + 3):
                            yield tick + step * n
                            if n < MSTEPS:
                                row_scores(L, n)
                            if n - 3 in ends:
                                g = ends[n - 3]
                                yield SHARED_TICKS[f"max{L}T"][g]
                                a0, a1 = GROUP_TILES[g]
                                transpose(f"max{L}T", mxm[L][:, a0:a1], a1 - a0, P, *nth(f"max{L}", g + 1), i=g)

                    def scores(L, u):
                        g, c = u // NC, u % NC
                        at, w = CHUNKS[c]
                        qs = q_stack[L][:].rearrange("p h t -> p (h t)")
                        if L == 2 and c == 0:
                            pe.wait_ge(*nth(f"k2_stacked{g}", STACKED))
                            pe.wait_ge(*nth(f"max2_stacked{g}", 32 if g == 3 else 16))
                        if L == 2 and u == 0:
                            pe.wait_ge(*nth("q2_stacked", STACKED))
                        if u >= 2:
                            pe.wait_ge(*nth(f"prob{L}", u - 1))
                        elif L == 2:
                            other(pe, "cross1", "prob1", USTEPS)
                        for i in range(2):
                            p = 2 * g + i
                            last = mm(unit[0:w, u % 2, i * 2 * T:(i + 1) * 2 * T], k_stack[:, p, at:at + w],
                                      qs[:, 2 * p * T:2 * (p + 1) * T], start=True, stop=True)
                        last.then_inc(sem(f"score{L}"), 1)

                    def values(L, u):
                        g, c = u // NC, u % NC
                        w = CHUNKS[c][1]
                        pe.wait_ge(*nth(f"prob{L}", u + 1))
                        if u == 0 and L == 2:
                            other(pe, "cross1", "pv1", 4)
                            pe.wait_ge(*nth("v2_out", 3))
                        for j in range(GROUP):
                            h = GROUP * g + j
                            last = mm(pv_acc[32 * j:32 * j + VW, g * T:(g + 1) * T], v_aug[L][0:w, c, VW * h:VW * (h + 1)],
                                      prob[u % PROBS][0:w, j * T:(j + 1) * T], start=(c == 0), stop=(c == NC - 1),
                                      skip_group_check=True)
                        last.then_inc(sem(f"prob{L}_used"), 1)

                    def cross(L, tick):
                        for u in range(USTEPS + LAG):
                            yield tick + UTICK * u
                            if u < USTEPS:
                                scores(L, u)
                            if u >= LAG:
                                values(L, u - LAG)

                    def pv_rows(L):
                        pe.wait_ge(*nth(f"pv{L}", 4))
                        bank_free(pe, f"pv{L}T")
                        for g in range(4):
                            last = nc.tensor.transpose(bank(f"pv{L}T")[0:T, g * P:(g + 1) * P], pv[:, g * T:(g + 1) * T], ident[:])
                        last.then_inc(sem(f"pv{L}T"), 1)

                    def local():
                        W = T + 1
                        yield 5
                        transpose("xn", xs["local"][:], D, T, *normed_at("xs0"))
                        yield 6
                        project("pool_ms", ones_mean[:], pool[:, 1:2], P, 1, *nth("pool_sq", 1))
                        yield 10
                        project("mem", w_mem[:], pool[:, 3:4], P, 1, *nth("pool_normed", 1))
                        for p in range(PAIRS):
                            yield 12 + 2 * p
                            if p == 0:
                                pe.wait_ge(*nth("xn_out", 1))
                                pe.wait_ge(*nth("mem_out", 1))
                            bank_free(pe, "qk", p)
                            for n, (w, at) in enumerate(((w_qkv, 0), (w_qkv, E0), (w_rot, 0), (w_rot, E0))):
                                last = mm(bank("qk", p)[:, n * W:(n + 1) * W], w[:, at + p * P:at + (p + 1) * P], xnT[:],
                                          start=True, stop=True)
                            last.then_inc(sem("qk"), 1)
                        for n in range(2):
                            yield 28 + 2 * n
                            bank_free(pe, "val0", n)
                            mm(bank("val0", n)[0:W, :], xnT[:], w_qkv[:, 2 * E0 + n * 512:2 * E0 + (n + 1) * 512],
                               start=True, stop=True).then_inc(sem("val0"), 1)
                        for g in range(4):
                            yield 32 + 2 * g
                            pe.wait_ge(*nth("roped", 3 * (2 * g + 2)))
                            bank_free(pe, "score0", g)
                            for i in range(2):
                                p = 2 * g + i
                                last = mm(bank("score0", g)[0:T, i * 2 * KEYS0:(i + 1) * 2 * KEYS0], qT0[:, p, :],
                                          kbd0[:, p].rearrange("p j k -> p (j k)"), start=True, stop=True)
                            last.then_inc(sem("score0"), 1)
                        for g in range(4):
                            yield 40 + 2 * g
                            pe.wait_ge(*nth("prob0", g + 1))
                            bank_free(pe, "probT0", g)
                            for i in range(4):
                                last = nc.tensor.transpose(bank("probT0", g)[0:KEYS0, i * T:(i + 1) * T], sm[:, 4 * g + i, :],
                                                           ident[0:T, 0:T])
                            last.then_inc(sem("probT0"), 1)
                        pe.wait_ge(*nth("val0_out", 2))
                        for n in range(2):
                            yield 48 + 2 * n
                            pe.wait_ge(*nth("probT0_out", 2 * n + 2))
                            bank_free(pe, "oT0", n)
                            for i in range(8):
                                h = 8 * n + i
                                j, k = h % 2, i // 2
                                last = mm(bank("oT0", n)[64 * j:64 * j + 64, k * T:(k + 1) * T], val0[:, h * DH0:(h + 1) * DH0],
                                          probT[0:KEYS0, h, :], start=True, stop=True)
                            last.then_inc(sem("oT0"), 1)
                        yield 57
                        pe.wait_ge(*nth("oT0_out", 2))
                        bank_free(pe, "out0")
                        for p in range(PAIRS):
                            last = mm(bank("out0")[0:T, 0:D], oT0[:, p, :], w_out0[:, p, :], start=(p == 0), stop=(p == PAIRS - 1))
                        last.then_inc(sem("out0"), 1)
                        yield 62
                        transpose("fx0", xs["local"][:], D, T, *normed_at("xs_ff"))
                        for n, name in enumerate(("ffa", "ffg")):
                            yield 64 + 2 * n
                            pe.wait_ge(*nth("fx0_out", 1))
                            bank_free(pe, name)
                            for t in range(FF0_TILES):
                                at = (n * FF0_TILES + t) * FF0
                                last = mm(bank(name)[0:FF0, t * T:(t + 1) * T], w_ff1[:, at:at + FF0], hT["local"][:], start=True, stop=True)
                            last.then_inc(sem(name), 1)
                        yield 71
                        pe.wait_ge(*nth("hid0", 1))
                        bank_free(pe, "ffo")
                        for t in range(FF0_TILES):
                            last = mm(bank("ffo")[0:T, 0:D], hid[0:FF0, t, :], w_ff2[:, t, :], start=(t == 0), stop=(t == FF0_TILES - 1))
                        last.then_inc(sem("ffo"), 1)

                    def prep1():
                        yield SHARED_TICKS["x1T"][0]
                        transpose("x1T", x2[:], D, T)
                        yield SHARED_TICKS["q1"][0]
                        project("q1", w1[:, 0, :], hT["prep1"][:], D, T, *nth("x1T_out", 1))
                        for n in range(3):
                            yield SHARED_TICKS["k1"][n]
                            key_piece(1, n, w1[:, 1, :], "prep1")
                        for n in range(3):
                            yield SHARED_TICKS["v1"][n]
                            value_piece(1, n, w1[:, 2, :], "prep1")

                    def maxima1():
                        yield from row_maxima(1, 0, M1_TICK)

                    def cross1():
                        yield from cross(1, 0.5)
                        yield 51
                        pv_rows(1)
                        yield 53
                        transpose("o1T", on["cross1"][:], D, T, *nth("pv1T_out", 1))
                        yield 55
                        project("out1", oT["cross1"][:], w1[:, 3, :], T, D, *nth("o1T_out", 1))
                        yield 63
                        transpose("hT", xs["cross1"][:], D, T, *normed_at("xs_ln1"))
                        yield 65
                        project("qs", wq1[:], hT["cross1"][:], D, T, *nth("hT_out", 1))
                        yield 66.5
                        project("ks", wkv1[:, 0:D], hT["cross1"][:], D, T, *nth("hT_out", 1))
                        yield 68
                        project("vs", hT["cross1"][:], wkv1[:, D:2 * D], T, D, *nth("hT_out", 1))
                        kb = kbds[:].rearrange("p h t -> p (h t)")
                        for g in range(4):
                            yield 70 + 1.8 * g
                            if g == 0:
                                pe.wait_ge(*nth("qs_out", 1))
                                pe.wait_ge(*nth("ks_out", 1))
                            bank_free(pe, "scs", g)
                            mm(bank("scs", g)[0:T, 0:4 * T], qss[:], kb[:, g * 4 * T:(g + 1) * 4 * T], start=True, stop=True
                               ).then_inc(sem("scs"), 1)
                        for g in range(4):
                            yield 77.5 + 1.5 * g
                            pe.wait_ge(*nth("exps", g + 1))
                            bank_free(pe, "probTs", g)
                            for i in range(4):
                                last = nc.tensor.transpose(bank("probTs", g)[0:T, i * T:(i + 1) * T], sm[:, 4 * g + i, 0:T], ident[0:T, 0:T])
                            last.then_inc(sem("probTs"), 1)
                        yield 84
                        pe.wait_ge(*nth("probTs_out", 4))
                        pe.wait_ge(*nth("vs_out", 1))
                        bank_free(pe, "os")
                        for h in range(H):
                            last = mm(bank("os")[0:T, h * DH:(h + 1) * DH], probT[0:T, h, :], vs[:, h * DH:(h + 1) * DH], start=True, stop=True)
                        last.then_inc(sem("os"), 1)
                        yield 86
                        transpose("osT", on["cross1"][:], D, T, *nth("os_out", 1))
                        yield 88
                        project("outs", oT["cross1"][:], wo1[:], T, D, *nth("osT_out", 1))
                        yield 93
                        transpose("h2T", xs["cross1"][:], D, T, *normed_at("xs_ln2"))
                        yield 95
                        project("q2", wq2[:], hT["cross1"][:], D, T, *nth("h2T_out", 1))

                    def keys2():
                        for n in range(3):
                            yield SHARED_TICKS["k2"][n]
                            key_piece(2, n, wkv2[:, 0:D], "cross1")

                    def maxima2():
                        yield from row_maxima(2, 0.5, M2_TICK)

                    def values2():
                        for n in range(3):
                            yield SHARED_TICKS["v2"][n]
                            value_piece(2, n, wkv2[:, D:2 * D], "cross2")

                    def cross2():
                        yield from cross(2, 66)
                        yield SHARED_TICKS["pv2T"][0]
                        pv_rows(2)
                        yield SHARED_TICKS["o2T"][0]
                        transpose("o2T", on["cross2"][:], D, T, *nth("pv2T_out", 1))
                        yield SHARED_TICKS["out2"][0]
                        project("out2", oT["cross2"][:], wo2[:], T, D, *nth("o2T_out", 1))

                    def final():
                        yield SHARED_TICKS["h3T"][0]
                        transpose("h3T", xs["final"][:], D, T, *normed_at("xs_ln3"))
                        for n, name in enumerate(("lin", "gate")):
                            yield SHARED_TICKS[name][0]
                            pe.wait_ge(*nth("h3T_out", 1))
                            bank_free(pe, name)
                            for t in range(FF2_TILES):
                                at = (n * FF2_TILES + t) * D
                                last = mm(bank(name)[:, t * T:(t + 1) * T], wf1[:, at:at + D], hT["final"][:], start=True, stop=True)
                            last.then_inc(sem(name), 1)
                        yield SHARED_TICKS["ff2o"][0]
                        pe.wait_ge(*nth("hid2", 1))
                        bank_free(pe, "ff2o")
                        for t in range(FF2_TILES):
                            last = mm(bank("ff2o")[0:T, 0:D], hid[:, t, :], wf2[:, t, :], start=(t == 0), stop=(t == FF2_TILES - 1))
                        last.then_inc(sem("ff2o"), 1)
                        yield SHARED_TICKS["x3T"][0]
                        transpose("x3T", x6[:], D, T, *nth("x6", 1))
                        for n in range(3):
                            yield SHARED_TICKS["sc3"][n]
                            if n == 0:
                                pe.wait_ge(*nth("x3T_out", 1))
                                pe.wait_ge(*nth("ctxT_final_in", 16))
                            at, w = K_CUTS[n]
                            bank_free(pe, "sc3", n)
                            mm(bank("sc3", n)[0:T, 0:w], hT["final"][:], ctxT["final"][:, at:at + w], start=True, stop=True
                               ).then_inc(sem("sc3"), 1)
                        for n in range(3):
                            yield SHARED_TICKS["pT3"][n]
                            pe.wait_ge(*nth("exp3", 1))
                            bank_free(pe, "pT3", n)
                            for i in range(4):
                                at, w = CHUNKS[4 * n + i]
                                last = nc.tensor.transpose(bank("pT3", n)[0:w, i * T:(i + 1) * T], p3[:, at:at + w], ident[0:T, 0:T])
                            last.then_inc(sem("pT3"), 1)
                        yield SHARED_TICKS["out3"][0]
                        pe.wait_ge(*nth("ctxN_in", 32))
                        bank_free(pe, "out3")
                        for c in range(NC):
                            w = CHUNKS[c][1]
                            last = mm(bank("out3")[0:T, 0:D], pT3[0:w, c, :], ctxN[0:w, c, :], start=(c == 0), stop=(c == NC - 1))
                        last.then_inc(sem("out3"), 1)

                    run("tensor", local=local, prep1=prep1, maxima1=maxima1, cross1=cross1, keys2=keys2, values2=values2, maxima2=maxima2, cross2=cross2, final=final)

                @block.scalar
                def _(act):
                    def move(name, n, dst, src, bias=0.0):
                        act.wait_ge(*nth(name, n + 1))
                        nc.scalar.activation(dst, src, ACT.Identity, bias=bias).then_inc(sem(name + "_out"), 1)

                    def four(t, width=T):
                        return t[:, 0:4 * width].rearrange("p (a n) -> p a n", a=4)

                    def key_piece(L, n):
                        at, w = K_CUTS[n]
                        act.wait_ge(*nth(f"k{L}", n + 1))
                        if n == 2:
                            act.wait_ge(*nth(f"k{L}_lo", 1))
                        if n == 0:
                            if L == 2:
                                other(act, "maxima2", "max2_read", MSTEPS)
                                for g in range(4):
                                    other(act, "cross2", f"k2_stacked{g}", STACKED)
                                other(act, "prep1", "k1_lo", 3)
                        bias = col("bk") if L == 1 else 0.0
                        src = bank(f"k{L}", n)[:, 0:w]
                        nc.scalar.activation(kpart[L, "hi"][:, at:at + w], src, ACT.Identity, bias=bias).then_inc(sem(f"k{L}_hi"), 1)
                        nc.scalar.activation(kf[:, n % 2, 0:w], src, ACT.Identity, bias=bias).then_inc(sem(f"k{L}_out"), 1)

                    def value_piece(L, n):
                        act.wait_ge(*nth(f"v{L}", n + 1))
                        if n == 0 and L == 1:
                            other(act, "cross1", "prob1_used", USTEPS)
                        src = bank(f"v{L}", n)[:].rearrange("p (c h d) -> p c h d", c=4, d=DH)
                        dst = v_aug[L][:, 4 * n:4 * n + 4, :].rearrange("p c (h w) -> p c h w", w=VW)[:, :, :, 0:DH]
                        full = min(NFULL - 4 * n, 4)
                        last = nc.scalar.activation(dst[:, 0:full], src[:, 0:full], ACT.Copy)
                        if full < 4:
                            last = nc.scalar.activation(dst[0:TAIL, full], src[0:TAIL, full], ACT.Copy)
                        last.then_inc(sem(f"v{L}_out"), 1)

                    def take_pv(L):
                        act.wait_ge(*nth(f"prob{L}_used", USTEPS))
                        if L == 2:
                            other(act, "cross1", "pv1T", 1)
                        for j in (2, 3):
                            q = slice(32 * j, 32 * j + VW)
                            nc.scalar.activation(pv[q, :], pv_acc[q, 0:4 * T], ACT.Copy).then_inc(sem(f"pv{L}"), 1)

                    def cross(L, tick):
                        scale = float(np.float32(1) / np.sqrt(np.float32(DH))) if L == 1 else 0.125
                        for u in range(USTEPS):
                            yield tick + UTICK * u
                            w = CHUNKS[u % NC][1]
                            act.wait_ge(*nth(f"score{L}", u + 1))
                            if u >= PROBS:
                                act.wait_ge(*nth(f"prob{L}_used", u - PROBS + 1))
                            elif L == 2 and u == 0:
                                other(act, "cross1", "prob1_used", USTEPS)
                            nc.scalar.activation(prob[u % PROBS][0:w, :], unit[0:w, u % 2, 0:GROUP * T], ACT.Exp, scale=scale
                                                 ).then_inc(sem(f"prob{L}"), 1)

                    def local():
                        yield 2
                        act.wait_ge(*nth("ctxT_local_in", 16))
                        nc.scalar.activation(ctxT["local"][:], ctxT["local"][:], ACT.Copy, accum_out=pool[:, 2:3]).then_inc(sem("pooled"), 1)
                        for n in range(2):
                            yield 29 + 2 * n
                            move("val0", n, val0[0:T + 1, n * 512:(n + 1) * 512], bank("val0", n)[0:T + 1, :])
                        for g in range(4):
                            yield 34.5 + 2 * g
                            act.wait_ge(*nth("shifted0", g + 1))
                            d = sm[:, 4 * g:4 * g + 4, :]
                            nc.scalar.activation(d, d, ACT.Exp, scale=0.125).then_inc(sem("exp0"), 1)
                        for g in range(4):
                            yield 41 + 2 * g
                            if g == 0:
                                other(act, "final", "out3", 1)
                            move("probT0", g, probT[0:KEYS0, 4 * g:4 * g + 4, :], four(bank("probT0", g)[0:KEYS0]))
                        for n in range(2):
                            yield 49 + 2 * n
                            move("oT0", n, oT0[:, 4 * n:4 * n + 4, :], four(bank("oT0", n)))
                        yield 68
                        act.wait_ge(*nth("ffg_out", 1))
                        nc.scalar.activation(egate[0:FF0, 0:FF0_TILES, :], gate[0:FF0, 0:FF0_TILES, :], ACT.Exp, scale=-1.0).then_inc(sem("eg0"), 1)

                    def prep1():
                        yield 0.6
                        move("x1T", 0, hT["prep1"][:], bank("x1T")[:, 0:T])
                        for n in range(3):
                            yield 46 + 2 * n
                            key_piece(1, n)
                        for n in range(3):
                            yield 53 + 2 * n
                            value_piece(1, n)

                    def cross1():
                        yield from cross(1, 0.7)
                        yield 50
                        take_pv(1)
                        yield 66
                        move("qs", 0, qss[:], bank("qs")[:, 0:T])
                        yield 69
                        move("vs", 0, vs[:], bank("vs")[0:T, 0:D])
                        for g in range(4):
                            yield 72 + 1.8 * g
                            act.wait_ge(*nth("scs_out", g + 1))
                            d = sm[:, 4 * g:4 * g + 4, 0:T]
                            nc.scalar.activation(d, d, ACT.Exp, scale=0.125).then_inc(sem("exps"), 1)
                        for g in range(4):
                            yield 78.2 + 1.5 * g
                            if g == 0:
                                other(act, "local", "oT0", 2)
                            move("probTs", g, probT[0:T, 4 * g:4 * g + 4, :], four(bank("probTs", g)[0:T]))
                        yield 87
                        move("osT", 0, oT["cross1"][:], bank("osT")[:, 0:T])

                    def keys2():
                        for n in range(3):
                            yield 98.7 + 2 * n
                            key_piece(2, n)

                    def values2():
                        for n in range(3):
                            yield 42 + 1.55 * n
                            value_piece(2, n)

                    def cross2():
                        yield from cross(2, 66.2)
                        yield 115
                        take_pv(2)
                        yield 118
                        move("o2T", 0, oT["cross2"][:], bank("o2T")[:, 0:T])

                    def final():
                        yield 10.5
                        act.wait_ge(*nth("gate_out", 1))
                        nc.scalar.activation(egate[:], gate[:], ACT.Exp, scale=-GELU).then_inc(sem("eg2"), 1)
                        yield 19
                        move("x3T", 0, hT["final"][:], bank("x3T")[:, 0:T])
                        for n in range(3):
                            yield 21 + 1.3 * n
                            at, w = K_CUTS[n]
                            move("sc3", n, p3[:, at:at + w], bank("sc3", n)[0:T, 0:w])
                        yield 27
                        act.wait_ge(*nth("max3", 1))
                        nc.scalar.activation(p3, p3, ACT.Exp, bias=stat["final"][0:T, 52:53], accum_out=stat["final"][0:T, 53:54]
                                             ).then_inc(sem("exp3"), 1)
                        for n in range(3):
                            yield 29.8 + 1.3 * n
                            act.wait_ge(*nth("pT3", n + 1))
                            full = min(NFULL - 4 * n, 4)
                            src = four(bank("pT3", n))
                            last = nc.scalar.activation(pT3[:, 4 * n:4 * n + full, :], src[:, 0:full], ACT.Copy)
                            if full < 4:
                                last = nc.scalar.activation(pT3[0:TAIL, NFULL, :], src[0:TAIL, full], ACT.Copy)
                            last.then_inc(sem("pT3_out"), 1)

                    run("scalar", local=local, prep1=prep1, cross1=cross1, keys2=keys2, values2=values2, cross2=cross2, final=final)

                @block.vector
                def _(dve):
                    v = nc.vector
                    steps = [0]

                    def link(ins):
                        steps[0] += 1
                        ins.then_inc(sem("dve_step"), 1)
                        dve.wait_ge(sem("dve_step"), steps[0])

                    def normed(name, src, tick, kind, *ready):
                        st = next(s for s in NORMS if name in NORMS[s])
                        sta = stat[st]
                        yield tick
                        if ready:
                            dve.wait_ge(*ready)
                        if kind == "rms":
                            link(v.tensor_tensor_reduce(junk[st][:], src, src, 1.0 / D, 0.0, ALU.mult, ALU.add, sta[0:T, 11:12]))
                        else:
                            link(v.bn_stats(sta[0:T, 4:10], src))
                            link(v.bn_aggr(sta[0:T, 10:12], sta[0:T, 4:10]))
                        v.tensor_scalar(sta[0:T, 1:2], sta[0:T, 11:12], EPS_RMS if kind == "rms" else EPS_LN, None, ALU.add
                                        ).then_inc(sem("norm_var_" + st), 1)
                        yield tick + 2
                        dve.wait_ge(*nth("norm_rstd_" + st, NORMS[st].index(name) + 1))
                        if kind == "rms":
                            v.tensor_scalar(xs[st][:], src, sta[0:T, 2:3], None, ALU.mult).then_inc(sem("xs_" + st), 1)
                        else:
                            v.tensor_scalar(xs[st][:], src, sta[0:T, 10:11], sta[0:T, 2:3], ALU.subtract, ALU.mult
                                            ).then_inc(sem("xs_" + st), 1)

                    def to_hT(name, scale, shift=None):
                        dve.wait_ge(*nth(name, 1))
                        dst, src = hT[STREAM_OF[name]][:], bank(name)[:, 0:T]
                        if shift is None:
                            ins = v.tensor_scalar(dst, src, scale, None, ALU.mult)
                        else:
                            ins = v.tensor_scalar(dst, src, scale, shift, ALU.mult, ALU.add)
                        ins.then_inc(sem(name + "_out"), 1)

                    def wide(t, n):
                        return t.unsqueeze(2).to_broadcast([t.shape[0], t.shape[1], n])

                    def sums(st, width, tag):
                        for g in range(4):
                            dve.wait_ge(*nth("exp" + tag, g + 1))
                            last = v.tensor_reduce(stat[st][0:T, 32 + 4 * g:36 + 4 * g], sm[:, 4 * g:4 * g + 4, 0:width], AX.X, ALU.add)
                        link(last)
                        v.reciprocal(stat[st][0:T, 32:48], stat[st][0:T, 32:48]).then_inc(sem("rsum" + tag), 1)

                    def add_out(name, dst, res, bias, tag):
                        st = STREAM_OF[name]
                        dve.wait_ge(*nth(name, 1))
                        v.tensor_tensor(junk[st][:], bank(name)[0:T, 0:D], bias, ALU.add).then_inc(sem(name + "_out"), 1)
                        dve.wait_ge(*nth(name + "_out", 1))
                        v.tensor_tensor(dst, junk[st][:], res, ALU.add).then_inc(sem(tag), 1)

                    def split_queries(L):
                        dve.wait_ge(*nth(f"q{L}", 1))
                        if L == 1:
                            v.tensor_scalar(qf[:], bank("q1")[:, 0:T], col("bq"), None, ALU.add).then_inc(sem("q1_out"), 1)
                        else:
                            other(dve, "prep1", "q1_parked", 48)
                            other(dve, "prep1", "q1_rows", 1)
                            v.tensor_copy(qf[:], bank("q2")[:, 0:T]).then_inc(sem("q2_out"), 1)
                        dve.wait_ge(*nth(f"q{L}_out", 1))
                        v.tensor_copy(qpart["hi"][:], qf[:]).then_inc(sem(f"q{L}_hi"), 1)
                        dve.wait_ge(*nth(f"q{L}_hi", 1))
                        link(v.tensor_tensor(qr[:], qf[:], qpart["hi"][:], ALU.subtract))
                        v.tensor_copy(qpart["mid"][:], qr[:]).then_inc(sem(f"q{L}_mid"), 1)
                        dve.wait_ge(*nth(f"q{L}_mid", 1))
                        v.tensor_tensor(qpart["lo"][:], qr[:], qpart["mid"][:], ALU.subtract).then_inc(sem(f"q{L}_lo"), 1)

                    def query_rows(L):
                        if L == 2:
                            other(dve, "cross2", "max2_read", MSTEPS)
                        v.tensor_tensor(q_rows[L][:], qpart["hi"][:].unsqueeze(1).to_broadcast([P, H, T]), wide(head_mask[:], T),
                                        ALU.mult).then_inc(sem(f"q{L}_rows"), 1)

                    def row_max(L, n):
                        t, s = n // 3, n % 3
                        w = min(P, H * T - t * P)
                        dve.wait_ge(*nth(f"max{L}_scored", n + 1))
                        v.tensor_reduce(mx[L][0:w, t, s:s + 1], rowmax[0:w, n % 2, 0:K_CUTS[s][1]], AX.X, ALU.max
                                        ).then_inc(sem(f"max{L}_read"), 1)

                    def group_max(L, g):
                        a0, a1 = GROUP_TILES[g]
                        full = min(a1, H * T // P)
                        dve.wait_ge(*nth(f"max{L}_read", 3 * a1))
                        last = v.tensor_reduce(mxm[L][:, a0:full], mx[L][:, a0:full, :], AX.X, ALU.max)
                        if full < a1:
                            rest = H * T - full * P
                            last = v.tensor_reduce(mxm[L][0:rest, full:a1], mx[L][0:rest, full:a1, :], AX.X, ALU.max)
                        last.then_inc(sem(f"max{L}"), 1)

                    def minus_maxima(L, g):
                        n = GROUP_TILES[g][1] - GROUP_TILES[g][0]
                        dve.wait_ge(*nth(f"max{L}T", g + 1))
                        v.tensor_scalar(mrow[L][0:n, g, :], bank(f"max{L}T")[0:n, 0:P], -1.0, None, ALU.mult
                                        ).then_inc(sem(f"max{L}T_out"), 1)

                    def row_maxima(L, tick, step):
                        ends = {3 * a1 - 1: g for g, (_, a1) in enumerate(GROUP_TILES)}
                        for n in range(MSTEPS + 3):
                            if n < MSTEPS:
                                yield tick + step * n
                                row_max(L, n)
                            if n in ends:
                                group_max(L, ends[n])
                            if n - 3 in ends:
                                yield tick + step * (n + 0.5)
                                minus_maxima(L, ends[n - 3])

                    def take_pv(L):
                        dve.wait_ge(*nth(f"prob{L}_used", USTEPS))
                        if L == 2:
                            other(dve, "cross1", "pv1T", 1)
                        for j in (0, 1):
                            q = slice(32 * j, 32 * j + VW)
                            v.tensor_copy(pv[q, :], pv_acc[q, 0:4 * T]).then_inc(sem(f"pv{L}"), 1)

                    def attended(L):
                        st = STREAM_OF[f"pv{L}T"]
                        dve.wait_ge(*nth(f"pv{L}T", 1))
                        view = bank(f"pv{L}T")[0:T, :].rearrange("p (h w) -> p h w", w=32)
                        link(v.reciprocal(stat[st][0:T, 16:32], view[:, :, DH]))
                        v.tensor_tensor(on[st][:].rearrange("p (h d) -> p h d", d=DH), view[:, :, 0:DH], wide(stat[st][0:T, 16:32], DH),
                                        ALU.mult).then_inc(sem(f"pv{L}T_out"), 1)

                    def gated(bank_lin, bank_gate, tick, m, tiles, biases, tag):
                        yield tick
                        dve.wait_ge(*nth(bank_lin, 1))
                        if tag == "0":
                            other(dve, "final", "ff2o", 1)
                        v.tensor_tensor(hid[0:m, 0:tiles, :], bank(bank_lin)[0:m, 0:tiles * T].rearrange("p (a n) -> p a n", a=tiles),
                                        wide(biases[:, 0:tiles], T), ALU.add).then_inc(sem(bank_lin + "_out"), 1)
                        yield tick + 2
                        dve.wait_ge(*nth(bank_gate, 1))
                        g = gate[0:m, 0:tiles, :]
                        e = egate[0:m, 0:tiles, :]
                        v.tensor_tensor(g, bank(bank_gate)[0:m, 0:tiles * T].rearrange("p (a n) -> p a n", a=tiles),
                                        wide(biases[:, tiles:2 * tiles], T), ALU.add).then_inc(sem(bank_gate + "_out"), 1)
                        dve.wait_ge(*nth(bank_gate + "_out", 1))
                        v.tensor_tensor(hid[0:m, 0:tiles, :], hid[0:m, 0:tiles, :], g, ALU.mult)
                        yield tick + 4
                        dve.wait_ge(*nth("eg" + tag, 1))
                        link(v.tensor_scalar(e, e, 1.0, None, ALU.add))
                        link(v.reciprocal(e, e))
                        v.tensor_tensor(hid[0:m, 0:tiles, :], hid[0:m, 0:tiles, :], e, ALU.mult).then_inc(sem("hid" + tag), 1)

                    def local():
                        sta = stat["local"]
                        yield from normed("xs0", x0[:], 2, "rms", *nth("x0_in", 16))
                        yield 5
                        dve.wait_ge(*nth("pooled", 1))
                        v.tensor_scalar(pool[:, 0:1], pool[:, 2:3], 1.0 / S, None, ALU.mult).then_inc(sem("pool"), 1)
                        yield 6
                        dve.wait_ge(*nth("xn", 1))
                        v.tensor_scalar(xnT[:, 0:T], bank("xn")[:, 0:T], col("attn_norm"), None, ALU.mult).then_inc(sem("xn_out"), 1)
                        yield 7
                        dve.wait_ge(*nth("pool_ms", 1))
                        v.tensor_scalar(pool[:, 4:5], bank("pool_ms")[:, 0:1], EPS_RMS, None, ALU.add).then_inc(sem("pool_ms_out"), 1)
                        yield 9
                        dve.wait_ge(*nth("pool_rstd", 1))
                        v.tensor_scalar(pool[:, 3:4], pool[:, 0:1], pool[:, 5:6], col("mem_norm"), ALU.mult, ALU.mult
                                        ).then_inc(sem("pool_normed"), 1)
                        yield 11
                        dve.wait_ge(*nth("mem", 1))
                        v.tensor_copy(xnT[:, T:T + 1], bank("mem")[:, 0:1]).then_inc(sem("mem_out"), 1)
                        W = T + 1
                        for p in range(PAIRS):
                            yield 13 + 2 * p
                            dve.wait_ge(*nth("qk", p + 1))
                            if p >= 2:
                                dve.wait_ge(*nth("roped", 3 * (p - 1)))
                            v.tensor_tensor(rope_a[:, p % 2, :], bank("qk", p)[:, 0:2 * W], cos2[:], ALU.mult)
                            v.tensor_tensor(rope_b[:, p % 2, :], bank("qk", p)[:, 2 * W:4 * W], sin2[:], ALU.mult).then_inc(sem("qk_out"), 1)
                        def group_sums(g):
                            dve.wait_ge(*nth("exp0", g + 1))
                            r = sta[0:T, 32 + 4 * g:36 + 4 * g]
                            link(v.tensor_reduce(r, sm[:, 4 * g:4 * g + 4, :], AX.X, ALU.add))
                            v.reciprocal(r, r).then_inc(sem("rsum0"), 1)

                        for g in range(4):
                            yield 33 + 2 * g
                            dve.wait_ge(*nth("score0", g + 1))
                            if g == 0:
                                other(dve, "final", "pT3", 3)
                            s = bank("score0", g)[0:T, 0:4 * KEYS0].rearrange("p (a n) -> p a n", a=4)
                            v.tensor_tensor(sm[:, 4 * g:4 * g + 4, :], s, mask0[:].unsqueeze(1).to_broadcast([T, 4, KEYS0]), ALU.add
                                            ).then_inc(sem("score0_out"), 1)
                            dve.wait_ge(*nth("score0_out", g + 1))
                            v.tensor_reduce(sta[0:T, 16 + 4 * g:20 + 4 * g], sm[:, 4 * g:4 * g + 4, :], AX.X, ALU.max).then_inc(sem("max0"), 1)
                            if g:
                                yield 34.8 + 2 * g
                                group_sums(g - 1)
                        yield 42
                        group_sums(3)
                        yield 58
                        dve.wait_ge(*nth("out0", 1))
                        v.tensor_tensor(x1[:], bank("out0")[0:T, 0:D], x0[:], ALU.add).then_inc(sem("out0_out"), 1)
                        yield from normed("xs_ff", x1[:], 59, "rms", *nth("out0_out", 1))
                        yield 63
                        to_hT("fx0", col("ff_norm"))
                        yield from gated("ffa", "ffg", 65, FF0, FF0_TILES, b_ff1[:], "0")
                        yield 71.5
                        other(dve, "prep1", "x2_kept", 1)
                        other(dve, "prep1", "x1T", 1)
                        add_out("ffo", x2[:], x1[:], row("ff_b2"), "x2")

                    def prep1():
                        yield 1.8
                        split_queries(1)
                        yield 58.5
                        other(dve, "cross1", "x3", 1)
                        v.tensor_copy(x2_kept[:], x2[:]).then_inc(sem("x2_kept"), 1)

                    def maxima1():
                        yield from row_maxima(1, 0.5, M1_TICK)

                    def cross1():
                        yield 50
                        take_pv(1)
                        yield 52
                        attended(1)
                        yield 54
                        dve.wait_ge(*nth("o1T", 1))
                        v.tensor_scalar(oT["cross1"][:], bank("o1T")[:, 0:T], col("bv"), None, ALU.add).then_inc(sem("o1T_out"), 1)
                        yield 56
                        add_out("out1", x3[:], x2_kept[:], row("bo"), "x3")
                        yield from normed("xs_l1", x3[:], 57, "ln", *nth("x3", 1))
                        dve.wait_ge(*normed_at("xs_l1"))
                        link(v.tensor_tensor(junk["cross1"][:], xs["cross1"][:], row("gamma"), ALU.mult))
                        v.tensor_tensor(x3[:], junk["cross1"][:], row("beta"), ALU.add).then_inc(sem("x3b"), 1)
                        yield from normed("xs_ln1", x3[:], 60, "ln", *nth("x3b", 1))
                        yield 64
                        to_hT("hT", col("ln1_s"), col("ln1_b"))
                        yield 67.5
                        dve.wait_ge(*nth("ks", 1))
                        other(dve, "local", "out0", 1)
                        v.tensor_tensor(kbds[:], bank("ks")[:, 0:T].unsqueeze(1).to_broadcast([P, H, T]), wide(head_mask[:], T), ALU.mult
                                        ).then_inc(sem("ks_out"), 1)
                        for g in range(4):
                            yield 71 + 1.8 * g
                            dve.wait_ge(*nth("scs", g + 1))
                            if g == 0:
                                other(dve, "local", "probT0", 4)
                            s = bank("scs", g)[0:T, 0:4 * T].rearrange("p (a n) -> p a n", a=4)
                            m = stat["cross1"][0:T, 16 + 4 * g:20 + 4 * g]
                            link(v.tensor_reduce(m, s, AX.X, ALU.max))
                            v.tensor_tensor(sm[:, 4 * g:4 * g + 4, 0:T], s, wide(m, T), ALU.subtract).then_inc(sem("scs_out"), 1)
                        yield 78.5
                        sums("cross1", T, "s")
                        yield 85
                        dve.wait_ge(*nth("rsums", 1))
                        dve.wait_ge(*nth("os", 1))
                        v.tensor_tensor(on["cross1"][:].rearrange("p (h d) -> p h d", d=DH), bank("os")[0:T, 0:D].rearrange("p (h d) -> p h d", d=DH),
                                        wide(stat["cross1"][0:T, 32:48], DH), ALU.mult).then_inc(sem("os_out"), 1)
                        yield 89
                        other(dve, "cross2", "x4_kept", 1)
                        add_out("outs", x4[:], x3[:], row("bo1"), "x4")
                        yield from normed("xs_ln2", x4[:], 90, "ln", *nth("x4", 1))
                        yield 94
                        to_hT("h2T", col("ln2_s"), col("ln2_b"))
                        yield 96.5
                        split_queries(2)
                        query_rows(2)

                    def maxima2():
                        yield from row_maxima(2, 1.2, M2_TICK)

                    def cross2():
                        yield 0.4
                        v.tensor_copy(x4_kept[:], x4[:]).then_inc(sem("x4_kept"), 1)
                        yield 115
                        take_pv(2)
                        yield 116.3
                        attended(2)
                        yield 119.5
                        other(dve, "final", "x6", 1)
                        add_out("out2", x5[:], x4_kept[:], row("bo2"), "x5")

                    def final():
                        sta = stat["final"]
                        yield from normed("xs_ln3", x5[:], 0.2, "ln")
                        yield 4.5
                        to_hT("h3T", col("ln3_s"), col("ln3_b"))
                        yield from gated("lin", "gate", 7, P, FF2_TILES, bf1[:], "2")
                        yield 17
                        add_out("ff2o", x6[:], x5[:], row("bff2"), "x6")
                        yield 25.5
                        dve.wait_ge(*nth("sc3_out", 3))
                        v.tensor_reduce(sta[0:T, 52:53], p3, AX.X, ALU.max, negate=True).then_inc(sem("max3"), 1)
                        yield 29
                        dve.wait_ge(*nth("exp3", 1))
                        link(v.reciprocal(sta[0:T, 58:59], sta[0:T, 53:54]))
                        yield 36
                        dve.wait_ge(*nth("out3", 1))
                        v.scalar_tensor_tensor(y[:], bank("out3")[0:T, 0:D], sta[0:T, 58:59], x6[:], ALU.mult, ALU.add).then_inc(sem("out3_out"), 1)

                    run("vector", local=local, prep1=prep1, maxima1=maxima1, cross1=cross1, maxima2=maxima2, cross2=cross2, final=final)

                @block.gpsimd
                def _(pool_eng):
                    g = nc.gpsimd

                    def rstd(ready, done, dst, src, n, count=1):
                        pool_eng.wait_ge(*nth(ready, count))
                        g.tensor_tensor(dst, src, minus_half[0:n, :], ALU.pow).then_inc(sem(done), 1)

                    def norm_rstd(name):
                        st = next(s for s in NORMS if name in NORMS[s])
                        rstd("norm_var_" + st, "norm_rstd_" + st, stat[st][0:T, 2:3], stat[st][0:T, 1:2], T, NORMS[st].index(name) + 1)

                    def key_piece(L, n):
                        at, w = K_CUTS[n]
                        f, r = kf[:, n % 2, 0:w], kr[:, n % 2, 0:w]
                        hi, mid_, lo = (kpart[L, part][:, at:at + w] for part in ("hi", "mid", "lo"))
                        pool_eng.wait_ge(*nth(f"k{L}_out", n + 1))
                        pool_eng.wait_ge(*nth(f"k{L}_hi", n + 1))
                        g.tensor_tensor(r, f, hi, ALU.subtract).then_inc(sem(f"k{L}_r"), 1)
                        pool_eng.wait_ge(*nth(f"k{L}_r", n + 1))
                        g.tensor_copy(mid_, r).then_inc(sem(f"k{L}_mid"), 1)
                        pool_eng.wait_ge(*nth(f"k{L}_mid", n + 1))
                        g.tensor_tensor(lo, r, mid_, ALU.subtract).then_inc(sem(f"k{L}_lo"), 1)

                    def by_head(t):
                        return t.unsqueeze(2).to_broadcast([T, 4, KEYS0])

                    def local():
                        sta = stat["local"]
                        yield 3
                        norm_rstd("xs0")
                        yield 5.5
                        pool_eng.wait_ge(*nth("pool", 1))
                        g.tensor_tensor(pool[:, 1:2], pool[:, 0:1], pool[:, 0:1], ALU.mult).then_inc(sem("pool_sq"), 1)
                        yield 8
                        rstd("pool_ms_out", "pool_rstd", pool[:, 5:6], pool[:, 4:5], P)
                        W = T + 1
                        for p in range(PAIRS):
                            yield 14 + 2 * p
                            pool_eng.wait_ge(*nth("qk_out", p + 1))
                            ra, rb = rope_a[:, p % 2, :], rope_b[:, p % 2, :]
                            g.tensor_tensor(qT0[:, p, :], ra[:, 0:T], rb[:, 0:T], ALU.add).then_inc(sem("roped"), 1)
                            for j in range(2):
                                pool_eng.wait_ge(*nth("roped", 3 * p + j + 1))
                                q = slice(64 * j, 64 * j + 64)
                                g.tensor_tensor(kbd0[q, p, j, 0:W], ra[q, W:2 * W], rb[q, W:2 * W], ALU.add).then_inc(sem("roped"), 1)
                            pool_eng.wait_ge(*nth("roped", 3 * p + 3))

                        def normalised(n):
                            pool_eng.wait_ge(*nth("rsum0", n + 1))
                            d = sm[:, 4 * n:4 * n + 4, :]
                            g.tensor_tensor(d, d, by_head(sta[0:T, 32 + 4 * n:36 + 4 * n]), ALU.mult).then_inc(sem("prob0"), 1)

                        for n in range(4):
                            yield 33.8 + 2 * n
                            pool_eng.wait_ge(*nth("max0", n + 1))
                            d = sm[:, 4 * n:4 * n + 4, :]
                            g.tensor_tensor(d, d, by_head(sta[0:T, 16 + 4 * n:20 + 4 * n]), ALU.subtract).then_inc(sem("shifted0"), 1)
                            if n:
                                yield 35.2 + 2 * n
                                normalised(n - 1)
                        yield 42.5
                        normalised(3)
                        yield 60
                        norm_rstd("xs_ff")

                    def prep1():
                        yield 6
                        pool_eng.wait_ge(*nth("q1_hi", 1))
                        g.tensor_tensor(q_rows[1][:], qpart["hi"][:].unsqueeze(1).to_broadcast([P, H, T]),
                                        head_mask[:].unsqueeze(2).to_broadcast([P, H, T]), ALU.mult).then_inc(sem("q1_rows"), 1)
                        for n in range(3):
                            yield 47 + 2 * n
                            key_piece(1, n)

                    def cross1():
                        yield 58
                        norm_rstd("xs_l1")
                        yield 61
                        norm_rstd("xs_ln1")
                        yield 91
                        norm_rstd("xs_ln2")

                    def keys2():
                        for n in range(3):
                            yield 99.5 + 2 * n
                            key_piece(2, n)

                    def final():
                        yield 1.2
                        norm_rstd("xs_ln3")

                    run("gpsimd", local=local, prep1=prep1, cross1=cross1, keys2=keys2, final=final)

            used = [s.num for s in sems.values()]
            nc.all_engine_barrier(sems_to_clear=range(min(used), max(used) + 1))

        for start in range(PRE):
            iteration({stream: start - lag for stream, lag in LAGS.items() if lag <= start})
        with nc.Fori(PRE, B) as b:
            iteration({stream: b - lag for stream, lag in LAGS.items()})
        for end in range(1, PRE + 1):
            iteration({stream: B - 1 + end - lag for stream, lag in LAGS.items() if lag >= end})


def _constants():
    W = T + 1
    inv = (1.0 / 10000.0 ** (np.arange(0, DH0, 2, dtype=np.float32) / np.float32(DH0))).astype(np.float32)
    ang = np.repeat(np.arange(T, dtype=np.float32)[:, None] * inv[None, :], 2, axis=-1).astype(np.float32)
    cos = np.ones((DH0, W), np.float32)
    sin = np.zeros((DH0, W), np.float32)
    cos[:, :T] = np.cos(ang.astype(np.float64)).T
    sin[:, :T] = np.sin(ang.astype(np.float64)).T
    sin[0::2] = -sin[0::2]
    q, k = np.arange(T)[:, None], np.arange(T)[None, :]
    mask = np.zeros((T, KEYS0), np.float32)
    mask[:, :T] = np.where((q >= k) & (q // SEG == k // SEG), 0.0, -1e30)
    mask[:, T] = DH0 ** 0.5 * np.log(float(NM))
    heads = (np.arange(D)[:, None] // DH == np.arange(H)[None, :]).astype(np.float32)
    return {
        "c_ident": np.eye(P, dtype=np.float32), "c_mean": np.full((P, P), 1.0 / D, np.float32),
        "c_cos": np.tile(cos, (2, 2)), "c_sin": np.tile(sin, (2, 2)), "c_mask": mask, "c_head_mask": heads,
    }


def _padded(x, n, axis=-1):
    shape = list(x.shape)
    shape[axis] = n
    out = np.zeros(shape, x.dtype)
    out[tuple(slice(0, k) for k in x.shape)] = x
    return out


def kernel(**inputs):
    import concourse.bacc as _bacc
    from concourse import mybir as _mybir
    from concourse.bass_utils import run_bass_kernel_spmd as _run

    i = {k: np.asarray(v) for k, v in inputs.items()}
    ctx = i["ctx_1024"]
    main = ctx[:, :NFULL * P].reshape(B, P, NFULL, D)
    tail = ctx[:, NFULL * P:]
    qkv = i["L0_xattn_to_qkv_w"]
    swapped = qkv[:, :2 * E0].reshape(D, E0, 2)[:, :, ::-1].reshape(D, 2 * E0)
    pm = i["L0_xattn_persist_mem"]
    ff1, ffb = i["L0_xattn_ff_w1"], i["L0_xattn_ff_b1"]
    n0 = FF0_TILES * FF0
    data = {
        "x": i["x"], "ctx_main": main, "ctx_tail": tail,
        "ctxT": np.concatenate([main.transpose(0, 3, 2, 1).reshape(B, D, NFULL * P), tail.transpose(0, 2, 1)], axis=2),
        "cols": np.stack([i["L0_xattn_attn_norm_w"], i["L0_xattn_mem_pool_norm_w"], i["L0_xattn_ff_norm_w"], i["L1_xattn_bq"],
                          i["L1_xattn_bk"], i["L1_xattn_bv"]] + [i[f"L2_xattn_ln{n}_{c}"] for n in (1, 2, 3) for c in "sb"], axis=1),
        "rows": np.tile(np.concatenate([i["L0_xattn_ff_b2"], i["L1_xattn_bo"], i["L1_xattn_gamma"], i["L1_xattn_beta"],
                                        i["L2_xattn_bo1"], i["L2_xattn_bo2"], i["L2_xattn_bff2"]])[None], (T, 1)),
        "w_qkv": qkv, "w_rot": swapped,
        "w_out0": i["L0_xattn_to_out_w"].reshape(PAIRS, P, D).transpose(1, 0, 2),
        "w_mem": i["L0_xattn_to_mem_tokens_w"],
        "w_ff1": np.concatenate([_padded(ff1[:, :DFF0], n0), _padded(ff1[:, DFF0:], n0)], axis=1),
        "b_ff1": np.concatenate([_padded(ffb[:DFF0], n0), _padded(ffb[DFF0:], n0)]).reshape(2 * FF0_TILES, FF0).T,
        "w_ff2": _padded(i["L0_xattn_ff_w2"], n0, 0).reshape(FF0_TILES, FF0, D).transpose(1, 0, 2),
        "w1": np.stack([i[f"L1_xattn_W{c}"].T for c in "qkvo"], axis=1),
        "wq1": i["L2_xattn_Wq1"], "wkv1": i["L2_xattn_Wkv1"], "wo1": i["L2_xattn_Wo1"],
        "wq2": i["L2_xattn_Wq2"], "wkv2": i["L2_xattn_Wkv2"], "wo2": i["L2_xattn_Wo2"],
        "wf1": i["L2_xattn_Wff1"], "bf1": i["L2_xattn_bff1"].reshape(2 * FF2_TILES, P).T,
        "wf2": i["L2_xattn_Wff2"].reshape(FF2_TILES, P, D).transpose(1, 0, 2),
        "pm_k": pm.reshape(PAIRS, 2, NPM, DH0).transpose(1, 3, 0, 2).reshape(P, PAIRS, NPM),
        "pm_v": pm.transpose(1, 0, 2).reshape(NPM, E0),
        **_constants(),
    }
    nc = _bacc.Bacc("TRN2", target_bir_lowering=False, num_devices=1)
    arrays, aps = {}, {}
    for name, arr in data.items():
        arr = np.ascontiguousarray(arr)
        arrays[f"in_{name}"] = arr
        aps[name] = nc.dram_tensor(f"in_{name}", arr.shape, _mybir.dt.from_np(arr.dtype), kind="ExternalInput").ap()
    aps["out"] = nc.dram_tensor("out_0", (B, T, D), F32, kind="ExternalOutput").ap()
    xattn_program(nc, aps)
    return _run(nc, [arrays], core_ids=[0]).results[0]["out_0"]
```
